# Optimizing a Trainium2 kernel written in Bass

```python
import numpy as np
import jax
import jax.numpy as jnp

def _softmax(x, axis=-1):
    return jax.nn.softmax(x, axis=axis)

def _gelu(x):
    return jax.nn.gelu(x, approximate=True)

def _silu(x):
    return jax.nn.silu(x)

def _sigmoid(x):
    return jax.nn.sigmoid(x)

def _layernorm(x, axis=-1, eps=1e-05):
    m = jnp.mean(x, axis=axis, keepdims=True)
    v = jnp.var(x, axis=axis, keepdims=True)
    return (x - m) / jnp.sqrt(v + eps)

def _scatter_add(tgt, idx, src, axis=0):
    return tgt.at[idx].add(src)

def _segment_sum(src, seg, n):
    return jax.ops.segment_sum(src, seg, n)
kernel_name = 'mk_seq_preln_d4_jaxref_r8_9a0b2e'

def setup_inputs(seed: int=0):
    np.random.seed(seed)
    _w = jnp.asarray

    def _L0_attn_setup():
        import jax, jax.numpy as jnp
        import numpy as np
        D_MODEL = 128
        D_STATE = 64
        D_HEAD = 64
        N_HEADS = 16
        D_INNER = D_HEAD * N_HEADS
        K = 4
        BATCH = 4
        SEQ = 512
        LN_EPS = 1e-05

        def _ssd_scan(xh, Bm, Cm, A_param):
            A_disc = jnp.exp(-jnp.exp(A_param))

            def step(h, inp):
                x_t, B_t, C_t = inp
                h = h * A_disc + B_t[:, None, None, :] * x_t[..., None]
                y_t = jnp.einsum('bhdn,bn->bhd', h, C_t)
                return (h, y_t)
            b = xh.shape[0]
            h0 = jnp.zeros((b, N_HEADS, D_HEAD, D_STATE), xh.dtype)
            xs = (jnp.swapaxes(xh, 0, 1), jnp.swapaxes(Bm, 0, 1), jnp.swapaxes(Cm, 0, 1))
            _, ys = jax.lax.scan(step, h0, xs)
            return jnp.swapaxes(ys, 0, 1)
        key = jax.random.key(seed)
        k0, k1, k2, k3, k4 = jax.random.split(key, 5)
        x = jax.random.normal(k0, (BATCH, SEQ, D_MODEL), jnp.float32)
        in_proj_w = jax.random.normal(k1, (2 * D_INNER + 2 * D_STATE, D_MODEL), jnp.float32) / np.sqrt(D_MODEL).astype(np.float32)
        conv_w = jax.random.normal(k2, (D_INNER, 1, K), jnp.float32) * 0.5
        conv_b = jax.random.normal(k3, (D_INNER,), jnp.float32) * 0.1
        A_param = jnp.broadcast_to(-jnp.log(jnp.arange(1, D_STATE + 1, dtype=jnp.float32))[None, None, :], (N_HEADS, D_HEAD, D_STATE))
        ln_w = jnp.ones((D_INNER,), jnp.float32)
        ln_b = jnp.zeros((D_INNER,), jnp.float32)
        out_proj_w = jax.random.normal(k4, (D_MODEL, D_INNER), jnp.float32) / np.sqrt(D_INNER).astype(np.float32)
        return {'x': x, 'in_proj_w': in_proj_w, 'conv_w': conv_w, 'conv_b': conv_b, 'A_param': A_param, 'ln_w': ln_w, 'ln_b': ln_b, 'out_proj_w': out_proj_w}
    _L0_attn_in = _L0_attn_setup()

    def _L0_ffn_setup():
        import jax, jax.numpy as jnp
        import numpy as np
        DIM = 128

        def _reference_tuple_inner(x, W_r, W_k, W_v, mu_r, mu_k):
            B, T, C = x.shape
            x_prev = jnp.concatenate([jnp.zeros((B, 1, C), x.dtype), x[:, :-1, :]], axis=1)
            xr = mu_r * x + (1.0 - mu_r) * x_prev
            xk = mu_k * x + (1.0 - mu_k) * x_prev
            r = jax.nn.sigmoid(jnp.einsum('btc,dc->btd', xr, W_r))
            k = jnp.einsum('btc,dc->btd', xk, W_k)
            k_act = jnp.square(jax.nn.relu(k))
            out = r * jnp.einsum('btc,dc->btd', k_act, W_v)
            new_state = x[:, -1, :]
            return (out, new_state)
        key = jax.random.key(seed)
        ks = jax.random.split(key, 6)
        B, T, C = (8, 256, DIM)
        x = jax.random.normal(ks[0], (B, T, C), dtype=jnp.float32)
        s = 1.0 / np.sqrt(C)
        W_r = jax.random.uniform(ks[1], (C, C), jnp.float32, -s, s)
        W_k = jax.random.uniform(ks[2], (C, C), jnp.float32, -s, s)
        W_v = jax.random.uniform(ks[3], (C, C), jnp.float32, -s, s)
        mu_r = jax.random.uniform(ks[4], (C,), jnp.float32)
        mu_k = jax.random.uniform(ks[5], (C,), jnp.float32)
        return {'x': x, 'W_r': W_r, 'W_k': W_k, 'W_v': W_v, 'mu_r': mu_r, 'mu_k': mu_k}
    _L0_ffn_in = _L0_ffn_setup()

    def _L1_attn_setup():
        import jax, jax.numpy as jnp
        import numpy as np
        from jax import lax
        D_MODEL = 128
        D_STATE = 16
        D_CONV = 4
        EXPAND = 2
        D_INNER = EXPAND * D_MODEL
        DT_RANK = (D_MODEL + 15) // 16
        LN_EPS = 1e-05

        def _mamba_block(x, ln_g, ln_b, W_in, conv_w, conv_b, W_xproj, W_dt, b_dt, A_log, D, W_out):
            B, L, _ = x.shape
            mu = jnp.mean(x, axis=-1, keepdims=True)
            var = jnp.var(x, axis=-1, keepdims=True)
            h = (x - mu) * lax.rsqrt(var + LN_EPS) * ln_g + ln_b
            xz = jnp.einsum('bld,de->ble', h, W_in)
            u, z = jnp.split(xz, 2, axis=-1)
            u_t = jnp.transpose(u, (0, 2, 1))
            u_t = lax.conv_general_dilated(u_t, conv_w, window_strides=(1,), padding=[(D_CONV - 1, 0)], feature_group_count=D_INNER, dimension_numbers=('NCH', 'OIH', 'NCH'))
            u_t = u_t + conv_b[None, :, None]
            u = jax.nn.silu(jnp.transpose(u_t, (0, 2, 1)))
            x_dbl = jnp.einsum('bld,de->ble', u, W_xproj)
            dt, Bm, Cm = jnp.split(x_dbl, [DT_RANK, DT_RANK + D_STATE], axis=-1)
            dt = jax.nn.softplus(jnp.einsum('blr,rd->bld', dt, W_dt) + b_dt)
            A = -jnp.exp(A_log)
            dA = jnp.exp(jnp.einsum('bld,dn->bldn', dt, A))
            dBu = jnp.einsum('bld,bln->bldn', dt * u, Bm)

            def step(hc, inp):
                dA_t, dBu_t, C_t = inp
                hc = dA_t * hc + dBu_t
                y_t = jnp.einsum('bdn,bn->bd', hc, C_t)
                return (hc, y_t)
            h0 = jnp.zeros((B, D_INNER, D_STATE), x.dtype)
            xs = (jnp.transpose(dA, (1, 0, 2, 3)), jnp.transpose(dBu, (1, 0, 2, 3)), jnp.transpose(Cm, (1, 0, 2)))
            _, ys = lax.scan(step, h0, xs)
            y = jnp.transpose(ys, (1, 0, 2)) + u * D
            y = y * jax.nn.silu(z)
            out = jnp.einsum('bld,dm->blm', y, W_out)
            return x + out
        key = jax.random.key(seed)
        ks = jax.random.split(key, 12)
        s = 0.02
        x = jax.random.normal(ks[0], (2, 256, D_MODEL), dtype=jnp.float32)
        params = {'x': x, 'ln_g': jnp.ones((D_MODEL,), jnp.float32), 'ln_b': jnp.zeros((D_MODEL,), jnp.float32), 'W_in': jax.random.normal(ks[1], (D_MODEL, 2 * D_INNER), jnp.float32) * s, 'conv_w': jax.random.normal(ks[2], (D_INNER, 1, D_CONV), jnp.float32) * 0.2, 'conv_b': jnp.zeros((D_INNER,), jnp.float32), 'W_xproj': jax.random.normal(ks[3], (D_INNER, DT_RANK + 2 * D_STATE), jnp.float32) * s, 'W_dt': jax.random.normal(ks[4], (DT_RANK, D_INNER), jnp.float32) * 0.1, 'b_dt': jax.random.normal(ks[5], (D_INNER,), jnp.float32) * 0.1, 'A_log': jnp.log(jnp.tile(jnp.arange(1.0, D_STATE + 1.0, dtype=jnp.float32), (D_INNER, 1))), 'D': jnp.ones((D_INNER,), jnp.float32), 'W_out': jax.random.normal(ks[6], (D_INNER, D_MODEL), jnp.float32) * s}
        return params
    _L1_attn_in = _L1_attn_setup()

    def _L1_ffn_setup():
        import jax, jax.numpy as jnp
        import numpy as np
        E, D, MULT, K = (8, 128, 4, 2)
        B, S = (4, 256)
        H = MULT * D
        key = jax.random.key(seed)
        k0, k1, k2, k3 = jax.random.split(key, 4)
        x = jax.random.normal(k0, (B, S, D), dtype=jnp.float32)
        Wr = jax.random.normal(k1, (E, D), dtype=jnp.float32) * D ** (-0.5)
        W1 = jax.random.normal(k2, (E, D, H), dtype=jnp.float32) * D ** (-0.5)
        b1 = jnp.zeros((E, H), dtype=jnp.float32)
        W2 = jax.random.normal(k3, (E, H, D), dtype=jnp.float32) * H ** (-0.5)
        b2 = jnp.zeros((E, D), dtype=jnp.float32)
        return {'x': x, 'Wr': Wr, 'W1': W1, 'b1': b1, 'W2': W2, 'b2': b2}
    _L1_ffn_in = _L1_ffn_setup()

    def _L2_attn_setup():
        import jax, jax.numpy as jnp
        import numpy as np
        DIM = 128
        H = 16
        HD = DIM // H
        EPS = 1e-06
        B, N = (1, 256)
        key = jax.random.key(seed)
        k1, k2, k3 = jax.random.split(key, 3)
        x = jax.random.normal(k1, (B, N, DIM), dtype=jnp.float32)
        qkv_w = jax.random.normal(k2, (3 * DIM, DIM), dtype=jnp.float32) * 0.02
        proj_w = jax.random.normal(k3, (DIM, DIM), dtype=jnp.float32) * 0.02
        alpha_log = jnp.zeros((H,), dtype=jnp.float32)
        beta_log = jnp.zeros((H,), dtype=jnp.float32)
        return {'x': x, 'qkv_w': qkv_w, 'proj_w': proj_w, 'alpha_log': alpha_log, 'beta_log': beta_log}
    _L2_attn_in = _L2_attn_setup()

    def _L2_ffn_setup():
        import jax, jax.numpy as jnp
        import numpy as np
        D_IN, D_HID = (128, 512)

        def _ternary(key, shape):
            return jax.random.randint(key, shape, -1, 2).astype(jnp.float32)

        def _tlin(x, w, s):
            return jnp.einsum('bsi,oi->bso', x, w) * s
        key = jax.random.key(seed)
        ks = jax.random.split(key, 12)
        inv = lambda fan: 1.0 / np.sqrt(fan).astype(np.float32)
        return {'x': jax.random.normal(ks[0], (4, 256, D_IN), dtype=jnp.float32), 'w1_w': _ternary(ks[1], (D_HID, D_IN)), 'w1_s': jax.random.uniform(ks[2], (D_HID,), dtype=jnp.float32) * inv(D_IN), 'w2_w': _ternary(ks[3], (D_HID, D_IN)), 'w2_s': jax.random.uniform(ks[4], (D_HID,), dtype=jnp.float32) * inv(D_IN), 'h1_w': _ternary(ks[5], (D_HID, D_HID)), 'h1_s': jax.random.uniform(ks[6], (D_HID,), dtype=jnp.float32) * inv(D_HID), 'h2_w': _ternary(ks[7], (D_HID, D_HID)), 'h2_s': jax.random.uniform(ks[8], (D_HID,), dtype=jnp.float32) * inv(D_HID), 'w3_w': _ternary(ks[9], (D_IN, D_HID)), 'w3_s': jax.random.uniform(ks[10], (D_IN,), dtype=jnp.float32) * inv(D_HID)}
    _L2_ffn_in = _L2_ffn_setup()

    def _L3_attn_setup():
        import jax, jax.numpy as jnp
        import numpy as np
        B, T, D_MODEL, N = (4, 256, 128, 16)
        D_INNER = 2 * D_MODEL

        def _ssm_scan(x_in, A, B_ssm, C_ssm):

            def step(state, ins):
                x_t, a_t, b_t, c_t = ins
                decay = jnp.exp(a_t)
                state = state * decay[:, None, :] + x_t[:, :, None] * b_t[:, None, :]
                out_t = (state * c_t[:, None, :]).sum(-1)
                return (state, out_t)
            b, t, d = x_in.shape
            n = A.shape[-1]
            init = jnp.zeros((b, d, n), dtype=x_in.dtype)
            xs = (jnp.swapaxes(x_in, 0, 1), jnp.swapaxes(A, 0, 1), jnp.swapaxes(B_ssm, 0, 1), jnp.swapaxes(C_ssm, 0, 1))
            _, outs = jax.lax.scan(step, init, xs)
            return jnp.swapaxes(outs, 0, 1)
        key = jax.random.key(seed)
        ks = jax.random.split(key, 7)
        s = 0.02
        return {'x': jax.random.normal(ks[0], (B, T, D_MODEL), dtype=jnp.float32), 'W_in': jax.random.normal(ks[1], (D_MODEL, 2 * D_INNER), dtype=jnp.float32) * s, 'W_A': jax.random.normal(ks[2], (D_INNER, N), dtype=jnp.float32) * s, 'W_B': jax.random.normal(ks[3], (D_INNER, N), dtype=jnp.float32) * s, 'W_C': jax.random.normal(ks[4], (D_INNER, N), dtype=jnp.float32) * s, 'W_out': jax.random.normal(ks[5], (D_INNER, D_MODEL), dtype=jnp.float32) * s, 'norm_w': jnp.ones((D_INNER,), dtype=jnp.float32)}
    _L3_attn_in = _L3_attn_setup()

    def _L3_ffn_setup():
        import jax, jax.numpy as jnp
        import numpy as np
        K = 2
        key = jax.random.key(seed)
        ks = jax.random.split(key, 8)
        B, S, D, Dff, E = (1, 256, 128, 512, 8)
        scale = 0.02
        return {'x': jax.random.normal(ks[0], (B, S, D), jnp.float32), 'Wg': jax.random.normal(ks[1], (D, E), jnp.float32) * scale, 'w_gate': jax.random.normal(ks[2], (E, D, Dff), jnp.float32) * scale, 'b_gate': jax.random.normal(ks[3], (E, Dff), jnp.float32) * scale, 'w_up': jax.random.normal(ks[4], (E, D, Dff), jnp.float32) * scale, 'b_up': jax.random.normal(ks[5], (E, Dff), jnp.float32) * scale, 'w_down': jax.random.normal(ks[6], (E, Dff, D), jnp.float32) * scale, 'b_down': jax.random.normal(ks[7], (E, D), jnp.float32) * scale}
    _L3_ffn_in = _L3_ffn_setup()
    _d = {'L0_attn_x': _L0_attn_in['x'], 'L0_attn_in_proj_w': _L0_attn_in['in_proj_w'], 'L0_attn_conv_w': _L0_attn_in['conv_w'], 'L0_attn_conv_b': _L0_attn_in['conv_b'], 'L0_attn_A_param': _L0_attn_in['A_param'], 'L0_attn_ln_w': _L0_attn_in['ln_w'], 'L0_attn_ln_b': _L0_attn_in['ln_b'], 'L0_attn_out_proj_w': _L0_attn_in['out_proj_w'], 'L0_ffn_W_r': _L0_ffn_in['W_r'], 'L0_ffn_W_k': _L0_ffn_in['W_k'], 'L0_ffn_W_v': _L0_ffn_in['W_v'], 'L0_ffn_mu_r': _L0_ffn_in['mu_r'], 'L0_ffn_mu_k': _L0_ffn_in['mu_k'], 'L1_attn_ln_g': _L1_attn_in['ln_g'], 'L1_attn_ln_b': _L1_attn_in['ln_b'], 'L1_attn_W_in': _L1_attn_in['W_in'], 'L1_attn_conv_w': _L1_attn_in['conv_w'], 'L1_attn_conv_b': _L1_attn_in['conv_b'], 'L1_attn_W_xproj': _L1_attn_in['W_xproj'], 'L1_attn_W_dt': _L1_attn_in['W_dt'], 'L1_attn_b_dt': _L1_attn_in['b_dt'], 'L1_attn_A_log': _L1_attn_in['A_log'], 'L1_attn_D': _L1_attn_in['D'], 'L1_attn_W_out': _L1_attn_in['W_out'], 'L1_ffn_Wr': _L1_ffn_in['Wr'], 'L1_ffn_W1': _L1_ffn_in['W1'], 'L1_ffn_b1': _L1_ffn_in['b1'], 'L1_ffn_W2': _L1_ffn_in['W2'], 'L1_ffn_b2': _L1_ffn_in['b2'], 'L2_attn_qkv_w': _L2_attn_in['qkv_w'], 'L2_attn_proj_w': _L2_attn_in['proj_w'], 'L2_attn_alpha_log': _L2_attn_in['alpha_log'], 'L2_attn_beta_log': _L2_attn_in['beta_log'], 'L2_ffn_w1_w': _L2_ffn_in['w1_w'], 'L2_ffn_w1_s': _L2_ffn_in['w1_s'], 'L2_ffn_w2_w': _L2_ffn_in['w2_w'], 'L2_ffn_w2_s': _L2_ffn_in['w2_s'], 'L2_ffn_h1_w': _L2_ffn_in['h1_w'], 'L2_ffn_h1_s': _L2_ffn_in['h1_s'], 'L2_ffn_h2_w': _L2_ffn_in['h2_w'], 'L2_ffn_h2_s': _L2_ffn_in['h2_s'], 'L2_ffn_w3_w': _L2_ffn_in['w3_w'], 'L2_ffn_w3_s': _L2_ffn_in['w3_s'], 'L3_attn_W_in': _L3_attn_in['W_in'], 'L3_attn_W_A': _L3_attn_in['W_A'], 'L3_attn_W_B': _L3_attn_in['W_B'], 'L3_attn_W_C': _L3_attn_in['W_C'], 'L3_attn_W_out': _L3_attn_in['W_out'], 'L3_attn_norm_w': _L3_attn_in['norm_w'], 'L3_ffn_Wg': _L3_ffn_in['Wg'], 'L3_ffn_w_gate': _L3_ffn_in['w_gate'], 'L3_ffn_b_gate': _L3_ffn_in['b_gate'], 'L3_ffn_w_up': _L3_ffn_in['w_up'], 'L3_ffn_b_up': _L3_ffn_in['b_up'], 'L3_ffn_w_down': _L3_ffn_in['w_down'], 'L3_ffn_b_down': _L3_ffn_in['b_down']}
    _x0 = _d['L0_attn_x']
    _d['L0_attn_x'] = jax.random.normal(jax.random.fold_in(jax.random.key(seed), 1), (4, 512, 128), dtype=_x0.dtype)
    del _x0
    return _d

def reference(L0_attn_x, L0_attn_in_proj_w, L0_attn_conv_w, L0_attn_conv_b, L0_attn_A_param, L0_attn_ln_w, L0_attn_ln_b, L0_attn_out_proj_w, L0_ffn_W_r, L0_ffn_W_k, L0_ffn_W_v, L0_ffn_mu_r, L0_ffn_mu_k, L1_attn_ln_g, L1_attn_ln_b, L1_attn_W_in, L1_attn_conv_w, L1_attn_conv_b, L1_attn_W_xproj, L1_attn_W_dt, L1_attn_b_dt, L1_attn_A_log, L1_attn_D, L1_attn_W_out, L1_ffn_Wr, L1_ffn_W1, L1_ffn_b1, L1_ffn_W2, L1_ffn_b2, L2_attn_qkv_w, L2_attn_proj_w, L2_attn_alpha_log, L2_attn_beta_log, L2_ffn_w1_w, L2_ffn_w1_s, L2_ffn_w2_w, L2_ffn_w2_s, L2_ffn_h1_w, L2_ffn_h1_s, L2_ffn_h2_w, L2_ffn_h2_s, L2_ffn_w3_w, L2_ffn_w3_s, L3_attn_W_in, L3_attn_W_A, L3_attn_W_B, L3_attn_W_C, L3_attn_W_out, L3_attn_norm_w, L3_ffn_Wg, L3_ffn_w_gate, L3_ffn_b_gate, L3_ffn_w_up, L3_ffn_b_up, L3_ffn_w_down, L3_ffn_b_down):

    def _L0_attn_ref(x, in_proj_w, conv_w, conv_b, A_param, ln_w, ln_b, out_proj_w):
        import jax, jax.numpy as jnp
        import numpy as np
        D_MODEL = 128
        D_STATE = 64
        D_HEAD = 64
        N_HEADS = 16
        D_INNER = D_HEAD * N_HEADS
        K = 4
        BATCH = 4
        SEQ = 512
        LN_EPS = 1e-05

        def _ssd_scan(xh, Bm, Cm, A_param):
            A_disc = jnp.exp(-jnp.exp(A_param))

            def step(h, inp):
                x_t, B_t, C_t = inp
                h = h * A_disc + B_t[:, None, None, :] * x_t[..., None]
                y_t = jnp.einsum('bhdn,bn->bhd', h, C_t)
                return (h, y_t)
            b = xh.shape[0]
            h0 = jnp.zeros((b, N_HEADS, D_HEAD, D_STATE), xh.dtype)
            xs = (jnp.swapaxes(xh, 0, 1), jnp.swapaxes(Bm, 0, 1), jnp.swapaxes(Cm, 0, 1))
            _, ys = jax.lax.scan(step, h0, xs)
            return jnp.swapaxes(ys, 0, 1)
        b, L, _ = x.shape
        xBC = x @ in_proj_w.T
        xc = xBC[..., :D_INNER]
        z = xBC[..., D_INNER:2 * D_INNER]
        Bm = xBC[..., 2 * D_INNER:2 * D_INNER + D_STATE]
        Cm = xBC[..., 2 * D_INNER + D_STATE:]
        xt = jnp.swapaxes(xc, 1, 2)
        y = jax.lax.conv_general_dilated(xt, conv_w, window_strides=(1,), padding=[(K - 1, 0)], feature_group_count=D_INNER, dimension_numbers=('NCH', 'OIH', 'NCH'))
        xc = jnp.swapaxes(y + conv_b[None, :, None], 1, 2)
        xc = jax.nn.silu(xc)
        xh = xc.reshape(b, L, N_HEADS, D_HEAD)
        yssd = _ssd_scan(xh, Bm, Cm, A_param).reshape(b, L, D_INNER)
        yg = yssd * jax.nn.silu(z)
        mu = yg.mean(-1, keepdims=True)
        var = yg.var(-1, keepdims=True)
        yn = (yg - mu) / jnp.sqrt(var + LN_EPS) * ln_w + ln_b
        return yn @ out_proj_w.T

    def _L0_ffn_ref(x, W_r, W_k, W_v, mu_r, mu_k):
        import jax, jax.numpy as jnp
        import numpy as np
        DIM = 128

        def _reference_tuple_inner(x, W_r, W_k, W_v, mu_r, mu_k):
            B, T, C = x.shape
            x_prev = jnp.concatenate([jnp.zeros((B, 1, C), x.dtype), x[:, :-1, :]], axis=1)
            xr = mu_r * x + (1.0 - mu_r) * x_prev
            xk = mu_k * x + (1.0 - mu_k) * x_prev
            r = jax.nn.sigmoid(jnp.einsum('btc,dc->btd', xr, W_r))
            k = jnp.einsum('btc,dc->btd', xk, W_k)
            k_act = jnp.square(jax.nn.relu(k))
            out = r * jnp.einsum('btc,dc->btd', k_act, W_v)
            new_state = x[:, -1, :]
            return (out, new_state)
        return _reference_tuple_inner(x, W_r, W_k, W_v, mu_r, mu_k)[0]

    def _L1_attn_ref(x, ln_g, ln_b, W_in, conv_w, conv_b, W_xproj, W_dt, b_dt, A_log, D, W_out):
        import jax, jax.numpy as jnp
        import numpy as np
        from jax import lax
        D_MODEL = 128
        D_STATE = 16
        D_CONV = 4
        EXPAND = 2
        D_INNER = EXPAND * D_MODEL
        DT_RANK = (D_MODEL + 15) // 16
        LN_EPS = 1e-05

        def _mamba_block(x, ln_g, ln_b, W_in, conv_w, conv_b, W_xproj, W_dt, b_dt, A_log, D, W_out):
            B, L, _ = x.shape
            mu = jnp.mean(x, axis=-1, keepdims=True)
            var = jnp.var(x, axis=-1, keepdims=True)
            h = (x - mu) * lax.rsqrt(var + LN_EPS) * ln_g + ln_b
            xz = jnp.einsum('bld,de->ble', h, W_in)
            u, z = jnp.split(xz, 2, axis=-1)
            u_t = jnp.transpose(u, (0, 2, 1))
            u_t = lax.conv_general_dilated(u_t, conv_w, window_strides=(1,), padding=[(D_CONV - 1, 0)], feature_group_count=D_INNER, dimension_numbers=('NCH', 'OIH', 'NCH'))
            u_t = u_t + conv_b[None, :, None]
            u = jax.nn.silu(jnp.transpose(u_t, (0, 2, 1)))
            x_dbl = jnp.einsum('bld,de->ble', u, W_xproj)
            dt, Bm, Cm = jnp.split(x_dbl, [DT_RANK, DT_RANK + D_STATE], axis=-1)
            dt = jax.nn.softplus(jnp.einsum('blr,rd->bld', dt, W_dt) + b_dt)
            A = -jnp.exp(A_log)
            dA = jnp.exp(jnp.einsum('bld,dn->bldn', dt, A))
            dBu = jnp.einsum('bld,bln->bldn', dt * u, Bm)

            def step(hc, inp):
                dA_t, dBu_t, C_t = inp
                hc = dA_t * hc + dBu_t
                y_t = jnp.einsum('bdn,bn->bd', hc, C_t)
                return (hc, y_t)
            h0 = jnp.zeros((B, D_INNER, D_STATE), x.dtype)
            xs = (jnp.transpose(dA, (1, 0, 2, 3)), jnp.transpose(dBu, (1, 0, 2, 3)), jnp.transpose(Cm, (1, 0, 2)))
            _, ys = lax.scan(step, h0, xs)
            y = jnp.transpose(ys, (1, 0, 2)) + u * D
            y = y * jax.nn.silu(z)
            out = jnp.einsum('bld,dm->blm', y, W_out)
            return x + out
        return _mamba_block(x, ln_g, ln_b, W_in, conv_w, conv_b, W_xproj, W_dt, b_dt, A_log, D, W_out)

    def _L1_ffn_ref(x, Wr, W1, b1, W2, b2):
        import jax, jax.numpy as jnp
        import numpy as np
        E, D, MULT, K = (8, 128, 4, 2)
        B, S = (4, 256)
        H = MULT * D
        probs = jax.nn.softmax(jnp.einsum('bsd,ed->bse', x, Wr), axis=-1)
        topv, topi = jax.lax.top_k(probs, K)
        combine = jnp.sum(topv[..., None] * jax.nn.one_hot(topi, E, dtype=x.dtype), axis=2)

        def body(acc, params):
            w1, bb1, w2, bb2, ce = params
            h = jax.nn.gelu(jnp.einsum('bsd,dh->bsh', x, w1) + bb1, approximate=False)
            y = jnp.einsum('bsh,hd->bsd', h, w2) + bb2
            return (acc + ce[..., None] * y, None)
        cE = jnp.moveaxis(combine, -1, 0)
        out, _ = jax.lax.scan(body, jnp.zeros_like(x), (W1, b1, W2, b2, cE))
        return out

    def _L2_attn_ref(x, qkv_w, proj_w, alpha_log, beta_log):
        import jax, jax.numpy as jnp
        import numpy as np
        DIM = 128
        H = 16
        HD = DIM // H
        EPS = 1e-06
        B, N = (1, 256)
        b, n, c = x.shape
        qkv = (x @ qkv_w.T).reshape(b, n, 3, H, HD).transpose(2, 0, 3, 1, 4)
        q, k, v = (qkv[0], qkv[1], qkv[2])
        phi_q = jax.nn.relu(q) + EPS
        phi_k = jax.nn.relu(k) + EPS
        kv = jnp.einsum('bhnd,bhne->bhnde', phi_k, v)
        S = jnp.cumsum(kv, axis=2)
        out = jnp.einsum('bhnd,bhnde->bhne', phi_q, S)
        alpha_p = jax.nn.softplus(alpha_log) + 1e-06
        beta_p = jax.nn.softplus(beta_log) + 1e-06
        scale = (alpha_p * beta_p * jnp.sqrt(jnp.float32(HD))).reshape(1, H, 1, 1)
        pos = jnp.arange(1, n + 1, dtype=x.dtype).reshape(1, 1, n, 1)
        denom = jnp.maximum(scale * pos, EPS)
        out = out / denom
        out = out.transpose(0, 2, 1, 3).reshape(b, n, c)
        return out @ proj_w.T

    def _L2_ffn_ref(x, w1_w, w1_s, w2_w, w2_s, h1_w, h1_s, h2_w, h2_s, w3_w, w3_s):
        import jax, jax.numpy as jnp
        import numpy as np
        D_IN, D_HID = (128, 512)

        def _ternary(key, shape):
            return jax.random.randint(key, shape, -1, 2).astype(jnp.float32)

        def _tlin(x, w, s):
            return jnp.einsum('bsi,oi->bso', x, w) * s
        h = jax.nn.silu(_tlin(x, w1_w, w1_s)) * _tlin(x, w2_w, w2_s)
        h = jax.nn.gelu(_tlin(h, h1_w, h1_s), approximate=False)
        h = jax.nn.gelu(_tlin(h, h2_w, h2_s), approximate=False)
        return _tlin(h, w3_w, w3_s)

    def _L3_attn_ref(x, W_in, W_A, W_B, W_C, W_out, norm_w):
        import jax, jax.numpy as jnp
        import numpy as np
        B, T, D_MODEL, N = (4, 256, 128, 16)
        D_INNER = 2 * D_MODEL

        def _ssm_scan(x_in, A, B_ssm, C_ssm):

            def step(state, ins):
                x_t, a_t, b_t, c_t = ins
                decay = jnp.exp(a_t)
                state = state * decay[:, None, :] + x_t[:, :, None] * b_t[:, None, :]
                out_t = (state * c_t[:, None, :]).sum(-1)
                return (state, out_t)
            b, t, d = x_in.shape
            n = A.shape[-1]
            init = jnp.zeros((b, d, n), dtype=x_in.dtype)
            xs = (jnp.swapaxes(x_in, 0, 1), jnp.swapaxes(A, 0, 1), jnp.swapaxes(B_ssm, 0, 1), jnp.swapaxes(C_ssm, 0, 1))
            _, outs = jax.lax.scan(step, init, xs)
            return jnp.swapaxes(outs, 0, 1)
        D = W_A.shape[0]
        xz = jnp.einsum('btm,md->btd', x, W_in)
        x_in = jax.nn.silu(xz[..., :D]) * jax.nn.sigmoid(xz[..., D:])
        A = -jnp.exp(jnp.clip(jnp.einsum('btd,dn->btn', x_in, W_A), -5.0, 0.0))
        B_ssm = jnp.einsum('btd,dn->btn', x_in, W_B)
        C_ssm = jnp.einsum('btd,dn->btn', x_in, W_C)
        out = _ssm_scan(x_in.astype(jnp.float32), A.astype(jnp.float32), B_ssm.astype(jnp.float32), C_ssm.astype(jnp.float32))
        out = out.astype(x.dtype)
        eps = jnp.finfo(jnp.float32).eps
        out = out * jax.lax.rsqrt(jnp.mean(out * out, axis=-1, keepdims=True) + eps) * norm_w
        return jnp.einsum('btd,dm->btm', out, W_out)

    def _L3_ffn_ref(x, Wg, w_gate, b_gate, w_up, b_up, w_down, b_down):
        import jax, jax.numpy as jnp
        import numpy as np
        K = 2
        B, S, D = x.shape
        E = Wg.shape[1]
        xt = x.reshape(B * S, D)
        logits = xt @ Wg
        probs = jax.nn.softmax(logits, axis=-1)
        topv, topi = jax.lax.top_k(probs, K)
        topv = topv / jnp.sum(topv, axis=-1, keepdims=True)
        combine = jnp.sum(jax.nn.one_hot(topi, E, dtype=xt.dtype) * topv[..., None], axis=1)
        g = jnp.einsum('nd,edf->enf', xt, w_gate) + b_gate[:, None, :]
        u = jnp.einsum('nd,edf->enf', xt, w_up) + b_up[:, None, :]
        h = jax.nn.silu(g) * u
        y = jnp.einsum('enf,efd->end', h, w_down) + b_down[:, None, :]
        out = jnp.einsum('ne,end->nd', combine, y)
        return out.reshape(B, S, D)
    x = L0_attn_x
    x = x + _L0_attn_ref(_layernorm(x, axis=-1), L0_attn_in_proj_w, L0_attn_conv_w, L0_attn_conv_b, L0_attn_A_param, L0_attn_ln_w, L0_attn_ln_b, L0_attn_out_proj_w)
    x = x + _L0_ffn_ref(_layernorm(x, axis=-1), L0_ffn_W_r, L0_ffn_W_k, L0_ffn_W_v, L0_ffn_mu_r, L0_ffn_mu_k)
    x = x + _L1_attn_ref(_layernorm(x, axis=-1), L1_attn_ln_g, L1_attn_ln_b, L1_attn_W_in, L1_attn_conv_w, L1_attn_conv_b, L1_attn_W_xproj, L1_attn_W_dt, L1_attn_b_dt, L1_attn_A_log, L1_attn_D, L1_attn_W_out)
    x = x + _L1_ffn_ref(_layernorm(x, axis=-1), L1_ffn_Wr, L1_ffn_W1, L1_ffn_b1, L1_ffn_W2, L1_ffn_b2)
    x = x + _L2_attn_ref(_layernorm(x, axis=-1), L2_attn_qkv_w, L2_attn_proj_w, L2_attn_alpha_log, L2_attn_beta_log)
    x = x + _L2_ffn_ref(_layernorm(x, axis=-1), L2_ffn_w1_w, L2_ffn_w1_s, L2_ffn_w2_w, L2_ffn_w2_s, L2_ffn_h1_w, L2_ffn_h1_s, L2_ffn_h2_w, L2_ffn_h2_s, L2_ffn_w3_w, L2_ffn_w3_s)
    x = x + _L3_attn_ref(_layernorm(x, axis=-1), L3_attn_W_in, L3_attn_W_A, L3_attn_W_B, L3_attn_W_C, L3_attn_W_out, L3_attn_norm_w)
    x = x + _L3_ffn_ref(_layernorm(x, axis=-1), L3_ffn_Wg, L3_ffn_w_gate, L3_ffn_b_gate, L3_ffn_w_up, L3_ffn_b_up, L3_ffn_w_down, L3_ffn_b_down)
    return x

_drawn_inputs = setup_inputs


def setup_inputs(seed=0):
    import zlib

    import numpy as np

    out = dict(_drawn_inputs(seed))
    spreads = {'L0_attn_ln_w': (1.0, 0.2),
     'L0_attn_ln_b': (0.0, 0.1),
     'L1_attn_ln_g': (1.0, 0.2),
     'L1_attn_ln_b': (0.0, 0.1),
     'L1_attn_conv_b': (0.0, 0.1),
     'L1_attn_D': (1.0, 0.2),
     'L1_ffn_b1': (0.0, 0.1),
     'L1_ffn_b2': (0.0, 0.1),
     'L2_attn_alpha_log': (0.0, 0.1),
     'L2_attn_beta_log': (0.0, 0.1),
     'L3_attn_norm_w': (1.0, 0.2)}
    factors = {}
    for name, (base, spread) in spreads.items():
        noise = np.random.default_rng([zlib.crc32(name.encode()), seed]).standard_normal(out[name].shape)
        drawn = base * np.exp(spread * noise) if base else spread * noise
        out[name] = jnp.asarray(drawn.astype(out[name].dtype))
    for name, factor in factors.items():
        out[name] = (out[name] * factor).astype(out[name].dtype)
    return out
```

```python
from contextlib import ExitStack

import concourse.bass as bass
from concourse import mybir

F32 = mybir.dt.float32
BF16 = mybir.dt.bfloat16
U32 = mybir.dt.uint32
I32 = mybir.dt.int32
ALU = mybir.AluOpType
ACT = mybir.ActivationFunctionType
AX = mybir.AxisListType

P = 128
T = 512
NC = T // P
NS = 2
PAD = 3
NE = 8
DI = 1024
NB0 = DI // P
N0 = 64
N3 = 16
NM = 16
REF = T - P
STEEPEST = 1.2
LN_EPS = 1e-5
RMS_EPS = 1.1920928955078125e-07
EPS6 = 1e-6

WCOLS = [("l0_in", 17 * P), ("l0_out", 8 * P), ("f0_r", P), ("f0_k", P), ("f0_v", P),
         ("m_in", 4 * P), ("m_dt", 2 * 8), ("m_bc", 2 * 96), ("m_out", 2 * P), ("r1", NE),
         ("a_qkv", 3 * P), ("a_out", P), ("t_w1", 4 * P), ("t_w2", 4 * P), ("t_h1", 16 * P),
         ("t_h2", 16 * P), ("t_w3", 4 * P), ("s_in", 4 * P), ("s_abc", 2 * 48), ("s_out", 2 * P),
         ("r3", NE)]
WOFF = {}
_n = 0
for _k, _w in WCOLS:
    WOFF[_k] = (_n, _w)
    _n += _w
WTOT = _n
PCOLS = [("conv0_w", 32), ("conv0_b", 8), ("lnw", 8), ("lnb", 8), ("mu_r", 1), ("mu_k", 1),
         ("g1", 1), ("b1g", 1), ("conv1_w", 8), ("conv1_b", 2), ("b_dt", 2), ("alog", 32), ("dm", 2),
         ("mb1", 32), ("w1_s", 4), ("w2_s", 4), ("h1_s", 4), ("h2_s", 4), ("normw", 2),
         ("bg", 32), ("bu", 32), ("alpha", 1), ("beta", 1), ("a0", 1), ("w3_s", P)]
POFF = {}
_n = 0
for _k, _w in PCOLS:
    POFF[_k] = (_n, _w)
    _n += _w
PTOT = _n
CCOLS = [("ident", P), ("tri", T), ("iota8", NE), ("pos", T), ("m_ref", REF + 64), ("mod128", T),
         ("mod64", T), ("pick", 32)]
COFF = {}
_n = 0
for _k, _w in CCOLS:
    COFF[_k] = (_n, _w)
    _n += _w
CTOT = _n

OFF_RECT = [0, 0, P, 3 * P]
OFF_D0 = 6 * P
OFF_D1 = OFF_D0 + T
NKEY = OFF_D1 + T
OFF_MT = [0, 512, 896, 1152]
NMT = 1280
RING = 3
NLAYERS = 8


class Signal:

    def __init__(self, sem, per):
        self.sem, self.per = sem, per

    def at(self, piece, k=None):
        return piece * self.per + (self.per if k is None else k + 1)


def network(nc, x_d, w_d, p_d, c_d, sel_d, a_d, e1_d, e3_d, r8_d, out_d, layers=NLAYERS):
    ctx = ExitStack()
    signals = []

    def sb(name, shape, dt=F32):
        return ctx.enter_context(nc.sbuf_tensor(name, shape, dt))

    def sem(name):
        h = ctx.enter_context(nc.semaphore(name))
        return h

    def S(name, per):
        s = Signal(sem(name), per)
        signals.append(s.sem)
        return s

    with ctx:
        W = sb("weights", [P, WTOT])
        PR = sb("params", [P, PTOT])
        CN = sb("consts", [P, COFF["pos"][0]])
        SEL = sb("selectors", [P, 24 * P])
        R8 = sb("rows8", [NE, 4 * P])
        ring = sb("expert_ring", [P, RING, 1536])
        PS = ctx.enter_context(nc.psum_tensor("ps", [P, 8, T], F32))
        X = [sb(f"x{s}", [P, NC, P]) for s in range(NS)]
        XN = [sb(f"xn{s}", [P, NC, P]) for s in range(NS)]
        XT = [sb(f"xT{s}", [P, PAD + T]) for s in range(NS)]
        BIG1 = [sb(f"big1_{s}", [P, 8, T]) for s in range(NS)]
        BIG2 = [sb(f"big2_{s}", [P, 4, T]) for s in range(NS)]
        MT = [sb(f"mt{s}", [P, NMT]) for s in range(NS)]
        KEY = [sb(f"key{s}", [P, NKEY]) for s in range(NS)]
        Q128 = [sb(f"q128_{s}", [N0, T]) for s in range(NS)]
        Q64 = [sb(f"q64_{s}", [N0, T]) for s in range(NS)]
        BT = [sb(f"bT{s}", [N0, T]) for s in range(NS)]
        UP = [sb(f"up{s}", [P, 2, PAD + T]) for s in range(NS)]
        CV = [sb(f"cv{s}", [P, 2, T]) for s in range(NS)]
        XH = [CV[s][:, 0, :].rearrange("p (c n) -> p c n", c=NC) for s in range(NS)]
        SETUP = BIG1[0][:, :, :].rearrange("p k n -> p (k n)")
        SPL = [sb(f"split{s}", [96, T], BF16) for s in range(NS)]
        SM = sb("row_pick", [96, 32], BF16)
        ekey = sb("ekey", [N0, REF + 64])
        eq128 = sb("eq128", [N0, T])
        eq64 = sb("eq64", [N0, T])
        rden = sb("rden", [P, T])
        nega = sb("nega", [P, 2 * NM])
        omu = sb("omu", [P, 2])
        nhalf = sb("nhalf", [P, NC])
        ones = sb("ones", [P, 1])
        sc = sb("setup_cols", [P, 17])
        stat = [sb(f"stat{s}", [P, NC, 2, 6]) for s in range(NS)]
        mv = [sb(f"mv{s}", [P, NC, 2]) for s in range(NS)]
        ve = [sb(f"ve{s}", [P, NC]) for s in range(NS)]
        rstd = [sb(f"rstd{s}", [P, NC]) for s in range(NS)]
        flag = sb("all_alike", [1, 1], I32)
        ones64 = sb("ones64", [N0, P])
        negr = [sb(f"negr{s}", [N3, 8]) for s in range(NS)]
        lg = [sb(f"lg{s}", [P, 4, NC, NE]) for s in range(NS)]
        top = [sb(f"top{s}", [P, NC, 8]) for s in range(NS)]
        topi = [sb(f"topi{s}", [P, NC, 8], U32) for s in range(NS)]
        topf = [sb(f"topf{s}", [P, NC, 8]) for s in range(NS)]
        cmb = [sb(f"cmb{s}", [P, NC, NE]) for s in range(NS)]
        cmbT = [BT[s][0:NE, :] for s in range(NS)]
        sm4 = [sb(f"sm4_{s}", [P, 4, NC]) for s in range(NS)]

        in_sem = {n: sem(f"in_{n}") for n in ("p", "c", "sel", "r8", "a")}
        wsem = [sem(f"in_w{i}") for i in range(4)]
        setup_dve = sem("setup_dve")
        setup_act = sem("setup_act")
        setup_pe = sem("setup_pe")
        known = sem("known")
        ready = sem("setup_ready")
        arrived = sem("arrived")
        go = {e: sem(f"go_{e}") for e in ("pe", "act", "dve", "pool")}
        stored = sem("stored")

        ring_in = [S(f"ring_in{i}", 1) for i in range(RING)]
        dve_own = S("dve_own", 1)
        act_own = S("act_own", 1)
        pool_own = S("pool_own", 1)
        x_in = [S(f"x_in{s}", 1) for s in range(NS)]
        x_done = S("x_done", 1)
        ln_var = S("ln_var", 1)
        ln_rstd = S("ln_rstd", 1)
        ln_norm = S("ln_norm", 1)
        ln_T = S("ln_T", 1)
        ln_xT = S("ln_xT", 1)
        l0_bc = S("l0_bc", 2)
        l0_bt = S("l0_bt", 1)
        l0_q = S("l0_q", 2)
        key_f = S("key_f", 1)
        l0_sc = S("l0_sc", 4)
        l0_mt = S("l0_mt", 4)
        l0_z = S("l0_z", 8)
        l0_zs = S("l0_zs", 8)
        l0_u = S("l0_u", 4)
        l0_up = S("l0_up", 4)
        l0_cv = S("l0_cv", 4)
        l0_sl = S("l0_sl", 4)
        l0_xt = S("l0_xt", 4)
        l0_xc = S("l0_xc", 4)
        l0_y = S("l0_y", 4)
        l0_yg = S("l0_yg", 4)
        l0_var = S("l0_var", 1)
        l0_rs = S("l0_rs", 1)
        l0_nm = S("l0_nm", 4)
        l0_yt = S("l0_yt", 4)
        l0_yn = S("l0_yn", 4)
        l0_o = S("l0_o", 1)
        g_c = S("g_c", 1)
        g_cs = S("g_cs", 1)
        g_a = S("g_a", 1)
        g_dma = S("g_dma", 1)
        g_u = S("g_u", 1)
        g_up = S("g_up", 1)
        g_cv = S("g_cv", 1)
        g_sl = S("g_sl", 1)
        g_row = S("g_row", N0)
        g_ps = S("g_ps", N0)
        g_sum = S("g_sum", 1)
        g_t = S("g_t", 1)
        g_yg = S("g_yg", 1)
        f0_mix = S("f0_mix", 2)
        f0_p = S("f0_p", 3)
        f0_rl = S("f0_rl", 1)
        f0_sg = S("f0_sg", 1)
        f0_ka = S("f0_ka", 1)
        m_uz = S("m_uz", 4)
        m_up = S("m_up", 2)
        m_z = S("m_z", 2)
        m_cv = S("m_cv", 2)
        m_u = S("m_u", 2)
        m_xd = S("m_xd", 2)
        m_d8 = S("m_d8", 1)
        m_sp3 = S("m_sp3", 1)
        m_dt = S("m_dt", 2)
        m_sp = S("m_sp", 2)
        m_du = S("m_du", 2)
        m_bc = S("m_bc", 2)
        m_bs = S("m_bs", 1)
        m_da = S("m_da", 2)
        m_d0 = S("m_d0", 1)
        m_d1 = S("m_d1", 1)
        m_sc = S("m_sc", 2)
        m_hc = S("m_hc", 1)
        m_ya = S("m_ya", 1)
        m_y = S("m_y", 2)
        m_o = S("m_o", 1)
        r_lg = S("r_lg", 1)
        r_sh = S("r_sh", 1)
        r_ex = S("r_ex", 1)
        r_cb = S("r_cb", 1)
        r_ct = S("r_ct", 1)
        r_cs = S("r_cs", 1)
        r_b = S("r_b", 1)
        r_bx = S("r_bx", 1)
        e_up = S("e_up", 1)
        e_act = S("e_act", 1)
        e_h = S("e_h", 1)
        e_dn = S("e_dn", 1)
        e_x = S("e_x", 1)
        a_p = S("a_p", 3)
        a_f = S("a_f", 3)
        a_r = S("a_r", 3)
        a_ks = S("a_ks", 1)
        a_kv = S("a_kv", 1)
        a_qs = S("a_qs", 1)
        a_cum = S("a_cum", 1)
        a_qk = S("a_qk", 1)
        a_red = S("a_red", 1)
        a_o = S("a_o", 1)
        a_y = S("a_y", 1)
        t_ab = S("t_ab", 2)
        t_sa = S("t_sa", 1)
        t_h0 = S("t_h0", 1)
        t_p1 = S("t_p1", 4)
        t_g1 = S("t_g1", 4)
        t_p2 = S("t_p2", 4)
        t_g2 = S("t_g2", 4)
        t_o = S("t_o", 1)
        s_ab = S("s_ab", 4)
        s_sl = S("s_sl", 2)
        s_sg = S("s_sg", 2)
        s_xi = S("s_xi", 2)
        s_abc = S("s_abc", 3)
        s_ea = S("s_ea", 1)
        s_cl = S("s_cl", 1)
        s_cp = S("s_cp", 1)
        s_cum = S("s_cum", 1)
        s_ex = S("s_ex", 1)
        s_f = S("s_f", 1)
        s_xt = S("s_xt", 2)
        s_xs = S("s_xs", 2)
        s_sc = S("s_sc", 4)
        s_mt = S("s_mt", 4)
        s_y = S("s_y", 2)
        s_yt = S("s_yt", 2)
        s_o = S("s_o", 2)
        s_var = S("s_var", 1)
        s_rs = S("s_rs", 1)

        def w(name, lo=0, n=None):
            o, width = WOFF[name]
            return W[:, o + lo:o + (width if n is None else lo + n)]

        def pr(name, j=0, n=1):
            o, _ = POFF[name]
            return PR[:, o + j:o + j + n]

        def cn(name, rows=P):
            o, width = COFF[name]
            kept = COFF["pos"][0]
            return CN[0:rows, o:o + width] if o < kept else SETUP[0:rows, o - kept:o - kept + width]

        def bank(s, k):
            return PS[:, 4 * s + k, :]

        def bank4(s, k):
            return PS[:, 4 * s + k, :].rearrange("p (c n) -> p c n", c=NC)

        def chunk(s, c, shift=0):
            return XT[s][:, PAD + c * P - shift:PAD + (c + 1) * P - shift]

        ident = cn("ident")
        STREAMS = range(NS)
        HALVES = range(2)
        L0, L0F, L1, L1F, L2, L2F, L3, L3F = range(8)
        on = [i < layers for i in range(8)]
        LNI = {L0: 0, L0F: 1, "outer": 2, L1: 3, L1F: 4, L2: 5, L2F: 6, L3: 7, L3F: 8}

        def turn_index(i):
            return i if i < 2 else i - 1

        block = ctx.enter_context(nc.Block())

        @block.sync
        def _(sp):
            sp.dma_start(BIG1[1][:, 0, :], a_d).then_inc(in_sem["a"], 16)
            sp.dma_start(PR[:], p_d).then_inc(in_sem["p"], 16)
            kept = COFF["pos"][0]
            sp.dma_start(CN[:], c_d[:, 0:kept]).then_inc(in_sem["c"], 16)
            sp.dma_start(SETUP[:, 0:CTOT - kept], c_d[:, kept:CTOT]).then_inc(in_sem["c"], 16)
            cuts = [0, WOFF["f0_r"][0], WOFF["a_qkv"][0], WOFF["s_in"][0], WTOT]
            sp.dma_start(W[:, cuts[0]:cuts[1]], w_d[:, cuts[0]:cuts[1]]).then_inc(wsem[0], 16)
            sp.dma_start(R8[:], r8_d).then_inc(in_sem["r8"], 16)
            for i in (1, 2, 3):
                sp.dma_start(W[:, cuts[i]:cuts[i + 1]], w_d[:, cuts[i]:cuts[i + 1]]).then_inc(wsem[i], 16)
            sp.dma_start(SEL[:], sel_d).then_inc(in_sem["sel"], 16)
            with sp.Fori(0, 4 // NS) as i:
                for s in STREAMS:
                    sp.dma_start(X[s][:], x_d[i * NS + s]).then_inc(x_in[s].sem, 16)
                for q in range(2 * NE):
                    if not on[L1F if q < NE else L3F]:
                        continue
                    if q >= RING:
                        sp.wait_ge(e_dn.sem, e_dn.at(2 * (q - RING) + 1))
                    slot = q % RING
                    if q < NE:
                        sp.dma_start(ring[:, slot, 0:1024], e1_d[q]).then_inc(ring_in[slot].sem, 16)
                    else:
                        sp.dma_start(ring[:, slot, :], e3_d[q - NE]).then_inc(ring_in[slot].sem, 16)
                for s in STREAMS:
                    sp.wait_ge(x_done.sem, x_done.at((layers - 1) * NS + s))
                    sp.dma_start(out_d[i * NS + s], X[s][:]).then_inc(stored, 16)
                sp.wait_ge(stored, 16 * NS)
                sp.wait_ge(arrived, 4)
                sp.sem_clear(arrived)
                sp.sem_clear(stored)
                for x in signals:
                    sp.sem_clear(x)
                sp.drain()
                for e in ("pe", "act", "dve", "pool"):
                    sp.sem_inc(go[e], 1)

        def end_of_pair(eng, name):
            eng.drain().then_inc(arrived, 1)
            eng.wait_ge(go[name], 1)
            eng.sem_clear(go[name])

        @block.gpsimd
        def _(pool):
            pool.wait_ge(ready, 2)

            def power(src, dst, done):
                pool.tensor_tensor(dst, src, nhalf[:, :], ALU.pow).then_inc(done.sem, 1)

            def ln(i):
                for s in STREAMS:
                    pool.wait_ge(ln_var.sem, ln_var.at(i * NS + s))
                    power(ve[s][:, :], rstd[s][:, :], ln_rstd)

            def keys_l0():
                for s in STREAMS:
                    pool.wait_ge(l0_bt.sem, l0_bt.at(s))
                    for c in range(1, NC):
                        pool.tensor_tensor(KEY[s][0:N0, OFF_RECT[c]:OFF_RECT[c] + c * P], BT[s][:, 0:c * P],
                                           ekey[:, REF - c * P:REF], ALU.mult)
                    b4 = BT[s][:, :].rearrange("p (c n) -> p c n", c=NC)
                    k0 = KEY[s][0:N0, OFF_D0:OFF_D0 + T].rearrange("p (c n) -> p c n", c=NC)
                    k1 = KEY[s][0:N0, OFF_D1:OFF_D1 + T].rearrange("p (c n) -> p c n", c=NC)
                    pool.tensor_tensor(k0[:, :, 0:64], b4[:, :, 0:64],
                                       ekey[:, REF:REF + 64].unsqueeze(1).broadcast_to([N0, NC, 64]), ALU.mult)
                    pool.tensor_tensor(k1, b4, ekey[:, REF - 64:REF + 64].unsqueeze(1).broadcast_to([N0, NC, P]),
                                       ALU.mult).then_inc(key_f.sem, 1)

            def scan_inputs():
                for q in range(NM * NS):
                    s = q % NS
                    pool.wait_ge(m_bs.sem, m_bs.at(q))
                    if q < NS:
                        pool.wait_ge(m_du.sem, m_du.at(s))
                    if q >= NS:
                        pool.wait_ge(m_sc.sem, m_sc.at(q - NS, 1))
                    pool.tensor_tensor(BIG2[s][:, 1, :], BIG1[s][:, 3, :], MT[s][:, 0:T], ALU.mult)\
                        .then_inc(m_d1.sem, 1)

            with pool.Fori(0, 4 // NS):
                if on[L0]:
                    ln(LNI[L0])
                    keys_l0()
                    for s in STREAMS:
                        pool.wait_ge(l0_var.sem, l0_var.at(s))
                        power(ve[s][:, :], rstd[s][:, :], l0_rs)
                if on[L0F]:
                    ln(LNI[L0F])
                if on[L1]:
                    ln(LNI["outer"])
                    ln(LNI[L1])
                    scan_inputs()
                for layer in (L1F, L2, L2F, L3):
                    if on[layer]:
                        ln(LNI[layer])
                if on[L3]:
                    for s in STREAMS:
                        pool.wait_ge(s_var.sem, s_var.at(s))
                        power(ve[s][:, :], rstd[s][:, :], s_rs)
                if on[L3F]:
                    ln(LNI[L3F])
                end_of_pair(pool, "pool")

        @block.scalar
        def _(act):
            own = [0]

            def step(ins):
                own[0] += 1
                ins.then_inc(act_own.sem, 1)
                act.wait_ge(act_own.sem, own[0])

            def setup():
                act.wait_ge(in_sem["p"], 16)
                act.wait_ge(in_sem["c"], 32)
                act.activation(sc[0:N0, 0:1], pr("a0")[0:N0], ACT.Exp).then_inc(setup_act, 1)
                act.activation(nega[:, :], pr("alog", 0, 32), ACT.Exp).then_inc(setup_act, 1)
                act.activation(sc[:, 2:3], pr("alpha"), ACT.Exp).then_inc(setup_act, 1)
                act.activation(sc[:, 3:4], pr("beta"), ACT.Exp).then_inc(setup_act, 1)
                act.wait_ge(setup_act, 4)
                act.wait_ge(setup_dve, 2)
                act.activation(ekey[:, :], cn("m_ref", N0), ACT.Exp, scale=sc[0:N0, 16:17])
                act.activation(eq128[:, :], cn("mod128", N0), ACT.Exp, scale=sc[0:N0, 1:2])
                act.activation(eq64[:, :], cn("mod64", N0), ACT.Exp, scale=sc[0:N0, 1:2])
                act.activation(sc[:, 4:6], sc[:, 2:4], ACT.Ln, bias=1.0).then_inc(setup_act, 1)
                act.wait_ge(setup_act, 5)
                act.drain().then_inc(ready, 1)

            def turned(i, gain=None):
                for s in STREAMS:
                    act.wait_ge(ln_T.sem, ln_T.at(turn_index(i) * NS + s))
                    if gain:
                        act.activation(XT[s][:, PAD:PAD + T], bank(s, 3), ACT.Identity, bias=pr("b1g"),
                                       scale=pr("g1")).then_inc(ln_xT.sem, 1)
                    else:
                        act.activation(XT[s][:, PAD:PAD + T], bank(s, 3), ACT.Copy).then_inc(ln_xT.sem, 1)

            def state_space():
                for s in STREAMS:
                    act.wait_ge(l0_bc.sem, l0_bc.at(s, 0))
                    act.activation(BT[s][:, :], bank(s, 0)[0:N0, :], ACT.Copy).then_inc(l0_bt.sem, 1)
                for s in STREAMS:
                    for k in range(8):
                        c, h = k // 2, k % 2
                        act.wait_ge(l0_z.sem, l0_z.at(s, k))
                        act.activation(BIG1[s][:, 2 * c + h, :], bank(s, k % 4), ACT.Silu).then_inc(l0_zs.sem, 1)
                with act.If(alike == 1):
                    inputs_alike()
                with act.Else():
                    inputs_general()
                for h in HALVES:
                    for s in STREAMS:
                        g = h * NS + s
                        if h == 1:
                            act.wait_ge(l0_o.sem, l0_o.at(s))
                        for j in range(4):
                            act.wait_ge(l0_yt.sem, l0_yt.at(g, j))
                            act.activation(BIG2[s][:, j, :], bank(s, j % 2), ACT.Identity,
                                           bias=pr("lnb", 4 * h + j), scale=pr("lnw", 4 * h + j))\
                                .then_inc(l0_yn.sem, 1)

            def inputs_alike():
                for h in HALVES:
                    for s in STREAMS:
                        g = h * NS + s
                        for k in range(4 + 3):
                            if k < 4:
                                act.wait_ge(l0_u.sem, l0_u.at(g, k))
                                if k >= 2:
                                    act.wait_ge(l0_cv.sem, l0_cv.at(g, k - 2))
                                elif g >= NS:
                                    act.wait_ge(l0_cv.sem, l0_cv.at(g - NS, k + 2))
                                act.activation(UP[s][:, k % 2, PAD:PAD + T], bank(s, k % 2), ACT.Copy)\
                                    .then_inc(l0_up.sem, 1)
                            if 1 <= k <= 4:
                                j = k - 1
                                act.wait_ge(l0_cv.sem, l0_cv.at(g, j))
                                act.activation(CV[s][:, j % 2, :], CV[s][:, j % 2, :], ACT.Silu)\
                                    .then_inc(l0_sl.sem, 1)
                            if 2 <= k <= 5:
                                j = k - 2
                                act.wait_ge(l0_xt.sem, l0_xt.at(g, j))
                                if j == 0 and h == 1:
                                    act.wait_ge(l0_y.sem, l0_y.at(s))
                                act.activation(BIG2[s][:, :, j * P:(j + 1) * P], bank4(s, 2 + j % 2), ACT.Copy)\
                                    .then_inc(l0_xc.sem, 1)

            def inputs_general():
                act.wait_ge(key_f.sem, key_f.at(NS - 1))
                decay = KEY[1][:, 0:NB0 * N0]
                act.dma_start(decay, a_d).then_inc(g_dma.sem, 16)
                act.wait_ge(g_dma.sem, 16)
                act.activation(decay, decay, ACT.Exp)
                act.drain()
                act.activation(decay, decay, ACT.Exp, scale=-1.0).then_inc(g_a.sem, 1)
                for s in STREAMS:
                    act.wait_ge(g_c.sem, g_c.at(s))
                    act.activation(Q64[s][:, :], bank(s, 1)[0:N0, :], ACT.Copy).then_inc(g_cs.sem, 1)
                    for j in range(NB0):
                        g = s * NB0 + j
                        act.wait_ge(g_u.sem, g_u.at(g))
                        act.activation(UP[s][:, 0, PAD:PAD + T], bank(s, 0), ACT.Copy).then_inc(g_up.sem, 1)
                        act.wait_ge(g_cv.sem, g_cv.at(g))
                        act.activation(CV[s][:, 0, :], CV[s][:, 0, :], ACT.Silu).then_inc(g_sl.sem, 1)

            def feed_forward():
                for s in STREAMS:
                    act.wait_ge(f0_p.sem, f0_p.at(s, 0))
                    act.activation(BIG1[s][:, 4, :], bank(s, 0), ACT.Relu).then_inc(f0_rl.sem, 1)
                for s in STREAMS:
                    act.wait_ge(f0_p.sem, f0_p.at(s, 1))
                    act.activation(BIG1[s][:, 6, :], bank(s, 1), ACT.Sigmoid).then_inc(f0_sg.sem, 1)

            def mamba():
                for s in STREAMS:
                    for j in range(2):
                        act.wait_ge(m_uz.sem, m_uz.at(s, j))
                        act.activation(UP[s][:, j, PAD:PAD + T], bank(s, j), ACT.Copy).then_inc(m_up.sem, 1)
                    for j in range(2):
                        act.wait_ge(m_uz.sem, m_uz.at(s, 2 + j))
                        act.activation(BIG1[s][:, 6 + j, :], bank(s, 2 + j), ACT.Silu).then_inc(m_z.sem, 1)
                    for j in range(2):
                        act.wait_ge(m_cv.sem, m_cv.at(s, j))
                        act.activation(BIG1[s][:, 4 + j, :], CV[s][:, j, :], ACT.Silu).then_inc(m_u.sem, 1)
                for s in STREAMS:
                    act.wait_ge(m_xd.sem, m_xd.at(s, 0))
                    act.activation(BT[s][0:8, :], bank(s, 0)[0:8, :], ACT.Copy).then_inc(m_d8.sem, 1)
                for s in STREAMS:
                    for j in range(2):
                        act.wait_ge(m_dt.sem, m_dt.at(s, j))
                        act.activation(CV[s][:, j, :], bank(s, 2 + j), ACT.Abs, bias=pr("b_dt", j))
                        step(act.activation(UP[s][:, j, PAD:PAD + T], bank(s, 2 + j), ACT.Relu, bias=pr("b_dt", j)))
                    step(act.activation(CV[s][:, :, :], CV[s][:, :, :], ACT.Exp, scale=-1.0))
                    for j in range(2):
                        act.activation(CV[s][:, j, :], CV[s][:, j, :], ACT.Ln, bias=1.0).then_inc(m_sp.sem, 1)
                for q in range(NM * NS):
                    n, s = q // NS, q % NS
                    act.wait_ge(m_bc.sem, m_bc.at(q, 0))
                    if q >= NS:
                        act.wait_ge(m_d1.sem, m_d1.at(q - NS))
                    act.activation(MT[s][:, 0:T], bank(s, 2), ACT.Copy).then_inc(m_bs.sem, 1)
                    for j in range(2):
                        if q < NS:
                            act.wait_ge(m_du.sem, m_du.at(s, j))
                        else:
                            act.wait_ge(m_sc.sem, m_sc.at(q - NS, j))
                        act.activation(CV[s][:, j, :], BIG1[s][:, j, :], ACT.Exp,
                                       scale=nega[:, j * NM + n:j * NM + n + 1]).then_inc(m_da.sem, 1)

            def route(m, i):
                for s in STREAMS:
                    act.wait_ge(r_sh.sem, r_sh.at(m * NS + s))
                    act.activation(lg[s][:, 1], lg[s][:, 0], ACT.Exp).then_inc(r_ex.sem, 1)
                for s in STREAMS:
                    act.wait_ge(r_ct.sem, r_ct.at(m * NS + s))
                    act.activation(cmbT[s][:, :], bank(s, 3)[0:NE, :], ACT.Copy).then_inc(r_cs.sem, 1)

            def experts_gelu():
                for q in range(NE * NS):
                    e, s = q // NS, q % NS
                    for k in range(4):
                        act.wait_ge(e_up.sem, q * 4 + k + 1)
                        if k == 0 and q >= 2 * NS:
                            act.wait_ge(e_dn.sem, e_dn.at(q - 2 * NS))
                        act.activation(BIG1[s][:, 4 * (e % 2) + k, :], bank(s, k % 3), ACT.Gelu,
                                       bias=pr("mb1", 4 * e + k)).then_inc(e_act.sem, 1)

            def experts_silu():
                for q in range(NE * NS):
                    e, s = q // NS, q % NS
                    for k in range(4):
                        act.wait_ge(e_up.sem, 64 + 8 * q + 2 * k + 1)
                        if k >= 2:
                            act.wait_ge(e_h.sem, 4 * q + k - 2 + 1)
                        elif q >= NS:
                            act.wait_ge(e_h.sem, 4 * (q - NS) + k + 2 + 1)
                        act.activation(CV[s][:, k % 2, :], bank(s, (2 * k) % 4), ACT.Silu,
                                       bias=pr("bg", 4 * e + k)).then_inc(e_act.sem, 1)

            def attention():
                for b in range(NB0):
                    for s in STREAMS:
                        g = b * NS + s
                        act.wait_ge(a_r.sem, a_r.at(g, 0))
                        if b:
                            act.wait_ge(a_kv.sem, a_kv.at(g - NS))
                        act.activation(CV[s][:, 0, :], bank(s, 0), ACT.Copy).then_inc(a_ks.sem, 1)

            def ternary():
                for s in STREAMS:
                    for j in range(4):
                        act.wait_ge(t_ab.sem, t_ab.at(4 * s + j, 0))
                        if j >= 2:
                            act.wait_ge(t_h0.sem, t_h0.at(4 * s + j - 2))
                        act.activation(CV[s][:, j % 2, :], bank(s, j % 2), ACT.Silu, scale=pr("w1_s", j))\
                            .then_inc(t_sa.sem, 1)
                for p, g, src, dst in ((t_p1, t_g1, "h1_s", 4), (t_p2, t_g2, "h2_s", 0)):
                    for s in STREAMS:
                        for j in range(4):
                            act.wait_ge(p.sem, p.at(s, j))
                            if dst == 0 and j == 0:
                                act.wait_ge(t_p1.sem, t_p1.at(s))
                            act.activation(BIG1[s][:, dst + j, :], bank(s, j), ACT.Gelu, scale=pr(src, j))\
                                .then_inc(g.sem, 1)

            def last_scan():
                for s in STREAMS:
                    for j in range(2):
                        act.wait_ge(s_ab.sem, s_ab.at(s, j))
                        act.activation(CV[s][:, j, :], bank(s, j), ACT.Silu).then_inc(s_sl.sem, 1)
                for s in STREAMS:
                    for j in range(2):
                        act.wait_ge(s_ab.sem, s_ab.at(s, 2 + j))
                        act.activation(UP[s][:, j, PAD:PAD + T], bank(s, 2 + j), ACT.Sigmoid).then_inc(s_sg.sem, 1)
                for s in STREAMS:
                    act.wait_ge(s_cl.sem, s_cl.at(s))
                    act.activation(BT[s][0:N3, :], BT[s][0:N3, :], ACT.Exp).then_inc(s_ea.sem, 1)
                for s in STREAMS:
                    act.wait_ge(s_cum.sem, s_cum.at(s))
                    cum = BT[s][0:N3, :]
                    for c in range(NC):
                        a = c * P
                        act.activation(Q128[s][0:N3, a:a + P], cum[:, a:a + P], ACT.Exp, scale=-1.0, bias=cum[:, a:a + 1])
                        act.activation(Q64[s][0:N3, a + 64:a + P], cum[:, a + 64:a + P], ACT.Exp, scale=-1.0,
                                       bias=cum[:, a + 64:a + 65])
                        if c:
                            act.activation(KEY[s][0:N3, OFF_RECT[c]:OFF_RECT[c] + a], cum[:, 0:a], ACT.Exp,
                                           bias=negr[s][:, 2 * c:2 * c + 1])
                        act.activation(KEY[s][0:N3, OFF_D0 + a:OFF_D0 + a + 64], cum[:, a:a + 64], ACT.Exp,
                                       bias=negr[s][:, 2 * c:2 * c + 1])
                        last = act.activation(KEY[s][0:N3, OFF_D1 + a:OFF_D1 + a + P], cum[:, a:a + P], ACT.Exp,
                                              bias=negr[s][:, 2 * c + 1:2 * c + 2])
                    last.then_inc(s_ex.sem, 1)
                for s in STREAMS:
                    for j in range(2):
                        act.wait_ge(s_xt.sem, s_xt.at(s, j))
                        act.activation(BIG2[s][:, :, j * P:(j + 1) * P], bank4(s, 2 + j), ACT.Copy)\
                            .then_inc(s_xs.sem, 1)
                for s in STREAMS:
                    for j in range(2):
                        act.wait_ge(s_y.sem, s_y.at(s, j))
                        act.activation(BIG1[s][:, 2 + j, :], bank(s, j), ACT.Copy)
                        act.activation(BIG1[s][:, 4 + j, :], bank(s, j), ACT.Square).then_inc(s_yt.sem, 1)

            setup()
            act.wait_ge(known, 3)
            alike = act.value_load(flag[0:1, 0:1], min_val=0, max_val=1)
            with act.Fori(0, 4 // NS):
                if on[L0]:
                    turned(LNI[L0])
                    state_space()
                if on[L0F]:
                    turned(LNI[L0F])
                    feed_forward()
                if on[L1]:
                    turned(LNI[L1], gain=True)
                    mamba()
                if on[L1F]:
                    turned(LNI[L1F])
                    route(0, L1F)
                    experts_gelu()
                if on[L2]:
                    turned(LNI[L2])
                    attention()
                if on[L2F]:
                    turned(LNI[L2F])
                    ternary()
                if on[L3]:
                    turned(LNI[L3])
                    last_scan()
                if on[L3F]:
                    turned(LNI[L3F])
                    route(1, L3F)
                    experts_silu()
                end_of_pair(act, "act")

        @block.vector
        def _(dve):
            own = [0]

            def step(ins):
                own[0] += 1
                ins.then_inc(dve_own.sem, 1)
                dve.wait_ge(dve_own.sem, own[0])

            def setup():
                for s in STREAMS:
                    dve.memset(XT[s][:, 0:PAD], 0.0)
                    dve.memset(UP[s][:, :, 0:PAD], 0.0)
                    dve.memset(KEY[s][:, :], 0.0)
                dve.memset(ones[:, :], 1.0)
                dve.memset(nhalf[:, :], -0.5).then_inc(setup_dve, 1)
                dve.memset(ones64[:, :], 1.0)
                dve.wait_ge(in_sem["a"], 16)
                rates = BIG1[1][:, 0, :].rearrange("p (b n) -> p n b", b=NB0)
                ends = BIG1[1][:, 1, 0:2 * N0]
                dve.tensor_reduce(ends[:, 0:N0], rates, AX.X, ALU.max)
                dve.tensor_reduce(ends[:, N0:2 * N0], rates, AX.X, ALU.min)
                dve.drain().then_inc(known, 1)
                dve.wait_ge(setup_pe, 1)
                dve.tensor_reduce(sc[0:N0, 10:11], bank(0, 0)[0:N0, 0:P], AX.X, ALU.max)
                dve.tensor_reduce(sc[0:N0, 11:12], bank(0, 1)[0:N0, 0:P], AX.X, ALU.min)
                dve.drain()
                dve.tensor_tensor(sc[0:N0, 12:13], sc[0:N0, 10:11], sc[0:N0, 11:12], ALU.is_equal)
                dve.wait_ge(setup_act, 4)
                dve.tensor_scalar(sc[0:N0, 13:14], sc[0:N0, 0:1], STEEPEST, None, ALU.is_le)
                dve.drain()
                dve.tensor_tensor(sc[0:N0, 14:15], sc[0:N0, 12:13], sc[0:N0, 13:14], ALU.mult)
                dve.drain().then_inc(known, 1)
                dve.wait_ge(setup_pe, 2)
                dve.tensor_reduce(sc[0:1, 15:16], bank(0, 2)[0:1, 0:N0], AX.X, ALU.min)
                dve.drain()
                dve.tensor_copy(flag[:, :], sc[0:1, 15:16])
                dve.drain().then_inc(known, 1)
                dve.wait_ge(in_sem["p"], 16)
                dve.wait_ge(setup_act, 4)
                dve.tensor_scalar(sc[0:N0, 16:17], sc[0:N0, 0:1], STEEPEST, None, ALU.min)
                dve.tensor_scalar(sc[0:N0, 1:2], sc[0:N0, 0:1], STEEPEST, -1.0, ALU.min, ALU.mult)\
                    .then_inc(setup_dve, 1)
                dve.tensor_scalar(omu[:, 0:2], pr("mu_r", 0, 2), -1.0, 1.0, ALU.mult, ALU.add)
                dve.tensor_scalar(nega[:, :], nega[:, :], -1.0, None, ALU.mult).then_inc(setup_dve, 1)
                for i in (2, 3):
                    dve.wait_ge(wsem[i], 16)
                for k in range(4):
                    dve.tensor_tensor(w("t_w3", k * P, P), w("t_w3", k * P, P), pr("w3_s", 0, P), ALU.mult)
                for j in range(2):
                    dve.tensor_scalar(w("s_out", j * P, P), w("s_out", j * P, P), pr("normw", j), None, ALU.mult)
                dve.wait_ge(setup_act, 5)
                dve.tensor_scalar(sc[:, 6:8], sc[:, 4:6], EPS6, None, ALU.add).then_inc(setup_dve, 1)
                dve.wait_ge(setup_dve, 4)
                dve.tensor_tensor(sc[:, 8:9], sc[:, 6:7], sc[:, 7:8], ALU.mult).then_inc(setup_dve, 1)
                dve.wait_ge(setup_dve, 5)
                dve.tensor_scalar(sc[:, 9:10], sc[:, 8:9], 8.0 ** 0.5, None, ALU.mult).then_inc(setup_dve, 1)
                dve.wait_ge(setup_dve, 6)
                dve.wait_ge(in_sem["c"], 32)
                dve.tensor_scalar(rden[:, :], cn("pos"), sc[:, 9:10], EPS6, ALU.mult, ALU.max).then_inc(setup_dve, 1)
                dve.wait_ge(setup_dve, 7)
                dve.tensor_copy(SM[:, :], cn("pick", 96))
                dve.reciprocal(rden[:, :], rden[:, :]).then_inc(setup_dve, 1)
                dve.wait_ge(setup_dve, 8)
                dve.drain().then_inc(ready, 1)
                dve.wait_ge(ready, 2)

            def norm(i, layer, src, dst, eps=LN_EPS):
                for s in STREAMS:
                    if i == 0:
                        dve.wait_ge(x_in[s].sem, 16)
                    elif layer is not None:
                        dve.wait_ge(x_done.sem, x_done.at((layer - 1) * NS + s))
                    else:
                        dve.wait_ge(ln_norm.sem, ln_norm.at((i - 1) * NS + s))
                    for c in range(NC):
                        last = dve.bn_stats(stat[s][:, c, 0, :], src[s][:, c, :])
                    step(last)
                    for c in range(NC):
                        last = dve.bn_aggr(mv[s][:, c, :], stat[s][:, c, 0, :])
                    step(last)
                    dve.tensor_scalar(ve[s][:, :], mv[s][:, :, 1], eps, None, ALU.add).then_inc(ln_var.sem, 1)
                for s in STREAMS:
                    dve.wait_ge(ln_rstd.sem, ln_rstd.at(i * NS + s))
                    for c in range(NC):
                        last = dve.tensor_scalar(dst[s][:, c, :], src[s][:, c, :], mv[s][:, c, 0:1],
                                                 rstd[s][:, c:c + 1], ALU.subtract, ALU.mult)
                    last.then_inc(ln_norm.sem, 1)

            def conv(s, j, wcol, bcol):
                u, v = UP[s], CV[s]
                step(dve.tensor_scalar(v[:, j, :], u[:, j, PAD:PAD + T], pr(*wcol(3)), pr(*bcol), ALU.mult, ALU.add))
                step(dve.scalar_tensor_tensor(v[:, j, :], u[:, j, 2:2 + T], pr(*wcol(2)), v[:, j, :], ALU.mult, ALU.add))
                step(dve.scalar_tensor_tensor(v[:, j, :], u[:, j, 1:1 + T], pr(*wcol(1)), v[:, j, :], ALU.mult, ALU.add))
                return dve.scalar_tensor_tensor(v[:, j, :], u[:, j, 0:T], pr(*wcol(0)), v[:, j, :], ALU.mult, ALU.add)

            def masked_scores(s, ready_, done):
                for k in range(4):
                    n = T - k * P
                    dve.wait_ge(ready_.sem, ready_.at(s, k))
                    dve.tensor_tensor(MT[s][:, OFF_MT[k]:OFF_MT[k] + n], bank(s, k)[:, k * P:T], cn("tri")[:, 0:n],
                                      ALU.mult).then_inc(done.sem, 1)

            def add_x(s, src, done=None):
                ins = dve.tensor_tensor(X[s][:, :, :], X[s][:, :, :], src, ALU.add)
                if done is None:
                    step(ins)
                else:
                    ins.then_inc(done.sem, 1)

            def state_space():
                for s in STREAMS:
                    dve.wait_ge(l0_bc.sem, l0_bc.at(s, 1))
                    dve.tensor_tensor(Q128[s][:, :], bank(s, 1)[0:N0, :], eq128[:, :], ALU.mult).then_inc(l0_q.sem, 1)
                    dve.tensor_tensor(Q64[s][:, :], bank(s, 1)[0:N0, :], eq64[:, :], ALU.mult).then_inc(l0_q.sem, 1)
                steps = own[0]
                with dve.If(alike == 1):
                    scan_alike()
                with dve.Else():
                    scan_general(own[0] - steps)
                for s in STREAMS:
                    dve.wait_ge(l0_yg.sem, l0_yg.at(NS + s))
                    for c in range(NC):
                        for h in HALVES:
                            last = dve.bn_stats(stat[s][:, c, h, :], BIG1[s][:, 2 * c + h, :])
                    step(last)
                    for c in range(NC):
                        last = dve.bn_aggr(mv[s][:, c, :], stat[s][:, c, :, :].rearrange("p h k -> p (h k)"))
                    step(last)
                    dve.tensor_scalar(ve[s][:, :], mv[s][:, :, 1], LN_EPS, None, ALU.add).then_inc(l0_var.sem, 1)
                for s in STREAMS:
                    dve.wait_ge(l0_rs.sem, l0_rs.at(s))
                    for c in range(NC):
                        y = BIG1[s][:, 2 * c:2 * c + 2, :]
                        dve.tensor_scalar(y, y, mv[s][:, c, 0:1], rstd[s][:, c:c + 1], ALU.subtract, ALU.mult)\
                            .then_inc(l0_nm.sem, 1)
                for h in HALVES:
                    for s in STREAMS:
                        dve.wait_ge(l0_o.sem, l0_o.at(h * NS + s))
                        add_x(s, bank4(s, 2 + h), x_done if h else None)

            def scan_general(skipped):
                decay = KEY[1]
                dve.wait_ge(g_a.sem, 1)
                for s in STREAMS:
                    dve.wait_ge(g_cs.sem, g_cs.at(s))
                    rows, y, h = KEY[0], CV[s][:, 1, :], BIG2[s]
                    for j in range(NB0):
                        g = s * NB0 + j
                        dve.wait_ge(g_up.sem, g_up.at(g))
                        for t in (3, 2, 1, 0):
                            if t == 3:
                                dve.tensor_scalar(CV[s][:, 0, :], UP[s][:, 0, PAD:PAD + T], pr("conv0_w", 4 * j + 3),
                                                  pr("conv0_b", j), ALU.mult, ALU.add)
                            else:
                                dve.scalar_tensor_tensor(CV[s][:, 0, :], UP[s][:, 0, t:t + T], pr("conv0_w", 4 * j + t),
                                                         CV[s][:, 0, :], ALU.mult, ALU.add)
                            dve.drain()
                        dve.memset(y, 0.0)
                        dve.drain().then_inc(g_cv.sem, 1)
                        dve.wait_ge(g_sl.sem, g_sl.at(g))
                        with dve.Fori(0, N0) as n:
                            dve.tensor_scalar(rows[0:N0, 0:T], BT[s][:, :], ident[0:N0, bass.ds(n, 1)], None, ALU.mult)
                            dve.tensor_scalar(rows[0:N0, T:2 * T], Q64[s][:, :], ident[0:N0, bass.ds(n, 1)], None, ALU.mult)
                            dve.drain().then_inc(g_row.sem, 1)
                            dve.wait_ge(g_ps.sem, n + (g * N0 + 1))
                            dve.tensor_tensor(h[:, 0, :], CV[s][:, 0, :], bank(s, 1), ALU.mult)
                            dve.drain()
                            dve.tensor_tensor_scan(h[:, 1, :], decay[:, bass.ds(n + j * N0, 1)].broadcast_to([P, T]),
                                                   h[:, 0, :], 0.0, ALU.mult, ALU.add)
                            dve.drain()
                            dve.tensor_tensor(h[:, 2, :], h[:, 1, :], bank(s, 2), ALU.mult)
                            dve.drain()
                            dve.tensor_tensor(y, y, h[:, 2, :], ALU.add)
                            dve.drain()
                        dve.sem_inc(g_sum.sem, 1)
                        dve.wait_ge(g_t.sem, g_t.at(g))
                        for c in range(NC):
                            z = BIG1[s][:, 2 * c + j // 4, (j % 4) * P:(j % 4 + 1) * P]
                            dve.tensor_tensor(z, bank4(s, 3)[:, c, :], z, ALU.mult)
                        dve.drain().then_inc(g_yg.sem, 1)
                dve.memset(KEY[0][:, :], 0.0)
                dve.memset(KEY[1][:, :], 0.0)
                dve.drain().then_inc(l0_yg.sem, NS * 2 * NC)
                dve.sem_inc(dve_own.sem, skipped)

            def scan_alike():
                for s in STREAMS:
                    masked_scores(s, l0_sc, l0_mt)
                for h in HALVES:
                    for s in STREAMS:
                        g = h * NS + s
                        for k in range(4):
                            j = 4 * h + k
                            dve.wait_ge(l0_up.sem, l0_up.at(g, k))
                            if k >= 2:
                                dve.wait_ge(l0_xt.sem, l0_xt.at(g, k - 2))
                            elif g >= NS:
                                dve.wait_ge(l0_xt.sem, l0_xt.at(g - NS, k + 2))
                            conv(s, k % 2, lambda t: ("conv0_w", 4 * j + t), ("conv0_b", j)).then_inc(l0_cv.sem, 1)
                    for s in STREAMS:
                        for c in range(NC):
                            dve.wait_ge(l0_y.sem, l0_y.at(h * NS + s, c))
                            dve.wait_ge(l0_zs.sem, l0_zs.at(s, 2 * c + h))
                            z = BIG1[s][:, 2 * c + h, :]
                            dve.tensor_tensor(z, bank(s, c), z, ALU.mult).then_inc(l0_yg.sem, 1)

            def feed_forward():
                for s in STREAMS:
                    dve.wait_ge(ln_xT.sem, ln_xT.at(turn_index(LNI[L0F]) * NS + s))
                    now, prev, b = XT[s][:, PAD:PAD + T], XT[s][:, PAD - 1:PAD - 1 + T], BIG1[s]
                    dve.tensor_scalar(b[:, 3, :], prev, omu[:, 1:2], None, ALU.mult)
                    step(dve.tensor_scalar(b[:, 2, :], prev, omu[:, 0:1], None, ALU.mult))
                    dve.scalar_tensor_tensor(b[:, 1, :], now, pr("mu_k"), b[:, 3, :], ALU.mult, ALU.add)\
                        .then_inc(f0_mix.sem, 1)
                    dve.scalar_tensor_tensor(b[:, 0, :], now, pr("mu_r"), b[:, 2, :], ALU.mult, ALU.add)\
                        .then_inc(f0_mix.sem, 1)
                for s in STREAMS:
                    dve.wait_ge(f0_rl.sem, f0_rl.at(s))
                    dve.tensor_tensor(BIG1[s][:, 5, :], BIG1[s][:, 4, :], BIG1[s][:, 4, :], ALU.mult)\
                        .then_inc(f0_ka.sem, 1)
                for s in STREAMS:
                    dve.wait_ge(f0_p.sem, f0_p.at(s, 2))
                    dve.wait_ge(f0_sg.sem, f0_sg.at(s))
                    step(dve.tensor_tensor(BIG1[s][:, 7, :], bank(s, 2), BIG1[s][:, 6, :], ALU.mult))
                    add_x(s, BIG1[s][:, 7, :].rearrange("p (c n) -> p c n", c=NC), x_done)

            def mamba():
                for s in STREAMS:
                    for j in range(2):
                        dve.wait_ge(m_up.sem, m_up.at(s, j))
                        conv(s, j, lambda t: ("conv1_w", 4 * j + t), ("conv1_b", j)).then_inc(m_cv.sem, 1)
                for s in STREAMS:
                    dve.wait_ge(m_xd.sem, m_xd.at(s, 1))
                    bc, r = bank(s, 1), BIG2[s][:, 0, :]
                    step(dve.tensor_copy(SPL[s][:, :], bc[0:96, :]))
                    step(dve.tensor_tensor(r[0:96], bc[0:96, :], SPL[s][:, :], ALU.subtract))
                    dve.tensor_copy(SPL[s][32:64, :], r[32:64])
                    step(dve.tensor_copy(SPL[s][64:96, :], r[64:96]))
                    step(dve.tensor_tensor(r[64:96], r[64:96], SPL[s][64:96, :], ALU.subtract))
                    dve.tensor_copy(SPL[s][64:96, :], r[64:96]).then_inc(m_sp3.sem, 1)
                for s in STREAMS:
                    for j in range(2):
                        dve.wait_ge(m_sp.sem, m_sp.at(s, j))
                        step(dve.tensor_tensor(BIG1[s][:, j, :], CV[s][:, j, :], UP[s][:, j, PAD:PAD + T], ALU.add))
                        dve.tensor_tensor(BIG1[s][:, 2 + j, :], BIG1[s][:, j, :], BIG1[s][:, 4 + j, :], ALU.mult)\
                            .then_inc(m_du.sem, 1)
                for q in range(NM * NS):
                    s = q % NS
                    dve.wait_ge(m_bs.sem, m_bs.at(q))
                    dve.tensor_tensor(BIG2[s][:, 0, :], bank(s, 2), BIG1[s][:, 2, :], ALU.mult).then_inc(m_d0.sem, 1)
                    dve.wait_ge(m_d0.sem, m_d0.at(q))
                    for j in range(2):
                        dve.wait_ge(m_da.sem, m_da.at(q, j))
                        if j:
                            dve.wait_ge(m_d1.sem, m_d1.at(q))
                        dve.tensor_tensor_scan(UP[s][:, j, PAD:PAD + T], CV[s][:, j, :], BIG2[s][:, j, :], 0.0,
                                               ALU.mult, ALU.add).then_inc(m_sc.sem, 1)
                    dve.wait_ge(m_sc.sem, m_sc.at(q, 1))
                    dve.wait_ge(m_bc.sem, m_bc.at(q, 1))
                    if q >= NS:
                        dve.wait_ge(m_ya.sem, m_ya.at(q - NS))
                    dve.tensor_tensor(BIG2[s][:, 2:4, :], UP[s][:, :, PAD:PAD + T],
                                      bank(s, 3).unsqueeze(1).broadcast_to([P, 2, T]), ALU.mult)\
                        .then_inc(m_hc.sem, 1)
                for s in STREAMS:
                    dve.wait_ge(m_ya.sem, m_ya.at((NM - 1) * NS + s))
                    for j in range(2):
                        step(dve.scalar_tensor_tensor(BIG2[s][:, j, :], BIG1[s][:, 4 + j, :], pr("dm", j), bank(s, j),
                                                      ALU.mult, ALU.add))
                        dve.tensor_tensor(BIG2[s][:, j, :], BIG2[s][:, j, :], BIG1[s][:, 6 + j, :], ALU.mult)\
                            .then_inc(m_y.sem, 1)
                    add_x(s, XN[s][:, :, :])
                for s in STREAMS:
                    dve.wait_ge(m_o.sem, m_o.at(s))
                    add_x(s, bank4(s, 2), x_done)

            def route(m, renorm):
                for s in STREAMS:
                    g = m * NS + s
                    dve.wait_ge(r_lg.sem, r_lg.at(g))
                    lgp = bank(s, 3)[:, 0:NC * NE].rearrange("p (c e) -> p c e", c=NC)
                    step(dve.tensor_reduce(sm4[s][:, 0, :], lgp, AX.X, ALU.max))
                    dve.tensor_tensor(lg[s][:, 0], lgp, sm4[s][:, 0, :].unsqueeze(2).broadcast_to([P, NC, NE]),
                                      ALU.subtract).then_inc(r_sh.sem, 1)
                for s in STREAMS:
                    g = m * NS + s
                    dve.wait_ge(r_ex.sem, r_ex.at(g))
                    step(dve.tensor_reduce(sm4[s][:, 1, :], lg[s][:, 1], AX.X, ALU.add))
                    step(dve.reciprocal(sm4[s][:, 2, :], sm4[s][:, 1, :]))
                    step(dve.tensor_tensor(lg[s][:, 2], lg[s][:, 1],
                                           sm4[s][:, 2, :].unsqueeze(2).broadcast_to([P, NC, NE]), ALU.mult))
                    for c in range(NC):
                        last = dve.max(top[s][:, c, :], lg[s][:, 2, c, :])
                    step(last)
                    for c in range(NC):
                        last = dve.max_index(topi[s][:, c, :], top[s][:, c, :], lg[s][:, 2, c, :])
                    step(last)
                    if renorm:
                        step(dve.tensor_tensor(sm4[s][:, 0, :], top[s][:, :, 0], top[s][:, :, 1], ALU.add))
                        step(dve.reciprocal(sm4[s][:, 3, :], sm4[s][:, 0, :]))
                        step(dve.tensor_tensor(top[s][:, :, 0:2], top[s][:, :, 0:2],
                                               sm4[s][:, 3, :].unsqueeze(2).broadcast_to([P, NC, 2]), ALU.mult))
                    step(dve.tensor_copy(topf[s][:, :, :], topi[s][:, :, :]))
                    for c in range(NC):
                        for r in range(2):
                            last = dve.tensor_scalar(lg[s][:, r, c, :], cn("iota8"), topf[s][:, c, r:r + 1],
                                                     top[s][:, c, r:r + 1], ALU.is_equal, ALU.mult)
                    step(last)
                    dve.tensor_tensor(cmb[s][:, :, :], lg[s][:, 0], lg[s][:, 1], ALU.add).then_inc(r_cb.sem, 1)
                for s in STREAMS:
                    dve.wait_ge(r_b.sem, r_b.at(m * NS + s))
                    add_x(s, bank4(s, 3), r_bx)

            def gated_sum(m, q):
                e, s = q // NS, q % NS
                dve.wait_ge(e_dn.sem, e_dn.at(m * NE * NS + q))
                for c in range(NC):
                    last = dve.scalar_tensor_tensor(X[s][:, c, :], bank4(s, 3)[:, c, :], cmb[s][:, c, e:e + 1],
                                                    X[s][:, c, :], ALU.mult, ALU.add)
                last.then_inc((e_x if e < NE - 1 else x_done).sem, 1)

            def experts_gelu():
                for s in STREAMS:
                    dve.wait_ge(r_bx.sem, r_bx.at(s))
                for q in range(NE * NS):
                    gated_sum(0, q)
                    if q % NS == NS - 1 and q < NE * NS - 1:
                        dve.wait_ge(e_x.sem, e_x.at(q))

            def experts_silu():
                def products(q):
                    e, s = q // NS, q % NS
                    for k in range(4):
                        dve.wait_ge(e_up.sem, 64 + 8 * q + 2 * k + 2)
                        dve.wait_ge(e_act.sem, 64 + 4 * q + k + 1)
                        if k == 0 and q >= 2 * NS:
                            dve.wait_ge(e_dn.sem, e_dn.at(NE * NS + q - 2 * NS))
                        dve.scalar_tensor_tensor(BIG1[s][:, 4 * (e % 2) + k, :], bank(s, (2 * k + 1) % 4),
                                                 pr("bu", 4 * e + k), CV[s][:, k % 2, :], ALU.add, ALU.mult)\
                            .then_inc(e_h.sem, 1)

                for s in STREAMS:
                    dve.wait_ge(r_bx.sem, r_bx.at(NS + s))
                for q in range(NE * NS + 1):
                    if q < NE * NS:
                        products(q)
                    if q:
                        if q > NS:
                            dve.wait_ge(e_x.sem, e_x.at((NE - 1) * NS + q - 1 - NS))
                        gated_sum(1, q - 1)

            def attention():
                for s in STREAMS:
                    for k, op in enumerate(("q", "k", "v")):
                        dve.wait_ge(a_p.sem, a_p.at(s, k))
                        if op == "v":
                            dve.tensor_copy(BIG1[s][:, k, :], bank(s, k)).then_inc(a_f.sem, 1)
                        else:
                            dve.tensor_scalar(BIG1[s][:, k, :], bank(s, k), 0.0, EPS6, ALU.max, ALU.add)\
                                .then_inc(a_f.sem, 1)
                for b in range(NB0):
                    for s in STREAMS:
                        g = b * NS + s
                        dve.wait_ge(a_ks.sem, a_ks.at(g))
                        dve.wait_ge(a_r.sem, a_r.at(g, 1))
                        dve.tensor_tensor(CV[s][:, 1, :], bank(s, 1), CV[s][:, 0, :], ALU.mult).then_inc(a_kv.sem, 1)
                        dve.wait_ge(a_kv.sem, a_kv.at(g))
                        dve.tensor_tensor_scan(UP[s][:, 0, PAD:PAD + T], ones[:, 0:1].broadcast_to([P, T]), CV[s][:, 1, :], 0.0,
                                               ALU.mult, ALU.add).then_inc(a_cum.sem, 1)
                        dve.wait_ge(a_cum.sem, a_cum.at(g))
                        dve.wait_ge(a_r.sem, a_r.at(g, 2))
                        if b:
                            dve.wait_ge(a_red.sem, a_red.at(g - NS))
                        dve.tensor_tensor(UP[s][:, 1, PAD:PAD + T], bank(s, 2), UP[s][:, 0, PAD:PAD + T], ALU.mult)\
                            .then_inc(a_qk.sem, 1)
                for s in STREAMS:
                    dve.wait_ge(a_red.sem, a_red.at((NB0 - 1) * NS + s))
                    dve.tensor_tensor(BIG2[s][:, 0, :], bank(s, 3), rden[:, :], ALU.mult).then_inc(a_o.sem, 1)
                for s in STREAMS:
                    dve.wait_ge(a_y.sem, a_y.at(s))
                    add_x(s, bank4(s, 0), x_done)

            def ternary():
                for s in STREAMS:
                    for j in range(4):
                        dve.wait_ge(t_ab.sem, t_ab.at(4 * s + j, 1))
                        dve.wait_ge(t_sa.sem, t_sa.at(4 * s + j))
                        dve.scalar_tensor_tensor(BIG1[s][:, j, :], bank(s, 2 + j % 2), pr("w2_s", j), CV[s][:, j % 2, :],
                                                 ALU.mult, ALU.mult).then_inc(t_h0.sem, 1)
                for s in STREAMS:
                    dve.wait_ge(t_o.sem, t_o.at(s))
                    add_x(s, bank4(s, 0), x_done)

            def last_scan():
                for s in STREAMS:
                    for j in range(2):
                        dve.wait_ge(s_sl.sem, s_sl.at(s, j))
                        dve.wait_ge(s_sg.sem, s_sg.at(s, j))
                        dve.tensor_tensor(BIG1[s][:, j, :], CV[s][:, j, :], UP[s][:, j, PAD:PAD + T], ALU.mult)\
                            .then_inc(s_xi.sem, 1)
                for s in STREAMS:
                    dve.wait_ge(s_abc.sem, s_abc.at(s, 0))
                    dve.tensor_scalar(BT[s][0:N3, :], bank(s, 0)[0:N3, :], -5.0, 0.0, ALU.max, ALU.min)\
                        .then_inc(s_cl.sem, 1)
                for s in STREAMS:
                    dve.wait_ge(s_ea.sem, s_ea.at(s))
                    cum = BT[s][0:N3, :]
                    step(dve.tensor_tensor_scan(Q128[s][0:N3, :], ones[0:N3, 0:1].broadcast_to([N3, T]), cum, 0.0, ALU.mult, ALU.add))
                    dve.tensor_copy(cum, Q128[s][0:N3, :])
                    dve.tensor_scalar(negr[s][:, :], Q128[s][0:N3, 0:T:64], -1.0, None, ALU.mult).then_inc(s_cum.sem, 1)
                for s in STREAMS:
                    dve.wait_ge(s_ex.sem, s_ex.at(s))
                    dve.wait_ge(s_abc.sem, s_abc.at(s, 2))
                    q4 = Q64[s][0:N3, :].rearrange("p (c n) -> p c n", c=NC)[:, :, 64:P]
                    c4 = bank4(s, 2)[0:N3, :, 64:P]
                    dve.tensor_tensor(Q128[s][0:N3, :], bank(s, 2)[0:N3, :], Q128[s][0:N3, :], ALU.mult)
                    dve.tensor_tensor(q4, c4, q4, ALU.mult)
                    for c in range(1, NC):
                        r = KEY[s][0:N3, OFF_RECT[c]:OFF_RECT[c] + c * P]
                        dve.tensor_tensor(r, bank(s, 1)[0:N3, 0:c * P], r, ALU.mult)
                    k0 = KEY[s][0:N3, OFF_D0:OFF_D0 + T].rearrange("p (c n) -> p c n", c=NC)[:, :, 0:64]
                    k1 = KEY[s][0:N3, OFF_D1:OFF_D1 + T]
                    dve.tensor_tensor(k0, bank4(s, 1)[0:N3, :, 0:64], k0, ALU.mult)
                    dve.tensor_tensor(k1, bank(s, 1)[0:N3, :], k1, ALU.mult).then_inc(s_f.sem, 1)
                for s in STREAMS:
                    masked_scores(s, s_sc, s_mt)
                for s in STREAMS:
                    dve.wait_ge(s_o.sem, s_o.at(s, 0))
                    dve.tensor_scalar(ve[s][:, :], bank(s, 3)[:, 0:NC], 1.0 / 256, RMS_EPS, ALU.mult, ALU.add)\
                        .then_inc(s_var.sem, 1)
                for s in STREAMS:
                    dve.wait_ge(s_rs.sem, s_rs.at(s))
                    dve.wait_ge(s_o.sem, s_o.at(s, 1))
                    for c in range(NC):
                        last = dve.scalar_tensor_tensor(X[s][:, c, :], bank4(s, 2)[:, c, :], rstd[s][:, c:c + 1],
                                                        X[s][:, c, :], ALU.mult, ALU.add)
                    last.then_inc(x_done.sem, 1)

            setup()
            alike = dve.value_load(flag[0:1, 0:1], min_val=0, max_val=1)
            with dve.Fori(0, 4 // NS):
                own[0] = 0
                if on[L0]:
                    norm(LNI[L0], L0, X, XH)
                    state_space()
                if on[L0F]:
                    norm(LNI[L0F], L0F, X, XH)
                    feed_forward()
                if on[L1]:
                    norm(LNI["outer"], L1, X, XN)
                    norm(LNI[L1], None, XN, XH)
                    mamba()
                if on[L1F]:
                    norm(LNI[L1F], L1F, X, XH)
                    route(0, False)
                    experts_gelu()
                if on[L2]:
                    norm(LNI[L2], L2, X, XH)
                    attention()
                if on[L2F]:
                    norm(LNI[L2F], L2F, X, XH)
                    ternary()
                if on[L3]:
                    norm(LNI[L3], L3, X, XH)
                    last_scan()
                if on[L3F]:
                    norm(LNI[L3F], L3F, X, XH)
                    route(1, True)
                    experts_silu()
                end_of_pair(dve, "dve")

        @block.tensor
        def _(pe):
            def turn(i):
                for s in STREAMS:
                    pe.wait_ge(ln_norm.sem, ln_norm.at(i * NS + s))
                    for c in range(NC):
                        last = pe.transpose(bank(s, 3)[:, c * P:(c + 1) * P], XH[s][:, c, :], ident)
                    last.then_inc(ln_T.sem, 1)

            def normed(i, s):
                pe.wait_ge(ln_xT.sem, ln_xT.at(turn_index(i) * NS + s))

            def by_token(s, k, lhs, rhs, blocks):
                for c in range(NC):
                    for b in range(blocks):
                        last = pe.matmul(bank4(s, k)[:, c, :], lhs(b, c), rhs(b), start=(b == 0), stop=(b == blocks - 1))
                return last

            def scores(s, n, done):
                for k in range(NC):
                    b = bank(s, k)
                    a = k * P
                    pe.matmul(b[:, a:a + 64], KEY[s][0:n, OFF_D0 + a:OFF_D0 + a + P], Q128[s][0:n, a:a + 64],
                              start=True, stop=True)
                    last = pe.matmul(b[:, a + 64:a + P], KEY[s][0:n, OFF_D1 + a:OFF_D1 + a + P],
                                     Q64[s][0:n, a + 64:a + P], start=True, stop=True)
                    for c in range(k + 1, NC):
                        last = pe.matmul(b[:, c * P:(c + 1) * P], KEY[s][0:n, OFF_RECT[c] + a:OFF_RECT[c] + a + P],
                                         Q128[s][0:n, c * P:(c + 1) * P], start=True, stop=True)
                    last.then_inc(done.sem, 1)

            def state_space():
                win = lambda j: w("l0_in", j * P, P)
                for s in STREAMS:
                    normed(LNI[L0], s)
                    for k in range(2):
                        pe.matmul(bank(s, k)[0:N0, :], w("l0_in", 16 * P + k * N0, N0), XT[s][:, PAD:PAD + T],
                                  start=True, stop=True).then_inc(l0_bc.sem, 1)
                for s in STREAMS:
                    for k in range(8):
                        c, h = k // 2, k % 2
                        if k == 0:
                            pe.wait_ge(l0_bt.sem, l0_bt.at(s))
                        elif k == 1:
                            pe.wait_ge(l0_q.sem, l0_q.at(s))
                        elif k >= 4:
                            pe.wait_ge(l0_zs.sem, l0_zs.at(s, k - 4))
                        pe.matmul(bank(s, k % 4), chunk(s, c), w("l0_in", DI + h * T, T), start=True, stop=True)\
                            .then_inc(l0_z.sem, 1)
                with pe.If(alike == 1):
                    products_alike(win)
                with pe.Else():
                    products_general(win)
                for h in HALVES:
                    for s in STREAMS:
                        g = h * NS + s
                        for j in range(4):
                            if j >= 2:
                                pe.wait_ge(l0_yn.sem, l0_yn.at(g, j - 2))
                            for c in range(NC):
                                if h == 0 and j == 0:
                                    pe.wait_ge(l0_nm.sem, l0_nm.at(s, c))
                                last = pe.transpose(bank4(s, j % 2)[:, c, :], BIG1[s][:, 2 * c + h, j * P:(j + 1) * P],
                                                    ident)
                            last.then_inc(l0_yt.sem, 1)
                        pe.wait_ge(l0_yn.sem, l0_yn.at(g))
                        by_token(s, 2 + h, lambda b, c: BIG2[s][:, b, c * P:(c + 1) * P],
                                 lambda b: w("l0_out", (4 * h + b) * P, P), 4).then_inc(l0_o.sem, 1)

            def products_general(win):
                for s in STREAMS:
                    pe.wait_ge(l0_zs.sem, l0_zs.at(s, 7))
                    pe.matmul(bank(s, 1)[0:N0, :], w("l0_in", 16 * P + N0, N0), XT[s][:, PAD:PAD + T],
                              start=True, stop=True).then_inc(g_c.sem, 1)
                    for j in range(NB0):
                        g = s * NB0 + j
                        pe.matmul(bank(s, 0), win(j), XT[s][:, PAD:PAD + T], start=True, stop=True).then_inc(g_u.sem, 1)
                        with pe.Fori(0, N0) as n:
                            pe.wait_ge(g_row.sem, n + (g * N0 + 1))
                            for k in range(2):
                                last = pe.matmul(bank(s, 1 + k), ones64[:, :], KEY[0][0:N0, k * T:(k + 1) * T],
                                                 start=True, stop=True)
                            last.then_inc(g_ps.sem, 1)
                        pe.wait_ge(g_sum.sem, g_sum.at(g))
                        if g:
                            pe.wait_ge(g_yg.sem, g_yg.at(g - 1))
                        for c in range(NC):
                            last = pe.transpose(bank4(s, 3)[:, c, :], CV[s][:, 1, c * P:(c + 1) * P], ident)
                        last.then_inc(g_t.sem, 1)

            def products_alike(win):
                for s in STREAMS:
                    pe.wait_ge(l0_q.sem, l0_q.at(s))
                    pe.wait_ge(key_f.sem, key_f.at(s))
                    pe.wait_ge(l0_zs.sem, l0_zs.at(s, 7))
                    scores(s, N0, l0_sc)
                for h in HALVES:
                    for s in STREAMS:
                        g = h * NS + s
                        for k in range(4 + 2):
                            if k < 4:
                                if k >= 2:
                                    pe.wait_ge(l0_up.sem, l0_up.at(g, k - 2))
                                elif h == 0:
                                    pe.wait_ge(l0_mt.sem, l0_mt.at(s, k))
                                else:
                                    pe.wait_ge(l0_yg.sem, l0_yg.at(s))
                                pe.matmul(bank(s, k % 2), win(4 * h + k), XT[s][:, PAD:PAD + T], start=True, stop=True)\
                                    .then_inc(l0_u.sem, 1)
                            if k >= 2:
                                j = k - 2
                                pe.wait_ge(l0_sl.sem, l0_sl.at(g, j))
                                if h == 0 and j < 2:
                                    pe.wait_ge(l0_mt.sem, l0_mt.at(s, 2 + j))
                                if j >= 2:
                                    pe.wait_ge(l0_xc.sem, l0_xc.at(g, j - 2))
                                for c in range(NC):
                                    last = pe.transpose(bank4(s, 2 + j % 2)[:, c, :], CV[s][:, j % 2, c * P:(c + 1) * P],
                                                        ident)
                                last.then_inc(l0_xt.sem, 1)
                    for s in STREAMS:
                        g = h * NS + s
                        pe.wait_ge(l0_xc.sem, l0_xc.at(g))
                        for c in range(NC):
                            for k in range(c + 1):
                                m = OFF_MT[k] + (c - k) * P
                                last = pe.matmul(bank(s, c), MT[s][:, m:m + P], BIG2[s][:, k, :],
                                                 start=(k == 0), stop=(k == c))
                            last.then_inc(l0_y.sem, 1)

            def feed_forward():
                for s in STREAMS:
                    pe.wait_ge(f0_mix.sem, f0_mix.at(s, 0))
                    pe.matmul(bank(s, 0), w("f0_k"), BIG1[s][:, 1, :], start=True, stop=True).then_inc(f0_p.sem, 1)
                    pe.wait_ge(f0_mix.sem, f0_mix.at(s, 1))
                    by_token(s, 1, lambda b, c: BIG1[s][:, 0, c * P:(c + 1) * P], lambda b: w("f0_r"), 1)\
                        .then_inc(f0_p.sem, 1)
                    pe.wait_ge(f0_ka.sem, f0_ka.at(s))
                    by_token(s, 2, lambda b, c: BIG1[s][:, 5, c * P:(c + 1) * P], lambda b: w("f0_v"), 1)\
                        .then_inc(f0_p.sem, 1)

            def mamba():
                for s in STREAMS:
                    normed(LNI[L1], s)
                    for j in range(4):
                        pe.matmul(bank(s, j), w("m_in", j * P, P), XT[s][:, PAD:PAD + T], start=True, stop=True)\
                            .then_inc(m_uz.sem, 1)
                for s in STREAMS:
                    for k, (m, name) in enumerate(((8, "m_dt"), (96, "m_bc"))):
                        for j in range(2):
                            pe.wait_ge(m_u.sem, m_u.at(s, j))
                            last = pe.matmul(bank(s, k)[0:m, :], w(name, j * m, m), BIG1[s][:, 4 + j, :],
                                             start=(j == 0), stop=(j == 1))
                        last.then_inc(m_xd.sem, 1)
                for s in STREAMS:
                    pe.wait_ge(m_d8.sem, m_d8.at(s))
                    for j in range(2):
                        pe.wait_ge(m_z.sem, m_z.at(s, j))
                        pe.matmul(bank(s, 2 + j), R8[:, 2 * P + j * P:2 * P + (j + 1) * P], BT[s][0:8, :],
                                  start=True, stop=True).then_inc(m_dt.sem, 1)

                def spread(q):
                    n, s = q // NS, q % NS
                    if q < NS:
                        pe.wait_ge(m_sp3.sem, m_sp3.at(s))
                        pe.wait_ge(m_sp.sem, m_sp.at(s))
                    for k in range(2):
                        if q >= NS:
                            if k == 0:
                                pe.wait_ge(m_d0.sem, m_d0.at(q - NS))
                                pe.wait_ge(m_bs.sem, m_bs.at(q - NS))
                            else:
                                pe.wait_ge(m_hc.sem, m_hc.at(q - NS))
                        r = 16 * k + n
                        pe.matmul(bank(s, 2 + k), SM[:, r:r + 1].broadcast_to([96, P]), SPL[s][:, :], start=True, stop=True)\
                            .then_inc(m_bc.sem, 1)

                def sum_states(q):
                    n, s = q // NS, q % NS
                    pe.wait_ge(m_hc.sem, m_hc.at(q))
                    for j in range(2):
                        last = pe.matmul(bank(s, j), ident, BIG2[s][:, 2 + j, :], start=(n == 0), stop=(n == NM - 1))
                    last.then_inc(m_ya.sem, 1)

                for q in range(NM * NS + 1):
                    if q < NM * NS:
                        spread(q)
                    if q:
                        sum_states(q - 1)
                for s in STREAMS:
                    pe.wait_ge(m_y.sem, m_y.at(s))
                    by_token(s, 2, lambda b, c: BIG2[s][:, b, c * P:(c + 1) * P], lambda b: w("m_out", b * P, P), 2)\
                        .then_inc(m_o.sem, 1)

            def route(m, name, i):
                for s in STREAMS:
                    normed(i, s)
                    for c in range(NC):
                        last = pe.matmul(bank(s, 3)[:, c * NE:(c + 1) * NE], chunk(s, c), w(name), start=True, stop=True)
                    last.then_inc(r_lg.sem, 1)
                for s in STREAMS:
                    g = m * NS + s
                    pe.wait_ge(r_cb.sem, r_cb.at(g))
                    for c in range(NC):
                        last = pe.transpose(bank(s, 3)[0:NE, c * P:(c + 1) * P], cmb[s][:, c, :], ident)
                    last.then_inc(r_ct.sem, 1)
                for s in STREAMS:
                    g = m * NS + s
                    pe.wait_ge(r_cs.sem, r_cs.at(g))
                    by_token(s, 3, lambda b, c: cmbT[s][:, c * P:(c + 1) * P], lambda b: R8[:, m * P:(m + 1) * P], 1)\
                        .then_inc(r_b.sem, 1)

            def loaded(load):
                pe.wait_ge(ring_in[load % RING].sem, 16 * (sum(1 for x in range(load + 1)
                                                                if x % RING == load % RING)))

            def down(m, q):
                e, s = q // NS, q % NS
                slot = (m * NE + e) % RING
                wd = ring[:, slot, 512 * (m + 1):512 * (m + 2)]
                if q < NS:
                    pe.wait_ge(r_bx.sem, r_bx.at(m * NS + s))
                else:
                    pe.wait_ge(e_x.sem, e_x.at(m * (NE - 1) * NS + q - NS))
                if m == 0:
                    pe.wait_ge(e_act.sem, 4 * q + 4)
                else:
                    pe.wait_ge(e_h.sem, 4 * q + 4)
                by_token(s, 3, lambda b, c: BIG1[s][:, 4 * (e % 2) + b, c * P:(c + 1) * P],
                         lambda b: wd[:, b * P:(b + 1) * P], 4).then_inc(e_dn.sem, 1)

            def experts_gelu():
                for q in range(NE * NS + 1):
                    if q < NE * NS:
                        e, s = q // NS, q % NS
                        loaded(e)
                        for k in range(4):
                            if k == 3:
                                pe.wait_ge(e_act.sem, 4 * q + 1)
                            elif q >= NS:
                                pe.wait_ge(e_act.sem, 4 * (q - NS) + (4 if k == 0 else k + 1))
                            pe.matmul(bank(s, k % 3), ring[:, e % RING, k * P:(k + 1) * P], XT[s][:, PAD:PAD + T],
                                      start=True, stop=True).then_inc(e_up.sem, 1)
                    if q:
                        down(0, q - 1)

            def experts_silu():
                for q in range(NE * NS + 1):
                    if q < NE * NS:
                        e, s = q // NS, q % NS
                        slot = (NE + e) % RING
                        loaded(NE + e)
                        for k in range(4):
                            for r in range(2):
                                b = (2 * k + r) % 4
                                if k >= 2:
                                    if r:
                                        pe.wait_ge(e_h.sem, 4 * q + k - 2 + 1)
                                    else:
                                        pe.wait_ge(e_act.sem, 64 + 4 * q + k - 2 + 1)
                                elif q >= NS:
                                    if b == 3:
                                        pe.wait_ge(e_x.sem, e_x.at((NE - 1) * NS + q - NS))
                                    elif r:
                                        pe.wait_ge(e_h.sem, 4 * (q - NS) + k + 2 + 1)
                                    else:
                                        pe.wait_ge(e_act.sem, 64 + 4 * (q - NS) + k + 2 + 1)
                                elif b == 3:
                                    pe.wait_ge(r_bx.sem, r_bx.at(NS + s))
                                pe.matmul(bank(s, b), ring[:, slot, r * T + k * P:r * T + (k + 1) * P],
                                          XT[s][:, PAD:PAD + T], start=True, stop=True).then_inc(e_up.sem, 1)
                    if q:
                        down(1, q - 1)

            def attention():
                sel = lambda k: SEL[:, k * P:(k + 1) * P]
                for s in STREAMS:
                    normed(LNI[L2], s)
                    for k in range(3):
                        pe.matmul(bank(s, k), w("a_qkv", k * P, P), XT[s][:, PAD:PAD + T], start=True, stop=True)\
                            .then_inc(a_p.sem, 1)

                def spread(g):
                    b, s = g // NS, g % NS
                    for k, (src, m, free) in enumerate(((1, b, a_ks), (2, NB0 + b, a_kv), (0, b, a_qk))):
                        if b:
                            pe.wait_ge(free.sem, free.at(g - NS))
                        else:
                            pe.wait_ge(a_f.sem, a_f.at(s))
                        pe.matmul(bank(s, k), sel(m), BIG1[s][:, src, :], start=True, stop=True).then_inc(a_r.sem, 1)

                def reduce(g):
                    b, s = g // NS, g % NS
                    pe.wait_ge(a_qk.sem, a_qk.at(g))
                    pe.matmul(bank(s, 3), sel(2 * NB0 + b), UP[s][:, 1, PAD:PAD + T], start=(b == 0),
                              stop=(b == NB0 - 1)).then_inc(a_red.sem, 1)

                for g in range(NB0 * NS + 1):
                    if g < NB0 * NS:
                        spread(g)
                    if g:
                        reduce(g - 1)
                for s in STREAMS:
                    pe.wait_ge(a_o.sem, a_o.at(s))
                    by_token(s, 0, lambda b, c: BIG2[s][:, 0, c * P:(c + 1) * P], lambda b: w("a_out"), 1)\
                        .then_inc(a_y.sem, 1)

            def ternary():
                for s in STREAMS:
                    normed(LNI[L2F], s)
                    for j in range(4):
                        for r, name in enumerate(("t_w1", "t_w2")):
                            if j >= 2:
                                free = t_h0 if r else t_sa
                                pe.wait_ge(free.sem, free.at(4 * s + j - 2))
                            pe.matmul(bank(s, 2 * r + j % 2), w(name, j * P, P), XT[s][:, PAD:PAD + T],
                                      start=True, stop=True).then_inc(t_ab.sem, 1)
                for name, p, src in (("t_h1", t_p1, 0), ("t_h2", t_p2, 4)):
                    for s in STREAMS:
                        if src == 0:
                            pe.wait_ge(t_h0.sem, t_h0.at(4 * s + 3))
                        for j in range(4):
                            for b in range(4):
                                if src:
                                    pe.wait_ge(t_g1.sem, t_g1.at(s, max(b, j)))
                                last = pe.matmul(bank(s, j), w(name, (4 * b + j) * P, P), BIG1[s][:, src + b, :],
                                                 start=(b == 0), stop=(b == 3))
                            last.then_inc(p.sem, 1)
                for s in STREAMS:
                    pe.wait_ge(t_g2.sem, t_g2.at(s))
                    by_token(s, 0, lambda b, c: BIG1[s][:, b, c * P:(c + 1) * P], lambda b: w("t_w3", b * P, P), 4)\
                        .then_inc(t_o.sem, 1)

            def last_scan():
                for s in STREAMS:
                    normed(LNI[L3], s)
                    for j in range(4):
                        pe.matmul(bank(s, j), w("s_in", j * P, P), XT[s][:, PAD:PAD + T], start=True, stop=True)\
                            .then_inc(s_ab.sem, 1)
                for s in STREAMS:
                    pe.wait_ge(s_xi.sem, s_xi.at(s))
                    for k in range(3):
                        for j in range(2):
                            last = pe.matmul(bank(s, k)[0:N3, :], w("s_abc", j * 48 + k * N3, N3), BIG1[s][:, j, :],
                                             start=(j == 0), stop=(j == 1))
                        last.then_inc(s_abc.sem, 1)
                for s in STREAMS:
                    pe.wait_ge(s_f.sem, s_f.at(s))
                    scores(s, N3, s_sc)
                for s in STREAMS:
                    for j in range(2):
                        pe.wait_ge(s_mt.sem, s_mt.at(s, 2 + j))
                        for c in range(NC):
                            last = pe.transpose(bank4(s, 2 + j)[:, c, :], BIG1[s][:, j, c * P:(c + 1) * P], ident)
                        last.then_inc(s_xt.sem, 1)
                for s in STREAMS:
                    pe.wait_ge(s_xs.sem, s_xs.at(s))
                    for j in range(2):
                        for k in range(NC):
                            last = pe.matmul(bank(s, j)[:, k * P:T], BIG2[s][:, k, j * P:(j + 1) * P],
                                             MT[s][:, OFF_MT[k]:OFF_MT[k] + T - k * P], start=(k == 0), stop=(k == NC - 1))
                        last.then_inc(s_y.sem, 1)
                for s in STREAMS:
                    pe.wait_ge(s_yt.sem, s_yt.at(s))
                    for c in range(NC):
                        for j in range(2):
                            last = pe.matmul(bank(s, 3)[:, c:c + 1], BIG1[s][:, 4 + j, c * P:(c + 1) * P], ones[:, 0:1],
                                             start=(j == 0), stop=(j == 1))
                    last.then_inc(s_o.sem, 1)
                    by_token(s, 2, lambda b, c: BIG1[s][:, 2 + b, c * P:(c + 1) * P], lambda b: w("s_out", b * P, P), 2)\
                        .then_inc(s_o.sem, 1)

            pe.wait_ge(in_sem["c"], 32)
            pe.wait_ge(known, 1)
            for k in range(2):
                last = pe.transpose(bank(0, k)[0:N0, 0:P], BIG1[1][:, 1, k * N0:(k + 1) * N0], ident)
            last.then_inc(setup_pe, 1)
            pe.wait_ge(known, 2)
            pe.transpose(bank(0, 2)[0:1, 0:N0], sc[0:N0, 14:15], ident[0:N0, 0:N0]).then_inc(setup_pe, 1)
            pe.wait_ge(known, 3)
            pe.wait_ge(ready, 2)
            for x in (*in_sem.values(), *wsem):
                pe.wait_ge(x, 16)
            alike = pe.value_load(flag[0:1, 0:1], min_val=0, max_val=1)
            with pe.Fori(0, 4 // NS):
                if on[L0]:
                    turn(LNI[L0])
                    state_space()
                if on[L0F]:
                    turn(LNI[L0F])
                    feed_forward()
                if on[L1]:
                    turn(LNI[L1])
                    mamba()
                if on[L1F]:
                    turn(LNI[L1F])
                    route(0, "r1", LNI[L1F])
                    experts_gelu()
                if on[L2]:
                    turn(LNI[L2])
                    attention()
                if on[L2F]:
                    turn(LNI[L2F])
                    ternary()
                if on[L3]:
                    turn(LNI[L3])
                    last_scan()
                if on[L3F]:
                    turn(LNI[L3F])
                    route(1, "r3", LNI[L3F])
                    experts_silu()
                end_of_pair(pe, "pe")


def layout(i):
    import numpy as np

    f = {k: np.asarray(v) for k, v in i.items()}
    blocks = lambda a: np.concatenate([a[k * P:(k + 1) * P] for k in range(a.shape[0] // P)], 1)
    cols = lambda v: np.ascontiguousarray(v.reshape(-1, P).T)
    wx = f["L1_attn_W_xproj"]
    bc = wx[:, 8:40]
    t4 = lambda a: blocks(a.T)
    hk = {
        "l0_in": f["L0_attn_in_proj_w"].T,
        "l0_out": blocks(f["L0_attn_out_proj_w"].T),
        "f0_r": f["L0_ffn_W_r"].T, "f0_k": f["L0_ffn_W_k"].T, "f0_v": f["L0_ffn_W_v"].T,
        "m_in": f["L1_attn_W_in"], "m_dt": blocks(wx[:, 0:8]),
        "m_bc": blocks(np.concatenate([bc, bc, bc], 1)), "m_out": blocks(f["L1_attn_W_out"]),
        "r1": f["L1_ffn_Wr"].T, "a_qkv": f["L2_attn_qkv_w"].T, "a_out": f["L2_attn_proj_w"].T,
        "t_w1": f["L2_ffn_w1_w"].T, "t_w2": f["L2_ffn_w2_w"].T, "t_h1": t4(f["L2_ffn_h1_w"]),
        "t_h2": t4(f["L2_ffn_h2_w"]), "t_w3": t4(f["L2_ffn_w3_w"]), "s_in": f["L3_attn_W_in"],
        "s_abc": blocks(np.concatenate([f["L3_attn_W_A"], f["L3_attn_W_B"], f["L3_attn_W_C"]], 1)),
        "s_out": blocks(f["L3_attn_W_out"]), "r3": f["L3_ffn_Wg"],
    }
    wts = np.concatenate([hk[k] for k, _ in WCOLS], 1)
    tap = lambda a: a[:, 0, :].reshape(-1, P, 4).transpose(1, 0, 2).reshape(P, -1)
    e4 = lambda a: a.reshape(NE, 4, P).transpose(2, 0, 1).reshape(P, 32)
    a0 = f["L0_attn_A_param"][0, 0]
    pk = {
        "conv0_w": tap(f["L0_attn_conv_w"]), "conv0_b": cols(f["L0_attn_conv_b"]), "lnw": cols(f["L0_attn_ln_w"]),
        "lnb": cols(f["L0_attn_ln_b"]), "mu_r": cols(f["L0_ffn_mu_r"]), "mu_k": cols(f["L0_ffn_mu_k"]),
        "g1": cols(f["L1_attn_ln_g"]), "b1g": cols(f["L1_attn_ln_b"]), "conv1_w": tap(f["L1_attn_conv_w"]),
        "conv1_b": cols(f["L1_attn_conv_b"]), "b_dt": cols(f["L1_attn_b_dt"]),
        "alog": f["L1_attn_A_log"].reshape(2, P, NM).transpose(1, 0, 2).reshape(P, 32), "dm": cols(f["L1_attn_D"]),
        "mb1": e4(f["L1_ffn_b1"]), "w1_s": cols(f["L2_ffn_w1_s"]), "w2_s": cols(f["L2_ffn_w2_s"]),
        "h1_s": cols(f["L2_ffn_h1_s"]), "h2_s": cols(f["L2_ffn_h2_s"]), "normw": cols(f["L3_attn_norm_w"]),
        "bg": e4(f["L3_ffn_b_gate"]), "bu": e4(f["L3_ffn_b_up"]),
        "alpha": np.repeat(f["L2_attn_alpha_log"], 8)[:, None], "beta": np.repeat(f["L2_attn_beta_log"], 8)[:, None],
        "a0": np.concatenate([a0, a0])[:, None],
        "w3_s": np.broadcast_to(f["L2_ffn_w3_s"], (P, P)),
    }
    prm = np.concatenate([pk[k] for k, _ in PCOLS], 1)
    row = lambda v: np.broadcast_to(np.asarray(v, np.float32), (P, len(v)))
    t = np.arange(T)
    ck = {
        "ident": np.eye(P, dtype=np.float32),
        "tri": (np.arange(P)[:, None] <= t[None, :]).astype(np.float32),
        "pos": row(t + 1), "m_ref": row(np.arange(REF + 64) - REF), "mod128": row(t % P), "mod64": row(t % 64),
        "iota8": row(np.arange(NE)),
        "pick": (np.arange(P)[:, None] % 32 == np.arange(32)[None, :]).astype(np.float32),
    }
    cst = np.concatenate([ck[k] for k, _ in CCOLS], 1)
    r = np.arange(P)
    h2, d, e = r // 64, r // 8 % 8, r % 8
    one = lambda rows: (r[:, None] == rows[None, :]).astype(np.float32)
    byd = [one(8 * (2 * b + h2) + d) for b in range(NB0)]
    bye = [one(8 * (2 * b + h2) + e) for b in range(NB0)]
    sel = np.concatenate(byd + bye + [m.T for m in bye], 1)
    w1, w2 = f["L1_ffn_W1"], f["L1_ffn_W2"]
    fold = lambda a: a.reshape(NE, 4, P, P).transpose(0, 2, 1, 3).reshape(NE, P, 4 * P)
    x4 = lambda a: a.reshape(4, NC, P, P)
    return {
        "x": x4(f["L0_attn_x"]).transpose(0, 2, 1, 3), "w": wts, "p": prm, "c": cst, "sel": sel,
        "a": f["L0_attn_A_param"].reshape(NB0, P, N0).transpose(1, 0, 2).reshape(P, NB0 * N0),
        "e1": np.concatenate([w1, fold(w2)], 2),
        "e3": np.concatenate([f["L3_ffn_w_gate"], f["L3_ffn_w_up"], fold(f["L3_ffn_w_down"])], 2),
        "r8": np.concatenate([f["L1_ffn_b2"], f["L3_ffn_b_down"], f["L1_attn_W_dt"]], 1),
    }


def build(nc, arrays, layers=NLAYERS):
    d = {k: nc.dram_tensor(f"in_{k}_dram", a.shape, mybir.dt.from_np(a.dtype), kind="ExternalInput").ap()
         for k, a in arrays.items()}
    out = nc.dram_tensor("out_0_dram", (4, T, P), F32, kind="ExternalOutput").ap()
    network(nc, d["x"], d["w"], d["p"], d["c"], d["sel"], d["a"], d["e1"], d["e3"], d["r8"],
            out.rearrange("b (c p) n -> b p c n", c=NC), layers)


def kernel(**inputs):
    import numpy as _np
    import concourse.bacc as _bacc
    from concourse.bass_utils import run_bass_kernel_spmd as _run

    arrays = {k: _np.ascontiguousarray(v) for k, v in layout(inputs).items()}
    nc = _bacc.Bacc("TRN2", target_bir_lowering=False, num_devices=1)
    build(nc, arrays)
    r = _run(nc, [{f"in_{k}_dram": v for k, v in arrays.items()}], core_ids=[0])
    return r.results[0]["out_0_dram"]
```

```python
from contextlib import ExitStack

import concourse.bass as bass
from concourse import mybir

F32 = mybir.dt.float32
F32R = mybir.dt.float32r
BF16 = mybir.dt.bfloat16
U32 = mybir.dt.uint32
I32 = mybir.dt.int32
ALU = mybir.AluOpType
ACT = mybir.ActivationFunctionType
AX = mybir.AxisListType

P = 128
T = 512
NC = T // P
NS = 2
PAD = 3
NE = 8
DI = 1024
NB0 = DI // P
N0 = 64
N3 = 16
NM = 16
REF = T - P
STEEPEST = 1.2
LN_EPS = 1e-5
RMS_EPS = 1.1920928955078125e-07
EPS6 = 1e-6

WCOLS = [("l0_in", 17 * P), ("l0_out", 8 * P), ("f0_r", P), ("f0_k", P), ("f0_v", P),
         ("m_in", 4 * P), ("m_x", 2 * 104), ("m_out", 2 * P), ("r1", NE),
         ("a_qkv", 3 * P), ("a_out", P), ("t_w1", 4 * P), ("t_w2", 4 * P), ("t_h1", 16 * P),
         ("t_h2", 16 * P), ("t_w3", 4 * P), ("s_in", 4 * P), ("s_abc", 2 * 96), ("s_out", 2 * P),
         ("r3", NE)]
WOFF = {}
_n = 0
for _k, _w in WCOLS:
    WOFF[_k] = (_n, _w)
    _n += _w
WTOT = _n
PCOLS = [("conv0_w", 32), ("conv0_b", 8), ("lnw", 8), ("lnb", 8), ("mu_r", 1), ("mu_k", 1),
         ("g1", 1), ("b1g", 1), ("conv1_w", 8), ("conv1_b", 2), ("b_dt", 2), ("alog", 32), ("dm", 2),
         ("mb1", 32), ("w1_s", 4), ("w2_s", 4), ("h1_s", 4), ("h2_s", 4), ("normw", 2),
         ("bg", 32), ("bu", 32), ("alpha", 1), ("beta", 1), ("a0", 1), ("w3_s", P)]
POFF = {}
_n = 0
for _k, _w in PCOLS:
    POFF[_k] = (_n, _w)
    _n += _w
PTOT = _n
CCOLS = [("ident", P), ("tri", T), ("iota8", NE), ("pos", T), ("m_ref", REF + 64), ("mod128", T),
         ("mod64", T), ("pick", 32)]
COFF = {}
_n = 0
for _k, _w in CCOLS:
    COFF[_k] = (_n, _w)
    _n += _w
CTOT = _n

OFF_RECT = [0, 0, P, 3 * P]
OFF_D0 = 6 * P
OFF_D1 = OFF_D0 + T
NKEY = OFF_D1 + T
OFF_MT = [0, 512, 896, 1152]
NMT = 1280
RING = 3
RUNS = {
    "pe": [
        1, 1, 1, 1, 1, 1, 8, 1, 3, 2, 1, 1, 1, 1, 2, 2, 1, 1, 1, 1, 1, 2, 1, 1, 2, 1, 1, 1, 1, 1, 1,
        1, 2, 2, 3, 1, 1, 1, 2, 1, 7, 1, 10, 1, 11, 2, 8, 1, 1, 1, 2, 3, 4, 4, 1, 36, 1, 1, 3, 1, 1,
        3, 2, 1, 9, 1, 6, 1, 4, 2, 4, 1, 6, 2, 1, 2, 1, 1, 6, 1, 2, 1, 2, 1, 1, 1, 1, 2, 4, 4, 1, 1,
        3, 5, 2, 2, 2, 2, 2, 1, 2, 3, 2, 6, 1, 4, 1, 8, 1, 2, 1, 4, 2, 1, 6, 1, 2, 1, 11, 1, 5, 1,
        7, 2, 1, 1, 3, 2, 2, 1, 3, 1, 7, 1, 2, 1, 6, 1, 1, 6, 1, 6, 1, 13, 1, 1, 1, 1, 1, 1, 2, 1,
        2, 1, 2, 1, 1, 1, 3, 2, 1, 1, 2, 1, 4, 1, 5, 1, 2, 1, 2, 1, 2, 2, 1, 3, 1, 7, 1, 1, 7, 1, 2,
        1, 2, 1, 2, 1, 6, 1, 1, 1, 4, 3, 1, 4, 2, 4, 1, 5, 1, 3, 1, 4, 1, 5, 1, 3, 2, 1, 2, 1, 6, 1,
        1, 10, 1, 7, 1, 1, 1, 3, 1, 3, 1, 1, 1, 18, 1, 1, 1, 1, 1, 1, 2, 3, 7, 1, 14, 1, 13, 1, 32,
        1, 6, 1, 9, 1, 2, 3, 2, 3, 3, 1, 1, 2, 1, 80],
    "act": [
        0, 1, 2, 1, 3, 1, 6, 1, 1, 2, 3, 1, 2, 2, 1, 1, 3, 1, 3, 1, 1, 2, 1, 1, 1, 1, 2, 2, 3, 1, 5,
        7, 2, 1, 2, 2, 2, 3, 2, 4, 1, 1, 2, 8, 8, 1, 2, 1, 1, 1, 9, 1, 4, 2, 1, 4, 2, 1, 2, 1, 2, 1,
        4, 3, 2, 1, 2, 1, 3, 1, 1, 1, 1, 1, 1, 1, 2, 1, 2, 2, 1, 4, 2, 2, 2, 3, 3, 2, 1, 13, 1, 1,
        1, 3, 1, 2, 13, 1, 5, 2, 2, 3, 8, 1, 1, 1, 3, 6, 1, 2, 1, 2, 1, 1, 1, 4, 1, 3, 1, 2, 1, 1,
        2, 1, 2, 2, 1, 6, 1, 1, 2, 1, 2, 1, 2, 5, 1, 4, 1, 3, 1, 1, 1, 2, 2, 3, 1, 1, 6, 1, 1, 1, 1,
        4, 2, 5, 2, 3, 1, 1, 7, 1, 2, 1, 17, 1, 2, 1, 1, 1, 3, 32],
    "dve": [
        2, 2, 1, 1, 1, 1, 8, 5, 3, 1, 4, 1, 1, 1, 2, 1, 1, 1, 2, 1, 1, 5, 1, 1, 2, 2, 1, 2, 1, 1, 5,
        1, 1, 2, 2, 2, 2, 1, 2, 1, 3, 1, 2, 1, 3, 1, 3, 1, 11, 1, 1, 1, 2, 1, 9, 1, 1, 1, 3, 1, 2,
        2, 3, 1, 2, 1, 3, 1, 1, 1, 1, 2, 3, 3, 1, 2, 1, 1, 4, 1, 1, 2, 1, 1, 1, 3, 1, 2, 1, 3, 1, 1,
        3, 1, 1, 1, 1, 1, 3, 3, 1, 2, 1, 2, 1, 1, 2, 3, 1, 3, 1, 5, 2, 5, 1, 5, 1, 1, 1, 4, 1, 3, 2,
        2, 1, 6, 1, 5, 1, 3, 1, 2, 3, 1, 2, 1, 2, 1, 4, 1, 9, 1, 14, 1, 3, 1, 5, 42, 12, 3, 4, 2, 1,
        1, 1, 2, 1, 1, 3, 1, 3, 2, 12, 1, 8, 1, 1, 1, 1, 1, 3, 1, 2, 1, 2, 1, 1, 1, 1, 1, 2, 4, 1,
        34],
    "pool": [
        2, 2, 1, 1, 2, 1, 2, 1, 1, 1, 2, 1, 11, 1, 4, 1, 2, 1, 1, 1, 1, 2, 2, 2, 1, 1, 1, 1, 2, 2,
        1, 2, 1, 2, 1, 4, 1, 12, 2, 2, 1, 1, 2, 2],
    "loads": [
        8, 8, 8, 8],
}
NLAYERS = 8


class Signal:

    def __init__(self, sems, bases, total):
        self.sems, self.bases, self.total = sems, bases, total

    def __getitem__(self, s):
        return self.sems[s]

    def at(self, s, k):
        return self.bases[s] + (self.total if k == -1 else k + 1)


def turns(who):
    return [i % 2 for i, run in enumerate(RUNS[who]) for _ in range(run)]


def expert_loads():
    met = [0] * NS
    order = []
    for s in turns("loads"):
        order.append((met[s] // NE, s, met[s] % NE))
        met[s] += 1
    return order


def network(nc, x_d, w_d, p_d, c_d, sel_d, a_d, e1_d, e3_d, r8_d, out_d, layers=NLAYERS):
    ctx = ExitStack()

    def sb(name, shape, dt=F32):
        return ctx.enter_context(nc.sbuf_tensor(name, shape, dt))

    def sem(name):
        return ctx.enter_context(nc.semaphore(name))

    with ctx:
        W = sb("weights", [P, WTOT])
        PR = sb("params", [P, PTOT])
        CN = sb("consts", [P, COFF["pos"][0]])
        SELR = sb("selectors_rounded", [P, 2 * NB0 * P], F32R)
        SEL = sb("selectors", [P, NB0 * P])
        R8 = sb("rows8", [NE, 4 * P])
        ring = sb("expert_ring", [P, RING, 1536])
        PS = ctx.enter_context(nc.psum_tensor("ps", [P, 8, T], F32))
        X = [sb(f"x{s}", [P, NC, P]) for s in range(NS)]
        XT = [sb(f"xT{s}", [P, PAD + T]) for s in range(NS)]
        BIG1 = [sb(f"big1_{s}", [P, 8, T]) for s in range(NS)]
        BIG2 = [sb(f"big2_{s}", [P, 4, T]) for s in range(NS)]
        MT = [sb(f"mt{s}", [P, NMT]) for s in range(NS)]
        KEY = [sb(f"key{s}", [P, NKEY]) for s in range(NS)]
        XN = [KEY[s][:, 0:T].rearrange("p (c n) -> p c n", c=NC) for s in range(NS)]
        PARTS = sb("qkv_parts", [P, 2, 3, T], F32R)
        QSPL = [sb(f"q128_{s}", [96, T]) for s in range(NS)]
        Q128 = [q[0:N0, :] for q in QSPL]
        BT = [sb(f"bT{s}", [N0, T]) for s in range(NS)]
        UP = [sb(f"up{s}", [P, 2, PAD + T]) for s in range(NS)]
        CV = [sb(f"cv{s}", [P, 2, T]) for s in range(NS)]
        Q64 = [CV[s][0:N0, 1, :] for s in range(NS)]
        XH = [CV[s][:, 0, :].rearrange("p (c n) -> p c n", c=NC) for s in range(NS)]
        SETUP = BIG1[0][:, :, :].rearrange("p k n -> p (k n)")
        SPL = [q[:, 0:T // 2].bitcast(BF16) for q in QSPL]
        SM = sb("row_pick", [96, 32], BF16)
        ekey = sb("ekey", [N0, REF + 64])
        eq128 = sb("eq128", [N0, P])
        eq64 = sb("eq64", [N0, P])
        rden = sb("rden", [P, T])
        nega = sb("nega", [P, 2 * NM])
        omu = sb("omu", [P, 2])
        nhalf = sb("nhalf", [P, NC])
        ones = sb("ones", [P, 1])
        sc = sb("setup_cols", [P, 17])
        stat = [sb(f"stat{s}", [P, NC, 2, 6]) for s in range(NS)]
        mv = [sb(f"mv{s}", [P, NC, 2]) for s in range(NS)]
        ve = [sb(f"ve{s}", [P, NC]) for s in range(NS)]
        rstd = [sb(f"rstd{s}", [P, NC]) for s in range(NS)]
        flag = sb("all_alike", [1, 1], I32)
        factored = sb("factored", [P, 1])
        ones64 = sb("ones64", [N0, P])
        negr = [sb(f"negr{s}", [N3, 8]) for s in range(NS)]
        lg = [sb(f"lg{s}", [P, 4, NC, NE]) for s in range(NS)]
        top = [sb(f"top{s}", [P, NC, 8]) for s in range(NS)]
        topi = [sb(f"topi{s}", [P, NC, 8], U32) for s in range(NS)]
        topf = [sb(f"topf{s}", [P, NC, 8]) for s in range(NS)]
        cmb = [sb(f"cmb{s}", [P, NC, NE]) for s in range(NS)]
        cmbT = [BT[s][0:NE, :] for s in range(NS)]
        sm4 = [sb(f"sm4_{s}", [P, 4, NC]) for s in range(NS)]

        in_sem = {n: sem(f"in_{n}") for n in ("p", "c", "selr", "sel", "r8", "a")}
        wsem = [sem(f"in_w{i}") for i in range(4)]
        setup_dve = sem("setup_dve")
        setup_act = sem("setup_act")
        setup_pe = sem("setup_pe")
        known = sem("known")
        ready = sem("setup_ready")
        arrived = sem("arrived")
        go = {e: sem(f"go_{e}") for e in ("pe", "act", "dve", "pool")}
        general_ended = sem("general_ended")
        stored = sem("stored")

        body_sems = []

        def body_sem(name):
            body_sems.append(sem(name))
            return body_sems[-1]

        x_in = [body_sem(f"x_in{s}") for s in range(NS)]
        ring_in = [body_sem(f"ring_in{i}") for i in range(RING)]
        dve_own = body_sem("dve_own")
        act_own = body_sem("act_own")
        g_dma, g_row, g_ps, g_sum = (body_sem(f"g_{n}") for n in ("dma", "row", "ps", "sum"))
        stage_sems = {(e, n, s): body_sem(f"{e}_stage{n}_stream{s}")
                      for e, m in (("pe", 9), ("act", 7), ("dve", 9), ("pool", 4)) for n in range(m) for s in range(NS)}
        raised = {}
        nth = {}

        def layer_begins():
            nth.clear()

        def S(engine, total):
            n = nth.get(engine, 0)
            nth[engine] = n + 1
            bases = [raised.get((engine, n), 0)] * NS
            raised[engine, n] = bases[0] + total
            return Signal([stage_sems[engine, n, s] for s in range(NS)], bases, total)

        class Norm:

            def __init__(self, turned=True):
                self.var = S("dve", 1)
                self.rs = S("pool", 1)
                self.done = S("dve", 1)
                if turned:
                    self.T = S("pe", 1)
                    self.xT = S("act", 1)

        layer_begins()
        n0 = Norm()
        x_done = [S("dve", 1)]
        l0_bc = S("pe", 1)
        l0_z = S("pe", 8)
        l0_sc = S("pe", 4)
        l0_u = S("pe", 8)
        l0_xt = S("pe", 8)
        l0_y = S("pe", 8)
        l0_yt = S("pe", 8)
        l0_o = S("pe", 2)
        l0_bt = S("act", 1)
        l0_zs = S("act", 8)
        l0_up = S("act", 8)
        l0_sl = S("act", 8)
        l0_xc = S("act", 8)
        l0_yn = S("act", 8)
        l0_q = S("dve", 2)
        l0_mt = S("dve", 4)
        l0_cv = S("dve", 8)
        l0_yg = S("dve", 8)
        l0_var = S("dve", 1)
        l0_nm = S("dve", 4)
        l0_key = S("pool", 1)
        l0_rs = S("pool", 1)
        layer_begins()
        n1 = Norm()
        x_done.append(S("dve", 1))
        f0_p = S("pe", 3)
        f0_rl = S("act", 1)
        f0_sg = S("act", 1)
        f0_mix = S("dve", 2)
        f0_ka = S("dve", 1)
        layer_begins()
        n2o = Norm(turned=False)
        n2 = Norm()
        x_done.append(S("dve", 1))
        m_uz = S("pe", 4)
        m_xd = S("pe", 1)
        m_dt = S("pe", 2)
        m_bc = S("pe", 2 * NM)
        m_ya = S("pe", NM)
        m_o = S("pe", 1)
        m_up = S("act", 2)
        m_uz_s = S("act", 4)
        m_d8 = S("act", 1)
        m_sp = S("act", 2)
        m_bs = S("act", NM)
        m_da = S("act", 2 * NM)
        m_cv = S("dve", 2)
        m_mix = S("dve", 5)
        m_scan = S("dve", 4 * NM)
        m_d1 = S("pool", NM)
        m_acc = S("pool", NM - 1)
        moe = []

        class Moe:
            def __init__(self, gated):
                layer_begins()
                self.n = Norm()
                x_done.append(S("dve", 1))
                self.lg = S("pe", 1)
                self.ct = S("pe", 1)
                self.b = S("pe", 1)
                self.up = S("pe", NE * (8 if gated else 4))
                self.dn = S("pe", NE)
                self.ex = S("act", 1)
                self.cs = S("act", 1)
                self.act = S("act", 4 * NE)
                self.sh = S("dve", 1)
                self.cb = S("dve", 1)
                self.bx = S("dve", 1)
                self.h = S("dve", 4 * NE if gated else 0)
                self.x = S("dve", NE - 1)

        moe.append(Moe(False))
        layer_begins()
        n4 = Norm()
        x_done.append(S("dve", 1))
        a_p = S("pe", 3)
        a_r = S("pe", 3 * NB0)
        a_red = S("pe", NB0)
        a_y = S("pe", 1)
        a_ks = S("act", NB0)
        a_hi = S("act", 3)
        a_f = S("dve", 3)
        a_lo = S("dve", 3)
        a_kv = S("dve", NB0)
        a_cum = S("dve", NB0)
        a_qk = S("dve", NB0)
        a_o = S("dve", 1)
        layer_begins()
        n5 = Norm()
        x_done.append(S("dve", 1))
        t_ab = S("pe", 8)
        t_p1 = S("pe", 4)
        t_p2 = S("pe", 4)
        t_o = S("pe", 1)
        t_sa = S("act", 4)
        t_g1 = S("act", 4)
        t_g2 = S("act", 4)
        t_h0 = S("dve", 4)
        layer_begins()
        n6 = Norm()
        x_done.append(S("dve", 1))
        s_ab = S("pe", 4)
        s_abc = S("pe", 1)
        s_sc = S("pe", 4)
        s_xt = S("pe", 2)
        s_y = S("pe", 2)
        s_o = S("pe", 2)
        s_slg = S("act", 4)
        s_ea = S("act", 1)
        s_ex = S("act", 1)
        s_xs = S("act", 2)
        s_yt = S("act", 2)
        s_xi = S("dve", 2)
        s_cl = S("dve", 2)
        s_f = S("dve", 1)
        s_mt = S("dve", 4)
        s_var = S("dve", 1)
        s_rs = S("pool", 1)
        moe.append(Moe(True))
        norms = [n0, n1, n2, moe[0].n, n4, n5, n6, moe[1].n]

        def w(name, lo=0, n=None):
            o, width = WOFF[name]
            return W[:, o + lo:o + (width if n is None else lo + n)]

        def pr(name, j=0, n=1):
            o, _ = POFF[name]
            return PR[:, o + j:o + j + n]

        def cn(name, rows=P):
            o, width = COFF[name]
            kept = COFF["pos"][0]
            return CN[0:rows, o:o + width] if o < kept else SETUP[0:rows, o - kept:o - kept + width]

        def bank(s, k):
            return PS[:, 4 * s + k, :]

        def bank4(s, k):
            return PS[:, 4 * s + k, :].rearrange("p (c n) -> p c n", c=NC)

        def chunk(s, c):
            return XT[s][:, PAD + c * P:PAD + (c + 1) * P]

        ident = cn("ident")
        STREAMS = range(NS)

        def whole(programs, s):
            for program in programs:
                yield from program(s)

        def walk(engine, programs):
            streams = [whole(programs, s) for s in STREAMS]
            for s in turns(engine):
                next(streams[s], None)
            assert all(next(g, "ended") == "ended" for g in streams)

        cuts = [0, WOFF["f0_r"][0], WOFF["a_qkv"][0], WOFF["s_in"][0], WTOT]

        block = ctx.enter_context(nc.Block())

        def end_of_pair(eng, name):
            eng.drain().then_inc(arrived, 1)
            eng.wait_ge(go[name], 1)
            eng.sem_clear(go[name])

        def first_block_general(eng, name, program):
            for s in STREAMS:
                for _ in program(s):
                    pass
            if name != "pool":
                eng.drain().then_inc(general_ended, 1)
                eng.wait_ge(go[name], 1)
                eng.sem_clear(go[name])
                return
            eng.wait_ge(general_ended, 3)
            eng.sem_clear(general_ended)
            for x in (*stage_sems.values(), dve_own, act_own, g_dma, g_row, g_ps, g_sum):
                eng.sem_clear(x)
            eng.drain()
            for e in ("pe", "act", "dve"):
                eng.sem_inc(go[e], 1)

        @block.sync
        def _(sp):
            sp.dma_start(BIG1[1][:, 0, :], a_d).then_inc(in_sem["a"], 16)
            sp.dma_start(PR[:], p_d).then_inc(in_sem["p"], 16)
            sp.dma_start(BIG1[1][:, 4:8, :], sel_d[:, 0:2 * NB0 * P].rearrange("p (k n) -> p k n", k=4))\
                .then_inc(in_sem["selr"], 16)
            kept = COFF["pos"][0]
            sp.dma_start(CN[:], c_d[:, 0:kept]).then_inc(in_sem["c"], 16)
            sp.dma_start(SETUP[:, 0:CTOT - kept], c_d[:, kept:CTOT]).then_inc(in_sem["c"], 16)
            sp.dma_start(W[:, cuts[0]:cuts[1]], w_d[:, cuts[0]:cuts[1]]).then_inc(wsem[0], 16)
            sp.dma_start(R8[:], r8_d).then_inc(in_sem["r8"], 16)
            with sp.Fori(0, 4 // NS) as i:
                for s in STREAMS:
                    sp.dma_start(X[s][:], x_d[i * NS + s]).then_inc(x_in[s], 16)
                loads = expert_loads()
                for q, (m, s, e) in enumerate(loads):
                    if q >= RING:
                        pm, ps_, pe_ = loads[q - RING]
                        sp.wait_ge(moe[pm].dn[ps_], moe[pm].dn.at(ps_, pe_))
                    dst = ring[:, q % RING, :] if m else ring[:, q % RING, 0:1024]
                    sp.dma_start(dst, (e3_d if m else e1_d)[e]).then_inc(ring_in[q % RING], 16)
                for s in STREAMS:
                    sp.wait_ge(x_done[layers - 1][s], x_done[layers - 1].at(s, -1))
                    sp.dma_start(out_d[i * NS + s], X[s][:]).then_inc(stored, 16)
                sp.wait_ge(stored, 16 * NS)
                sp.wait_ge(arrived, 4)
                sp.sem_clear(arrived)
                sp.sem_clear(stored)
                for x in body_sems:
                    sp.sem_clear(x)
                sp.drain()
                for e in ("pe", "act", "dve", "pool"):
                    sp.sem_inc(go[e], 1)

        @block.gpsimd
        def _(pool):
            def power(s, after, done):
                yield
                pool.wait_ge(after[s], after.at(s, 0))
                pool.tensor_tensor(rstd[s][:, :], ve[s][:, :], nhalf[:, :], ALU.pow).then_inc(done[s], 1)

            def ln(n, s):
                yield from power(s, n.var, n.rs)

            def state_space(general):
                def layer(s):
                    yield from ln(n0, s)
                    if general:
                        pool.sem_inc(l0_key[s], 1)
                    else:
                        yield
                        pool.wait_ge(l0_bt[s], l0_bt.at(s, 0))
                        for c in range(1, NC):
                            pool.tensor_tensor(KEY[s][0:N0, OFF_RECT[c]:OFF_RECT[c] + c * P], BT[s][:, 0:c * P],
                                               ekey[:, REF - c * P:REF], ALU.mult)
                        b4 = BT[s][:, :].rearrange("p (c n) -> p c n", c=NC)
                        k0 = KEY[s][0:N0, OFF_D0:OFF_D0 + T].rearrange("p (c n) -> p c n", c=NC)
                        k1 = KEY[s][0:N0, OFF_D1:OFF_D1 + T].rearrange("p (c n) -> p c n", c=NC)
                        pool.tensor_tensor(k0[:, :, 0:64], b4[:, :, 0:64],
                                           ekey[:, REF:REF + 64].unsqueeze(1).broadcast_to([N0, NC, 64]), ALU.mult)
                        pool.tensor_tensor(k1, b4, ekey[:, REF - 64:REF + 64].unsqueeze(1).broadcast_to([N0, NC, P]),
                                           ALU.mult).then_inc(l0_key[s], 1)
                    yield from power(s, l0_var, l0_rs)
                return layer

            def add_state(s, n):
                yield
                pool.wait_ge(m_scan[s], m_scan.at(s, 4 * n + 3))
                if n > 1:
                    pool.wait_ge(m_acc[s], m_acc.at(s, n - 2))
                total = MT[s][:, T:2 * T]
                pool.tensor_tensor(total, total, BIG2[s][:, 3, :], ALU.add).then_inc(m_acc[s], 1)

            def mamba(s):
                yield from ln(n2o, s)
                yield from ln(n2, s)
                for n in range(NM):
                    yield
                    pool.wait_ge(m_bs[s], m_bs.at(s, n))
                    if n == 0:
                        pool.wait_ge(m_mix[s], m_mix.at(s, 2))
                    else:
                        pool.wait_ge(m_scan[s], m_scan.at(s, 4 * n - 2))
                    pool.tensor_tensor(BIG2[s][:, 1, :], BIG1[s][:, 3, :], MT[s][:, 0:T], ALU.mult).then_inc(m_d1[s], 1)
                    if n >= 2:
                        yield from add_state(s, n - 1)
                yield from add_state(s, NM - 1)

            def plain(layer):
                return lambda s: ln(norms[layer], s)

            def last_scan(s):
                yield from ln(n6, s)
                yield from power(s, s_var, s_rs)

            pool.wait_ge(ready, 2)
            pool.wait_ge(known, 3)
            alike = pool.value_load(flag[0:1, 0:1], min_val=0, max_val=1)

            with pool.Fori(0, 4 // NS):
                with pool.If(alike == 0):
                    first_block_general(pool, "pool", state_space(True))
                walk("pool", [state_space(False), plain(1), mamba, plain(3), plain(4), plain(5), last_scan, plain(7)])
                end_of_pair(pool, "pool")

        @block.scalar
        def _(act):
            own = [0]

            def step(ins):
                own[0] += 1
                ins.then_inc(act_own, 1)
                act.wait_ge(act_own, own[0])

            def setup():
                act.wait_ge(in_sem["p"], 16)
                act.wait_ge(in_sem["c"], 32)
                act.activation(sc[0:N0, 0:1], pr("a0")[0:N0], ACT.Exp).then_inc(setup_act, 1)
                act.activation(nega[:, :], pr("alog", 0, 32), ACT.Exp).then_inc(setup_act, 1)
                act.activation(sc[:, 2:3], pr("alpha"), ACT.Exp).then_inc(setup_act, 1)
                act.activation(sc[:, 3:4], pr("beta"), ACT.Exp).then_inc(setup_act, 1)
                act.wait_ge(setup_act, 4)
                act.wait_ge(setup_dve, 2)
                act.activation(ekey[:, :], cn("m_ref", N0), ACT.Exp, scale=sc[0:N0, 16:17])
                act.activation(eq128[:, :], cn("mod128", N0)[:, 0:P], ACT.Exp, scale=sc[0:N0, 1:2])
                act.activation(eq64[:, :], cn("mod64", N0)[:, 0:P], ACT.Exp, scale=sc[0:N0, 1:2])
                act.activation(sc[:, 4:6], sc[:, 2:4], ACT.Ln, bias=1.0).then_inc(setup_act, 1)
                act.wait_ge(setup_act, 5)
                act.drain().then_inc(ready, 1)
                act.wait_ge(wsem[0], 16)
                for i in (1, 2, 3):
                    act.dma_start(W[:, cuts[i]:cuts[i + 1]], w_d[:, cuts[i]:cuts[i + 1]]).then_inc(wsem[i], 16)
                act.dma_start(SEL[:], sel_d[:, 2 * NB0 * P:]).then_inc(in_sem["sel"], 16)

            def turned(n, s, gain=None):
                yield
                act.wait_ge(n.T[s], n.T.at(s, 0))
                if gain:
                    act.activation(XT[s][:, PAD:PAD + T], bank(s, 3), ACT.Identity, bias=pr("b1g"),
                                   scale=pr("g1")).then_inc(n.xT[s], 1)
                else:
                    act.activation(XT[s][:, PAD:PAD + T], bank(s, 3), ACT.Copy).then_inc(n.xT[s], 1)

            def state_space(general):
                def conv_block(s, b):
                    yield
                    if b < 8:
                        act.wait_ge(l0_u[s], l0_u.at(s, b))
                        if b >= 2:
                            act.wait_ge(l0_cv[s], l0_cv.at(s, b - 2))
                        act.activation(UP[s][:, b % 2, PAD:PAD + T], bank(s, b % 2), ACT.Copy).then_inc(l0_up[s], 1)
                    if b >= 1:
                        j = b - 1
                        yield
                        act.wait_ge(l0_xt[s], l0_xt.at(s, j))
                        if j == 4:
                            act.wait_ge(l0_y[s], l0_y.at(s, 3))
                        act.activation(BIG2[s][:, :, (j % 4) * P:(j % 4 + 1) * P], bank4(s, 2 + j % 2), ACT.Copy)\
                            .then_inc(l0_xc[s], 1)
                    yield
                    if b < 8:
                        act.wait_ge(l0_cv[s], l0_cv.at(s, b))
                        act.activation(CV[s][:, b % 2, :], CV[s][:, b % 2, :], ACT.Silu).then_inc(l0_sl[s], 1)

                def inputs_general(s):
                    if s:
                        act.wait_ge(l0_yg[0], l0_yg.at(0, 7))
                    decay = KEY[1][:, 0:NB0 * N0]
                    act.dma_start(decay, a_d).then_inc(g_dma, 16)
                    act.wait_ge(g_dma, 16 * (s + 1))
                    act.activation(decay, decay, ACT.Exp)
                    act.drain()
                    act.activation(decay, decay, ACT.Exp, scale=-1.0)
                    act.wait_ge(l0_sc[s], l0_sc.at(s, 0))
                    act.activation(Q128[s][:, :], bank(s, 1)[0:N0, :], ACT.Copy)
                    act.drain().then_inc(l0_xc[s], 8)
                    for j in range(NB0):
                        act.wait_ge(l0_u[s], l0_u.at(s, j))
                        act.activation(UP[s][:, 0, PAD:PAD + T], bank(s, 0), ACT.Copy).then_inc(l0_up[s], 1)
                        act.wait_ge(l0_cv[s], l0_cv.at(s, j))
                        act.activation(CV[s][:, 0, :], CV[s][:, 0, :], ACT.Silu).then_inc(l0_sl[s], 1)

                def layer(s):
                    yield from turned(n0, s)
                    yield
                    act.wait_ge(l0_bc[s], l0_bc.at(s, 0))
                    act.activation(BT[s][:, :], bank(s, 0)[0:N0, :], ACT.Copy).then_inc(l0_bt[s], 1)
                    for k in range(8):
                        c, h = k // 2, k % 2
                        yield
                        act.wait_ge(l0_z[s], l0_z.at(s, k))
                        act.activation(BIG1[s][:, 2 * c + h, :], bank(s, k % 4), ACT.Silu).then_inc(l0_zs[s], 1)
                    if general:
                        inputs_general(s)
                    else:
                        for b in range(9):
                            yield from conv_block(s, b)
                    for j in range(8):
                        yield
                        act.wait_ge(l0_yt[s], l0_yt.at(s, j))
                        if j == 4:
                            act.wait_ge(l0_o[s], l0_o.at(s, 0))
                        act.activation(BIG2[s][:, j % 4, :], bank(s, j % 2), ACT.Identity, bias=pr("lnb", j),
                                       scale=pr("lnw", j)).then_inc(l0_yn[s], 1)
                return layer

            def feed_forward(s):
                yield from turned(n1, s)
                yield
                act.wait_ge(f0_p[s], f0_p.at(s, 0))
                act.activation(BIG1[s][:, 4, :], bank(s, 0), ACT.Relu).then_inc(f0_rl[s], 1)
                yield
                act.wait_ge(f0_p[s], f0_p.at(s, 1))
                act.activation(BIG1[s][:, 6, :], bank(s, 1), ACT.Sigmoid).then_inc(f0_sg[s], 1)

            def mamba(s):
                yield from turned(n2, s, gain=True)
                for j in range(2):
                    yield
                    act.wait_ge(m_uz[s], m_uz.at(s, j))
                    act.activation(UP[s][:, j, PAD:PAD + T], bank(s, j), ACT.Copy).then_inc(m_up[s], 1)
                for j in range(2):
                    yield
                    act.wait_ge(m_uz[s], m_uz.at(s, 2 + j))
                    act.activation(BIG1[s][:, 6 + j, :], bank(s, 2 + j), ACT.Silu).then_inc(m_uz_s[s], 1)
                for j in range(2):
                    yield
                    act.wait_ge(m_cv[s], m_cv.at(s, j))
                    act.activation(BIG1[s][:, 4 + j, :], CV[s][:, j, :], ACT.Silu).then_inc(m_uz_s[s], 1)
                yield
                act.wait_ge(m_xd[s], m_xd.at(s, 0))
                act.activation(BT[s][0:8, :], bank(s, 1)[96:104, :], ACT.Copy).then_inc(m_d8[s], 1)
                for j in range(2):
                    yield
                    act.wait_ge(m_dt[s], m_dt.at(s, j))
                    act.activation(CV[s][:, j, :], bank(s, 2 + j), ACT.Abs, bias=pr("b_dt", j))
                    last = act.activation(UP[s][:, j, PAD:PAD + T], bank(s, 2 + j), ACT.Relu, bias=pr("b_dt", j))
                step(last)
                step(act.activation(CV[s][:, :, :], CV[s][:, :, :], ACT.Exp, scale=-1.0))
                for j in range(2):
                    act.activation(CV[s][:, j, :], CV[s][:, j, :], ACT.Ln, bias=1.0).then_inc(m_sp[s], 1)
                for n in range(NM):
                    yield
                    act.wait_ge(m_bc[s], m_bc.at(s, 2 * n))
                    if n:
                        act.wait_ge(m_d1[s], m_d1.at(s, n - 1))
                    act.activation(MT[s][:, 0:T], bank(s, 2), ACT.Copy).then_inc(m_bs[s], 1)
                    for j in range(2):
                        yield
                        if n == 0:
                            act.wait_ge(m_mix[s], m_mix.at(s, 1 + j))
                        else:
                            act.wait_ge(m_scan[s], m_scan.at(s, 4 * n - 3 + j))
                        act.activation(CV[s][:, j, :], BIG1[s][:, j, :], ACT.Exp,
                                       scale=nega[:, j * NM + n:j * NM + n + 1]).then_inc(m_da[s], 1)

            def route(g, s):
                yield
                act.wait_ge(g.sh[s], g.sh.at(s, 0))
                act.activation(lg[s][:, 1], lg[s][:, 0], ACT.Exp).then_inc(g.ex[s], 1)
                yield
                act.wait_ge(g.ct[s], g.ct.at(s, 0))
                act.activation(cmbT[s][:, :], bank(s, 3)[0:NE, :], ACT.Copy).then_inc(g.cs[s], 1)

            def experts_gelu(s):
                g = moe[0]
                yield from turned(g.n, s)
                yield from route(g, s)
                for e in range(NE):
                    for k in range(4):
                        yield
                        act.wait_ge(g.up[s], g.up.at(s, 4 * e + k))
                        if k == 0 and e >= 2:
                            act.wait_ge(g.dn[s], g.dn.at(s, e - 2))
                        act.activation(BIG1[s][:, 4 * (e % 2) + k, :], bank(s, k % 3), ACT.Gelu,
                                       bias=pr("mb1", 4 * e + k)).then_inc(g.act[s], 1)

            def experts_silu(s):
                g = moe[1]
                yield from turned(g.n, s)
                yield from route(g, s)
                for e in range(NE):
                    for k in range(4):
                        yield
                        act.wait_ge(g.up[s], g.up.at(s, 8 * e + 2 * k))
                        if 4 * e + k >= 2:
                            act.wait_ge(g.h[s], g.h.at(s, 4 * e + k - 2))
                        act.activation(CV[s][:, k % 2, :], bank(s, (8 * e + 2 * k) % 3), ACT.Silu,
                                       bias=pr("bg", 4 * e + k)).then_inc(g.act[s], 1)

            def attention(s):
                yield from turned(n4, s)
                for k in range(3):
                    yield
                    act.wait_ge(a_f[s], a_f.at(s, k))
                    if s and k == 0:
                        act.wait_ge(a_r[0], a_r.at(0, -1))
                    act.activation(PARTS[:, 0, k, :], BIG1[s][:, k, :], ACT.Copy).then_inc(a_hi[s], 1)
                for b in range(NB0):
                    yield
                    act.wait_ge(a_r[s], a_r.at(s, 3 * b))
                    if b:
                        act.wait_ge(a_kv[s], a_kv.at(s, b - 1))
                    act.activation(CV[s][:, 0, :], bank(s, 0), ACT.Copy).then_inc(a_ks[s], 1)

            def ternary(s):
                yield from turned(n5, s)
                for j in range(4):
                    yield
                    act.wait_ge(t_ab[s], t_ab.at(s, 2 * j))
                    if j >= 2:
                        act.wait_ge(t_h0[s], t_h0.at(s, j - 2))
                    act.activation(CV[s][:, j % 2, :], bank(s, j % 2), ACT.Silu, scale=pr("w1_s", j))\
                        .then_inc(t_sa[s], 1)
                for p, g, src, dst in ((t_p1, t_g1, "h1_s", 4), (t_p2, t_g2, "h2_s", 0)):
                    for j in range(4):
                        yield
                        act.wait_ge(p[s], p.at(s, j))
                        if dst == 0 and j == 0:
                            act.wait_ge(t_p1[s], t_p1.at(s, 3))
                        act.activation(BIG1[s][:, dst + j, :], bank(s, j), ACT.Gelu, scale=pr(src, j)).then_inc(g[s], 1)

            def last_scan(s):
                yield from turned(n6, s)
                for j in range(2):
                    yield
                    act.wait_ge(s_ab[s], s_ab.at(s, j))
                    act.activation(CV[s][:, j, :], bank(s, j), ACT.Silu).then_inc(s_slg[s], 1)
                for j in range(2):
                    yield
                    act.wait_ge(s_ab[s], s_ab.at(s, 2 + j))
                    act.activation(UP[s][:, j, PAD:PAD + T], bank(s, 2 + j), ACT.Sigmoid).then_inc(s_slg[s], 1)
                yield
                act.wait_ge(s_cl[s], s_cl.at(s, 0))
                act.activation(BT[s][0:N3, :], BT[s][0:N3, :], ACT.Exp).then_inc(s_ea[s], 1)
                for j in range(2):
                    yield
                    act.wait_ge(s_xt[s], s_xt.at(s, j))
                    act.activation(BIG2[s][:, 2 * j:2 * j + 2, 0:2 * P],
                                   bank(s, 3).rearrange("p (c n) -> p c n", c=2), ACT.Copy).then_inc(s_xs[s], 1)
                yield
                act.wait_ge(s_cl[s], s_cl.at(s, 1))
                cum = BT[s][0:N3, :]
                for c in range(NC):
                    a = c * P
                    act.activation(Q128[s][0:N3, a:a + P], cum[:, a:a + P], ACT.Exp, scale=-1.0, bias=cum[:, a:a + 1])
                    act.activation(Q64[s][0:N3, a + 64:a + P], cum[:, a + 64:a + P], ACT.Exp, scale=-1.0,
                                   bias=cum[:, a + 64:a + 65])
                    if c:
                        act.activation(KEY[s][0:N3, OFF_RECT[c]:OFF_RECT[c] + a], cum[:, 0:a], ACT.Exp,
                                       bias=negr[s][:, 2 * c:2 * c + 1])
                    act.activation(KEY[s][0:N3, OFF_D0 + a:OFF_D0 + a + 64], cum[:, a:a + 64], ACT.Exp,
                                   bias=negr[s][:, 2 * c:2 * c + 1])
                    last = act.activation(KEY[s][0:N3, OFF_D1 + a:OFF_D1 + a + P], cum[:, a:a + P], ACT.Exp,
                                          bias=negr[s][:, 2 * c + 1:2 * c + 2])
                last.then_inc(s_ex[s], 1)
                for j in range(2):
                    yield
                    act.wait_ge(s_y[s], s_y.at(s, j))
                    act.activation(BIG1[s][:, 2 + j, :], bank(s, j), ACT.Identity, scale=pr("normw", j))
                    act.activation(BIG1[s][:, 4 + j, :], bank(s, j), ACT.Square).then_inc(s_yt[s], 1)

            setup()
            act.wait_ge(known, 3)
            alike = act.value_load(flag[0:1, 0:1], min_val=0, max_val=1)

            with act.Fori(0, 4 // NS):
                own[0] = 0
                with act.If(alike == 0):
                    first_block_general(act, "act", state_space(True))
                own[0] = 0
                walk("act", [state_space(False), feed_forward, mamba, experts_gelu, attention, ternary, last_scan,
                      experts_silu])
                end_of_pair(act, "act")

        @block.vector
        def _(dve):
            own = [0]

            def step(ins):
                own[0] += 1
                ins.then_inc(dve_own, 1)
                dve.wait_ge(dve_own, own[0])

            def setup():
                for s in STREAMS:
                    dve.memset(XT[s][:, 0:PAD], 0.0)
                    dve.memset(UP[s][:, :, 0:PAD], 0.0)
                    dve.memset(KEY[s][:, :], 0.0)
                dve.memset(ones[:, :], 1.0)
                dve.memset(nhalf[:, :], -0.5).then_inc(setup_dve, 1)
                dve.memset(ones64[:, :], 1.0)
                dve.wait_ge(in_sem["a"], 16)
                rates = BIG1[1][:, 0, :].rearrange("p (b n) -> p n b", b=NB0)
                ends = BIG1[1][:, 1, 0:2 * N0]
                dve.tensor_reduce(ends[:, 0:N0], rates, AX.X, ALU.max)
                dve.tensor_reduce(ends[:, N0:2 * N0], rates, AX.X, ALU.min)
                dve.drain().then_inc(known, 1)
                dve.wait_ge(setup_pe, 1)
                dve.tensor_reduce(sc[0:N0, 10:11], bank(0, 0)[0:N0, 0:P], AX.X, ALU.max)
                dve.tensor_reduce(sc[0:N0, 11:12], bank(0, 1)[0:N0, 0:P], AX.X, ALU.min)
                dve.drain()
                dve.tensor_tensor(sc[0:N0, 12:13], sc[0:N0, 10:11], sc[0:N0, 11:12], ALU.is_equal)
                dve.wait_ge(setup_act, 4)
                dve.tensor_scalar(sc[0:N0, 13:14], sc[0:N0, 0:1], STEEPEST, None, ALU.is_le)
                dve.drain()
                dve.tensor_tensor(sc[0:N0, 14:15], sc[0:N0, 12:13], sc[0:N0, 13:14], ALU.mult)
                dve.drain().then_inc(known, 1)
                dve.wait_ge(setup_pe, 2)
                dve.tensor_scalar(factored[:, :], bank(0, 2)[:, 0:1], float(N0), None, ALU.is_equal)
                dve.drain()
                dve.tensor_copy(flag[:, :], factored[0:1, :])
                dve.drain().then_inc(known, 1)
                dve.wait_ge(in_sem["p"], 16)
                dve.wait_ge(setup_act, 4)
                dve.tensor_scalar(sc[0:N0, 16:17], sc[0:N0, 0:1], STEEPEST, factored[0:N0, 0:1], ALU.min, ALU.mult)
                dve.drain()
                dve.tensor_scalar(sc[0:N0, 1:2], sc[0:N0, 16:17], -1.0, None, ALU.mult)\
                    .then_inc(setup_dve, 1)
                dve.tensor_scalar(omu[:, 0:2], pr("mu_r", 0, 2), -1.0, 1.0, ALU.mult, ALU.add)
                dve.tensor_scalar(nega[:, :], nega[:, :], -1.0, None, ALU.mult).then_inc(setup_dve, 1)
                dve.wait_ge(setup_act, 5)
                dve.tensor_scalar(sc[:, 6:8], sc[:, 4:6], EPS6, None, ALU.add).then_inc(setup_dve, 1)
                dve.wait_ge(setup_dve, 4)
                dve.tensor_tensor(sc[:, 8:9], sc[:, 6:7], sc[:, 7:8], ALU.mult).then_inc(setup_dve, 1)
                dve.wait_ge(setup_dve, 5)
                dve.tensor_scalar(sc[:, 9:10], sc[:, 8:9], 8.0 ** 0.5, None, ALU.mult).then_inc(setup_dve, 1)
                dve.wait_ge(setup_dve, 6)
                dve.wait_ge(in_sem["c"], 32)
                dve.tensor_scalar(rden[:, :], cn("pos"), sc[:, 9:10], EPS6, ALU.mult, ALU.max).then_inc(setup_dve, 1)
                dve.wait_ge(setup_dve, 7)
                dve.tensor_copy(SM[:, :], cn("pick", 96))
                dve.reciprocal(rden[:, :], rden[:, :]).then_inc(setup_dve, 1)
                dve.wait_ge(setup_dve, 8)
                dve.wait_ge(in_sem["selr"], 16)
                dve.tensor_copy(SELR[:, :].rearrange("p (k n) -> p k n", k=4), BIG1[1][:, 4:8, :])
                dve.drain().then_inc(ready, 1)
                dve.wait_ge(ready, 2)

            def variance(s, parts, done, eps):
                for c in range(NC):
                    last = dve.bn_aggr(mv[s][:, c, :], stat[s][:, c, 0:parts, :].rearrange("p h k -> p (h k)"))
                step(last)
                dve.tensor_scalar(ve[s][:, :], mv[s][:, :, 1], eps, None, ALU.add).then_inc(done[s], 1)

            def norm(n, s, src, dst):
                for c in range(NC):
                    last = dve.bn_stats(stat[s][:, c, 0, :], src[s][:, c, :])
                step(last)
                variance(s, 1, n.var, LN_EPS)
                yield
                dve.wait_ge(n.rs[s], n.rs.at(s, 0))
                for c in range(NC):
                    last = dve.tensor_scalar(dst[s][:, c, :], src[s][:, c, :], mv[s][:, c, 0:1],
                                             rstd[s][:, c:c + 1], ALU.subtract, ALU.mult)
                last.then_inc(n.done[s], 1)

            def layer_norm(layer, s):
                yield
                if layer:
                    dve.wait_ge(x_done[layer - 1][s], x_done[layer - 1].at(s, 0))
                else:
                    dve.wait_ge(x_in[s], 16)
                yield from norm(norms[layer], s, X, XH)

            def conv(s, j, wcol, bcol):
                u, v = UP[s], CV[s]
                step(dve.tensor_scalar(v[:, j, :], u[:, j, PAD:PAD + T], pr(*wcol(3)), pr(*bcol), ALU.mult, ALU.add))
                step(dve.scalar_tensor_tensor(v[:, j, :], u[:, j, 2:2 + T], pr(*wcol(2)), v[:, j, :], ALU.mult, ALU.add))
                step(dve.scalar_tensor_tensor(v[:, j, :], u[:, j, 1:1 + T], pr(*wcol(1)), v[:, j, :], ALU.mult, ALU.add))
                return dve.scalar_tensor_tensor(v[:, j, :], u[:, j, 0:T], pr(*wcol(0)), v[:, j, :], ALU.mult, ALU.add)

            def masked_scores(s, ready_, done):
                for k in range(4):
                    n = T - k * P
                    yield
                    dve.wait_ge(ready_[s], ready_.at(s, k))
                    dve.tensor_tensor(MT[s][:, OFF_MT[k]:OFF_MT[k] + n], bank(s, k)[:, k * P:T], cn("tri")[:, 0:n],
                                      ALU.mult).then_inc(done[s], 1)

            def add_x(s, src, done=None):
                ins = dve.tensor_tensor(X[s][:, :, :], X[s][:, :, :], src, ALU.add)
                if done is None:
                    step(ins)
                else:
                    ins.then_inc(done[s], 1)

            def state_space(general):
                def conv_block(s, b):
                    yield
                    dve.wait_ge(l0_up[s], l0_up.at(s, b))
                    if b >= 2:
                        dve.wait_ge(l0_xt[s], l0_xt.at(s, b - 2))
                    conv(s, b % 2, lambda t: ("conv0_w", 4 * b + t), ("conv0_b", b)).then_inc(l0_cv[s], 1)

                def gate_y(s, h):
                    for c in range(NC):
                        yield
                        dve.wait_ge(l0_y[s], l0_y.at(s, 4 * h + c))
                        dve.wait_ge(l0_zs[s], l0_zs.at(s, 2 * c + h))
                        z = BIG1[s][:, 2 * c + h, :]
                        dve.tensor_tensor(z, bank(s, c), z, ALU.mult).then_inc(l0_yg[s], 1)

                def scan_general(s):
                    decay, rows, y, h = KEY[1], KEY[0], CV[s][:, 1, :], BIG2[s]
                    dve.sem_inc(l0_mt[s], 4)
                    dve.wait_ge(l0_xc[s], l0_xc.at(s, 7))
                    for j in range(NB0):
                        dve.wait_ge(l0_up[s], l0_up.at(s, j))
                        for t in (3, 2, 1, 0):
                            if t == 3:
                                dve.tensor_scalar(CV[s][:, 0, :], UP[s][:, 0, PAD:PAD + T], pr("conv0_w", 4 * j + 3),
                                                  pr("conv0_b", j), ALU.mult, ALU.add)
                            else:
                                dve.scalar_tensor_tensor(CV[s][:, 0, :], UP[s][:, 0, t:t + T], pr("conv0_w", 4 * j + t),
                                                         CV[s][:, 0, :], ALU.mult, ALU.add)
                            dve.drain()
                        dve.memset(y, 0.0)
                        dve.drain().then_inc(l0_cv[s], 1)
                        dve.wait_ge(l0_sl[s], l0_sl.at(s, j))
                        with dve.Fori(0, N0) as n:
                            dve.tensor_scalar(rows[0:N0, 0:T], BT[s][:, :], ident[0:N0, bass.ds(n, 1)], None, ALU.mult)
                            dve.tensor_scalar(rows[0:N0, T:2 * T], Q128[s][:, :], ident[0:N0, bass.ds(n, 1)], None, ALU.mult)
                            dve.drain().then_inc(g_row, 1)
                            dve.wait_ge(g_ps, n + ((s * NB0 + j) * N0 + 1))
                            dve.tensor_tensor(h[:, 0, :], CV[s][:, 0, :], bank(s, 1), ALU.mult)
                            dve.drain()
                            dve.tensor_tensor_scan(h[:, 1, :], decay[:, bass.ds(n + j * N0, 1)].broadcast_to([P, T]),
                                                   h[:, 0, :], 0.0, ALU.mult, ALU.add)
                            dve.drain()
                            dve.tensor_tensor(h[:, 2, :], h[:, 1, :], bank(s, 2), ALU.mult)
                            dve.drain()
                            dve.tensor_tensor(y, y, h[:, 2, :], ALU.add)
                            dve.drain()
                        dve.sem_inc(g_sum, 1)
                        dve.wait_ge(l0_y[s], l0_y.at(s, j))
                        for c in range(NC):
                            z = BIG1[s][:, 2 * c + j // 4, (j % 4) * P:(j % 4 + 1) * P]
                            dve.tensor_tensor(z, bank4(s, 3)[:, c, :], z, ALU.mult)
                        if j == NB0 - 1:
                            dve.memset(KEY[0][:, :], 0.0)
                            dve.memset(KEY[1][:, :], 0.0)
                        dve.drain().then_inc(l0_yg[s], 1)

                def layer(s):
                    yield from layer_norm(0, s)
                    yield
                    dve.wait_ge(l0_bc[s], l0_bc.at(s, 0))
                    for q, table in ((Q128, eq128), (Q64, eq64)):
                        dve.tensor_tensor(q[s][:, :].rearrange("p (c n) -> p c n", c=NC), bank4(s, 0)[N0:2 * N0],
                                          table[:, :].unsqueeze(1).broadcast_to([N0, NC, P]), ALU.mult)\
                            .then_inc(l0_q[s], 1)
                    if general:
                        scan_general(s)
                    else:
                        yield from masked_scores(s, l0_sc, l0_mt)
                        for b in range(8):
                            yield from conv_block(s, b)
                            if b == 4:
                                yield from gate_y(s, 0)
                        yield from gate_y(s, 1)
                    yield
                    dve.wait_ge(l0_yg[s], l0_yg.at(s, 7))
                    for c in range(NC):
                        for h in range(2):
                            last = dve.bn_stats(stat[s][:, c, h, :], BIG1[s][:, 2 * c + h, :])
                    step(last)
                    variance(s, 2, l0_var, LN_EPS)
                    yield
                    dve.wait_ge(l0_rs[s], l0_rs.at(s, 0))
                    for c in range(NC):
                        y = BIG1[s][:, 2 * c:2 * c + 2, :]
                        dve.tensor_scalar(y, y, mv[s][:, c, 0:1], rstd[s][:, c:c + 1], ALU.subtract, ALU.mult)\
                            .then_inc(l0_nm[s], 1)
                    for h in range(2):
                        yield
                        dve.wait_ge(l0_o[s], l0_o.at(s, h))
                        if general:
                            last = dve.tensor_tensor(X[s][:, :, :], X[s][:, :, :], bank4(s, 2 + h), ALU.add)
                        else:
                            last = dve.scalar_tensor_tensor(X[s][:, :, :], bank4(s, 2 + h), factored[:, 0:1], X[s][:, :, :],
                                                            ALU.mult, ALU.add)
                        if h == 0:
                            step(last)
                        else:
                            last.then_inc(x_done[0][s], 1)
                return layer

            def feed_forward(s):
                yield from layer_norm(1, s)
                yield
                dve.wait_ge(n1.xT[s], n1.xT.at(s, 0))
                now, prev, b = XT[s][:, PAD:PAD + T], XT[s][:, PAD - 1:PAD - 1 + T], BIG1[s]
                dve.tensor_scalar(b[:, 3, :], prev, omu[:, 1:2], None, ALU.mult)
                step(dve.tensor_scalar(b[:, 2, :], prev, omu[:, 0:1], None, ALU.mult))
                dve.scalar_tensor_tensor(b[:, 1, :], now, pr("mu_k"), b[:, 3, :], ALU.mult, ALU.add).then_inc(f0_mix[s], 1)
                dve.scalar_tensor_tensor(b[:, 0, :], now, pr("mu_r"), b[:, 2, :], ALU.mult, ALU.add).then_inc(f0_mix[s], 1)
                yield
                dve.wait_ge(f0_rl[s], f0_rl.at(s, 0))
                dve.tensor_tensor(b[:, 5, :], b[:, 4, :], b[:, 4, :], ALU.mult).then_inc(f0_ka[s], 1)
                yield
                dve.wait_ge(f0_p[s], f0_p.at(s, 2))
                dve.wait_ge(f0_sg[s], f0_sg.at(s, 0))
                step(dve.tensor_tensor(b[:, 7, :], bank(s, 2), b[:, 6, :], ALU.mult))
                add_x(s, b[:, 7, :].rearrange("p (c n) -> p c n", c=NC), x_done[1])

            def mamba(s):
                yield
                dve.wait_ge(x_done[1][s], x_done[1].at(s, 0))
                yield from norm(n2o, s, X, XN)
                yield
                dve.wait_ge(n2o.done[s], n2o.done.at(s, 0))
                yield from norm(n2, s, XN, XH)
                for j in range(2):
                    yield
                    dve.wait_ge(m_up[s], m_up.at(s, j))
                    conv(s, j, lambda t: ("conv1_w", 4 * j + t), ("conv1_b", j)).then_inc(m_cv[s], 1)
                yield
                dve.wait_ge(m_xd[s], m_xd.at(s, 0))
                bc, r = bank(s, 1), BIG2[s][:, 0, :]
                step(dve.tensor_copy(SPL[s][:, :], bc[0:96, :]))
                step(dve.tensor_tensor(r[0:96], bc[0:96, :], SPL[s][:, :], ALU.subtract))
                dve.tensor_copy(SPL[s][32:64, :], r[32:64])
                step(dve.tensor_copy(SPL[s][64:96, :], r[64:96]))
                step(dve.tensor_tensor(r[64:96], r[64:96], SPL[s][64:96, :], ALU.subtract))
                dve.tensor_copy(SPL[s][64:96, :], r[64:96]).then_inc(m_mix[s], 1)
                for j in range(2):
                    yield
                    dve.wait_ge(m_sp[s], m_sp.at(s, j))
                    step(dve.tensor_tensor(BIG1[s][:, j, :], CV[s][:, j, :], UP[s][:, j, PAD:PAD + T], ALU.add))
                    dve.tensor_tensor(BIG1[s][:, 2 + j, :], BIG1[s][:, j, :], BIG1[s][:, 4 + j, :], ALU.mult)\
                        .then_inc(m_mix[s], 1)
                for n in range(NM):
                    yield
                    dve.wait_ge(m_bs[s], m_bs.at(s, n))
                    dve.tensor_tensor(BIG2[s][:, 0, :], bank(s, 2), BIG1[s][:, 2, :], ALU.mult).then_inc(m_scan[s], 1)
                    yield
                    dve.wait_ge(m_scan[s], m_scan.at(s, 4 * n))
                    for j in range(2):
                        yield
                        dve.wait_ge(m_da[s], m_da.at(s, 2 * n + j))
                        if j:
                            dve.wait_ge(m_d1[s], m_d1.at(s, n))
                        dve.tensor_tensor_scan(UP[s][:, j, PAD:PAD + T], CV[s][:, j, :], BIG2[s][:, j, :], 0.0,
                                               ALU.mult, ALU.add).then_inc(m_scan[s], 1)
                    yield
                    dve.wait_ge(m_scan[s], m_scan.at(s, 4 * n + 2))
                    dve.wait_ge(m_bc[s], m_bc.at(s, 2 * n + 1))
                    if n:
                        dve.wait_ge(m_ya[s], m_ya.at(s, n - 1))
                    if n > 1:
                        dve.wait_ge(m_acc[s], m_acc.at(s, n - 2))
                    if n:
                        dve.tensor_tensor(BIG2[s][:, 2:4, :], UP[s][:, :, PAD:PAD + T],
                                          bank(s, 3).unsqueeze(1).broadcast_to([P, 2, T]), ALU.mult).then_inc(m_scan[s], 1)
                    else:
                        dve.tensor_tensor(MT[s][:, T:2 * T], UP[s][:, 1, PAD:PAD + T], bank(s, 3), ALU.mult)
                        dve.tensor_tensor(BIG2[s][:, 2, :], UP[s][:, 0, PAD:PAD + T], bank(s, 3), ALU.mult)\
                            .then_inc(m_scan[s], 1)
                yield
                dve.wait_ge(m_ya[s], m_ya.at(s, NM - 1))
                dve.wait_ge(m_acc[s], m_acc.at(s, NM - 2))
                for j in range(2):
                    summed = MT[s][:, T:2 * T] if j else bank(s, 0)
                    step(dve.scalar_tensor_tensor(BIG2[s][:, j, :], BIG1[s][:, 4 + j, :], pr("dm", j), summed,
                                                  ALU.mult, ALU.add))
                    dve.tensor_tensor(BIG2[s][:, j, :], BIG2[s][:, j, :], BIG1[s][:, 6 + j, :], ALU.mult)\
                        .then_inc(m_mix[s], 1)
                add_x(s, XN[s][:, :, :])
                yield
                dve.wait_ge(m_o[s], m_o.at(s, 0))
                add_x(s, bank4(s, 2), x_done[2])

            def route(m, s):
                g = moe[m]
                yield
                dve.wait_ge(g.lg[s], g.lg.at(s, 0))
                lgp = bank(s, 3)[:, 0:NC * NE].rearrange("p (c e) -> p c e", c=NC)
                step(dve.tensor_reduce(sm4[s][:, 0, :], lgp, AX.X, ALU.max))
                dve.tensor_tensor(lg[s][:, 0], lgp, sm4[s][:, 0, :].unsqueeze(2).broadcast_to([P, NC, NE]),
                                  ALU.subtract).then_inc(g.sh[s], 1)
                yield
                dve.wait_ge(g.ex[s], g.ex.at(s, 0))
                step(dve.tensor_reduce(sm4[s][:, 1, :], lg[s][:, 1], AX.X, ALU.add))
                step(dve.reciprocal(sm4[s][:, 2, :], sm4[s][:, 1, :]))
                step(dve.tensor_tensor(lg[s][:, 2], lg[s][:, 1],
                                       sm4[s][:, 2, :].unsqueeze(2).broadcast_to([P, NC, NE]), ALU.mult))
                for c in range(NC):
                    last = dve.max(top[s][:, c, :], lg[s][:, 2, c, :])
                step(last)
                for c in range(NC):
                    last = dve.max_index(topi[s][:, c, :], top[s][:, c, :], lg[s][:, 2, c, :])
                step(last)
                if m:
                    step(dve.tensor_tensor(sm4[s][:, 0, :], top[s][:, :, 0], top[s][:, :, 1], ALU.add))
                    step(dve.reciprocal(sm4[s][:, 3, :], sm4[s][:, 0, :]))
                    step(dve.tensor_tensor(top[s][:, :, 0:2], top[s][:, :, 0:2],
                                           sm4[s][:, 3, :].unsqueeze(2).broadcast_to([P, NC, 2]), ALU.mult))
                step(dve.tensor_copy(topf[s][:, :, :], topi[s][:, :, :]))
                for c in range(NC):
                    for r in range(2):
                        last = dve.tensor_scalar(lg[s][:, r, c, :], cn("iota8"), topf[s][:, c, r:r + 1],
                                                 top[s][:, c, r:r + 1], ALU.is_equal, ALU.mult)
                step(last)
                dve.tensor_tensor(cmb[s][:, :, :], lg[s][:, 0], lg[s][:, 1], ALU.add).then_inc(g.cb[s], 1)
                yield
                dve.wait_ge(g.b[s], g.b.at(s, 0))
                add_x(s, bank4(s, 3), g.bx)

            def gated_sum(m, s, e):
                g = moe[m]
                yield
                dve.wait_ge(g.dn[s], g.dn.at(s, e))
                if e:
                    dve.wait_ge(g.x[s], g.x.at(s, e - 1))
                else:
                    dve.wait_ge(g.bx[s], g.bx.at(s, 0))
                for c in range(NC):
                    last = dve.scalar_tensor_tensor(X[s][:, c, :], bank4(s, 3)[:, c, :], cmb[s][:, c, e:e + 1],
                                                    X[s][:, c, :], ALU.mult, ALU.add)
                last.then_inc(g.x[s] if e < NE - 1 else x_done[7 if m else 3][s], 1)

            def experts_gelu(s):
                yield from layer_norm(3, s)
                yield from route(0, s)
                for e in range(NE):
                    if e:
                        yield from gated_sum(0, s, e - 1)
                yield from gated_sum(0, s, NE - 1)

            def experts_silu(s):
                g = moe[1]
                yield from layer_norm(7, s)
                yield from route(1, s)
                for e in range(NE):
                    for k in range(4):
                        yield
                        dve.wait_ge(g.up[s], g.up.at(s, 8 * e + 2 * k + 1))
                        dve.wait_ge(g.act[s], g.act.at(s, 4 * e + k))
                        if k == 0 and e >= 2:
                            dve.wait_ge(g.dn[s], g.dn.at(s, e - 2))
                        dve.scalar_tensor_tensor(BIG1[s][:, 4 * (e % 2) + k, :], bank(s, (8 * e + 2 * k + 1) % 3),
                                                 pr("bu", 4 * e + k), CV[s][:, k % 2, :], ALU.add, ALU.mult)\
                            .then_inc(g.h[s], 1)
                    if e:
                        yield from gated_sum(1, s, e - 1)
                yield from gated_sum(1, s, NE - 1)

            def attention(s):
                yield from layer_norm(4, s)
                for k in range(3):
                    yield
                    dve.wait_ge(a_p[s], a_p.at(s, k))
                    if k == 2:
                        dve.tensor_copy(BIG1[s][:, k, :], bank(s, k)).then_inc(a_f[s], 1)
                    else:
                        dve.tensor_scalar(BIG1[s][:, k, :], bank(s, k), 0.0, EPS6, ALU.max, ALU.add).then_inc(a_f[s], 1)
                for k in range(3):
                    yield
                    dve.wait_ge(a_hi[s], a_hi.at(s, k))
                    dve.tensor_tensor(PARTS[:, 1, k, :], BIG1[s][:, k, :], PARTS[:, 0, k, :].bitcast(F32),
                                      ALU.subtract).then_inc(a_lo[s], 1)
                for b in range(NB0):
                    yield
                    dve.wait_ge(a_ks[s], a_ks.at(s, b))
                    dve.wait_ge(a_r[s], a_r.at(s, 3 * b + 1))
                    dve.tensor_tensor(CV[s][:, 1, :], bank(s, 1), CV[s][:, 0, :], ALU.mult).then_inc(a_kv[s], 1)
                    yield
                    dve.wait_ge(a_kv[s], a_kv.at(s, b))
                    dve.tensor_tensor_scan(UP[s][:, 0, PAD:PAD + T], ones[:, 0:1].broadcast_to([P, T]), CV[s][:, 1, :],
                                           0.0, ALU.mult, ALU.add).then_inc(a_cum[s], 1)
                    yield
                    dve.wait_ge(a_cum[s], a_cum.at(s, b))
                    dve.wait_ge(a_r[s], a_r.at(s, 3 * b + 2))
                    if b:
                        dve.wait_ge(a_red[s], a_red.at(s, b - 1))
                    dve.tensor_tensor(UP[s][:, 1, PAD:PAD + T], bank(s, 2), UP[s][:, 0, PAD:PAD + T], ALU.mult)\
                        .then_inc(a_qk[s], 1)
                yield
                dve.wait_ge(a_red[s], a_red.at(s, NB0 - 1))
                dve.tensor_tensor(BIG2[s][:, 0, :], bank(s, 3), rden[:, :], ALU.mult).then_inc(a_o[s], 1)
                yield
                dve.wait_ge(a_y[s], a_y.at(s, 0))
                add_x(s, bank4(s, 0), x_done[4])

            def ternary(s):
                yield from layer_norm(5, s)
                for j in range(4):
                    yield
                    dve.wait_ge(t_ab[s], t_ab.at(s, 2 * j + 1))
                    dve.wait_ge(t_sa[s], t_sa.at(s, j))
                    dve.scalar_tensor_tensor(BIG1[s][:, j, :], bank(s, 2 + j % 2), pr("w2_s", j), CV[s][:, j % 2, :],
                                             ALU.mult, ALU.mult).then_inc(t_h0[s], 1)
                yield
                dve.wait_ge(t_o[s], t_o.at(s, 0))
                step(dve.tensor_tensor(XH[s], bank4(s, 0), pr("w3_s", 0, P).unsqueeze(1).broadcast_to([P, NC, P]), ALU.mult))
                add_x(s, XH[s], x_done[5])

            def last_scan(s):
                yield from layer_norm(6, s)
                for j in range(2):
                    yield
                    dve.wait_ge(s_slg[s], s_slg.at(s, 2 + j))
                    dve.tensor_tensor(BIG1[s][:, j, :], CV[s][:, j, :], UP[s][:, j, PAD:PAD + T], ALU.mult)\
                        .then_inc(s_xi[s], 1)
                yield
                dve.wait_ge(s_abc[s], s_abc.at(s, 0))
                dve.tensor_scalar(BT[s][0:N3, :], bank(s, 0)[0:N3, :], -5.0, 0.0, ALU.max, ALU.min).then_inc(s_cl[s], 1)
                yield
                dve.wait_ge(s_ea[s], s_ea.at(s, 0))
                cum = BT[s][0:N3, :]
                step(dve.tensor_tensor_scan(Q128[s][0:N3, :], ones[0:N3, 0:1].broadcast_to([N3, T]), cum, 0.0,
                                            ALU.mult, ALU.add))
                dve.tensor_copy(cum, Q128[s][0:N3, :])
                dve.tensor_scalar(negr[s][:, :], Q128[s][0:N3, 0:T:64], -1.0, None, ALU.mult).then_inc(s_cl[s], 1)
                yield
                dve.wait_ge(s_ex[s], s_ex.at(s, 0))
                q4 = Q64[s][0:N3, :].rearrange("p (c n) -> p c n", c=NC)[:, :, 64:P]
                dve.tensor_tensor(Q128[s][0:N3, :], bank(s, 0)[64:64 + N3, :], Q128[s][0:N3, :], ALU.mult)
                dve.tensor_tensor(q4, bank4(s, 0)[64:64 + N3, :, 64:P], q4, ALU.mult)
                for c in range(1, NC):
                    r = KEY[s][0:N3, OFF_RECT[c]:OFF_RECT[c] + c * P]
                    dve.tensor_tensor(r, bank(s, 0)[32:32 + N3, 0:c * P], r, ALU.mult)
                k0 = KEY[s][0:N3, OFF_D0:OFF_D0 + T].rearrange("p (c n) -> p c n", c=NC)[:, :, 0:64]
                k1 = KEY[s][0:N3, OFF_D1:OFF_D1 + T]
                dve.tensor_tensor(k0, bank4(s, 0)[32:32 + N3, :, 0:64], k0, ALU.mult)
                dve.tensor_tensor(k1, bank(s, 0)[32:32 + N3, :], k1, ALU.mult).then_inc(s_f[s], 1)
                yield from masked_scores(s, s_sc, s_mt)
                yield
                dve.wait_ge(s_o[s], s_o.at(s, 0))
                dve.tensor_scalar(ve[s][:, :], bank(s, 3)[:, 0:NC], 1.0 / 256, RMS_EPS, ALU.mult, ALU.add)\
                    .then_inc(s_var[s], 1)
                yield
                dve.wait_ge(s_rs[s], s_rs.at(s, 0))
                dve.wait_ge(s_o[s], s_o.at(s, 1))
                for c in range(NC):
                    last = dve.scalar_tensor_tensor(X[s][:, c, :], bank4(s, 2)[:, c, :], rstd[s][:, c:c + 1],
                                                    X[s][:, c, :], ALU.mult, ALU.add)
                last.then_inc(x_done[6][s], 1)

            setup()
            alike = dve.value_load(flag[0:1, 0:1], min_val=0, max_val=1)

            with dve.Fori(0, 4 // NS):
                own[0] = 0
                with dve.If(alike == 0):
                    first_block_general(dve, "dve", state_space(True))
                own[0] = 0
                walk("dve", [state_space(False), feed_forward, mamba, experts_gelu, attention, ternary, last_scan,
                      experts_silu])
                end_of_pair(dve, "dve")

        @block.tensor
        def _(pe):
            def turn(n, s):
                yield
                pe.wait_ge(n.done[s], n.done.at(s, 0))
                for c in range(NC):
                    last = pe.transpose(bank(s, 3)[:, c * P:(c + 1) * P], XH[s][:, c, :], ident)
                last.then_inc(n.T[s], 1)
                yield
                pe.wait_ge(n.xT[s], n.xT.at(s, 0))

            def by_token(s, k, lhs, rhs, blocks):
                for c in range(NC):
                    for b in range(blocks):
                        last = pe.matmul(bank4(s, k)[:, c, :], lhs(b, c), rhs(b), start=(b == 0), stop=(b == blocks - 1))
                return last

            def scores(s, n, done):
                for k in range(NC):
                    b = bank(s, k)
                    a = k * P
                    pe.matmul(b[:, a:a + 64], KEY[s][0:n, OFF_D0 + a:OFF_D0 + a + P], Q128[s][0:n, a:a + 64],
                              start=True, stop=True)
                    last = pe.matmul(b[:, a + 64:a + P], KEY[s][0:n, OFF_D1 + a:OFF_D1 + a + P],
                                     Q64[s][0:n, a + 64:a + P], start=True, stop=True)
                    for c in range(k + 1, NC):
                        last = pe.matmul(b[:, c * P:(c + 1) * P], KEY[s][0:n, OFF_RECT[c] + a:OFF_RECT[c] + a + P],
                                         Q128[s][0:n, c * P:(c + 1) * P], start=True, stop=True)
                    last.then_inc(done[s], 1)

            def state_space(general):
                win = lambda j: w("l0_in", j * P, P)

                def conv_block(s, b):
                    yield
                    if b < 8:
                        if b < 2:
                            pe.wait_ge(l0_mt[s], l0_mt.at(s, b))
                        elif b == 5 or b == 6:
                            pe.wait_ge(l0_yg[s], l0_yg.at(s, b % 2))
                        else:
                            pe.wait_ge(l0_up[s], l0_up.at(s, b - 2))
                        pe.matmul(bank(s, b % 2), win(b), XT[s][:, PAD:PAD + T], start=True, stop=True)\
                            .then_inc(l0_u[s], 1)
                    if b >= 1:
                        j = b - 1
                        yield
                        pe.wait_ge(l0_sl[s], l0_sl.at(s, j))
                        if j < 2:
                            pe.wait_ge(l0_mt[s], l0_mt.at(s, 2 + j))
                        elif j == 4 or j == 5:
                            pe.wait_ge(l0_yg[s], l0_yg.at(s, 2 + j % 2))
                        else:
                            pe.wait_ge(l0_xc[s], l0_xc.at(s, j - 2))
                        for c in range(NC):
                            last = pe.transpose(bank4(s, 2 + j % 2)[:, c, :], CV[s][:, j % 2, c * P:(c + 1) * P], ident)
                        last.then_inc(l0_xt[s], 1)

                def scan(s, h):
                    yield
                    pe.wait_ge(l0_xc[s], l0_xc.at(s, 4 * h + 3))
                    pe.wait_ge(l0_up[s], l0_up.at(s, 4 if h == 0 else 7))
                    for c in range(NC):
                        for k in range(c + 1):
                            m = OFF_MT[k] + (c - k) * P
                            last = pe.matmul(bank(s, c), MT[s][:, m:m + P], BIG2[s][:, k, :],
                                             start=(k == 0), stop=(k == c))
                        last.then_inc(l0_y[s], 1)

                def products_general(s):
                    pe.matmul(bank(s, 1)[0:N0, :], w("l0_in", 16 * P + N0, N0), XT[s][:, PAD:PAD + T],
                              start=True, stop=True).then_inc(l0_sc[s], 4)
                    pe.sem_inc(l0_xt[s], 8)
                    for j in range(NB0):
                        pe.matmul(bank(s, 0), win(j), XT[s][:, PAD:PAD + T], start=True, stop=True).then_inc(l0_u[s], 1)
                        with pe.Fori(0, N0) as n:
                            pe.wait_ge(g_row, n + ((s * NB0 + j) * N0 + 1))
                            for k in range(2):
                                last = pe.matmul(bank(s, 1 + k), ones64[:, :], KEY[0][0:N0, k * T:(k + 1) * T],
                                                 start=True, stop=True)
                            last.then_inc(g_ps, 1)
                        pe.wait_ge(g_sum, s * NB0 + j + 1)
                        if j:
                            pe.wait_ge(l0_yg[s], l0_yg.at(s, j - 1))
                        for c in range(NC):
                            last = pe.transpose(bank4(s, 3)[:, c, :], CV[s][:, 1, c * P:(c + 1) * P], ident)
                        last.then_inc(l0_y[s], 1)

                def turn_block(s, j):
                    yield
                    if j >= 2:
                        pe.wait_ge(l0_yn[s], l0_yn.at(s, j - 2))
                    for c in range(NC):
                        yield
                        if j == 0:
                            pe.wait_ge(l0_nm[s], l0_nm.at(s, c))
                        last = pe.transpose(bank4(s, j % 2)[:, c, :],
                                            BIG1[s][:, 2 * c + j // 4, (j % 4) * P:(j % 4 + 1) * P], ident)
                    last.then_inc(l0_yt[s], 1)

                def out(s, h):
                    yield
                    pe.wait_ge(l0_yn[s], l0_yn.at(s, 4 * h + 3))
                    by_token(s, 2 + h, lambda b, c: BIG2[s][:, b, c * P:(c + 1) * P],
                             lambda b: w("l0_out", (4 * h + b) * P, P), 4).then_inc(l0_o[s], 1)

                def layer(s):
                    yield from turn(n0, s)
                    pe.matmul(bank(s, 0), w("l0_in", 16 * P, 2 * N0), XT[s][:, PAD:PAD + T], start=True, stop=True)\
                        .then_inc(l0_bc[s], 1)
                    for k in range(8):
                        c, h = k // 2, k % 2
                        yield
                        if k == 0:
                            pe.wait_ge(l0_bt[s], l0_bt.at(s, 0))
                            pe.wait_ge(l0_q[s], l0_q.at(s, 1))
                        elif k >= 4:
                            pe.wait_ge(l0_zs[s], l0_zs.at(s, k - 4))
                        pe.matmul(bank(s, k % 4), chunk(s, c), w("l0_in", DI + h * T, T), start=True, stop=True)\
                            .then_inc(l0_z[s], 1)
                    yield
                    pe.wait_ge(l0_zs[s], l0_zs.at(s, 7))
                    if general:
                        products_general(s)
                    else:
                        yield
                        pe.wait_ge(l0_key[s], l0_key.at(s, 0))
                        scores(s, N0, l0_sc)
                        for b in range(9):
                            yield from conv_block(s, b)
                            if b == 4:
                                yield from scan(s, 0)
                        yield from scan(s, 1)
                    yield from turn_block(s, 0)
                    for j in range(1, 8):
                        yield from turn_block(s, j)
                        if j == 4:
                            yield from out(s, 0)
                    yield from out(s, 1)
                return layer

            def feed_forward(s):
                yield from turn(n1, s)
                pe.wait_ge(wsem[1], 16)
                yield
                pe.wait_ge(f0_mix[s], f0_mix.at(s, 0))
                pe.matmul(bank(s, 0), w("f0_k"), BIG1[s][:, 1, :], start=True, stop=True).then_inc(f0_p[s], 1)
                yield
                pe.wait_ge(f0_mix[s], f0_mix.at(s, 1))
                by_token(s, 1, lambda b, c: BIG1[s][:, 0, c * P:(c + 1) * P], lambda b: w("f0_r"), 1)\
                    .then_inc(f0_p[s], 1)
                yield
                pe.wait_ge(f0_ka[s], f0_ka.at(s, 0))
                by_token(s, 2, lambda b, c: BIG1[s][:, 5, c * P:(c + 1) * P], lambda b: w("f0_v"), 1)\
                    .then_inc(f0_p[s], 1)

            def mamba(s):
                yield from turn(n2, s)
                for j in range(4):
                    pe.matmul(bank(s, j), w("m_in", j * P, P), XT[s][:, PAD:PAD + T], start=True, stop=True)\
                        .then_inc(m_uz[s], 1)
                for j in range(2):
                    yield
                    pe.wait_ge(m_uz_s[s], m_uz_s.at(s, 2 + j))
                    last = pe.matmul(bank(s, 1)[0:104, :], w("m_x", j * 104, 104), BIG1[s][:, 4 + j, :],
                                     start=(j == 0), stop=(j == 1))
                last.then_inc(m_xd[s], 1)
                yield
                pe.wait_ge(in_sem["r8"], 16)
                pe.wait_ge(m_d8[s], m_d8.at(s, 0))
                for j in range(2):
                    pe.matmul(bank(s, 2 + j), R8[:, 2 * P + j * P:2 * P + (j + 1) * P], BT[s][0:8, :],
                              start=True, stop=True).then_inc(m_dt[s], 1)

                def sum_states(n):
                    yield
                    pe.wait_ge(m_scan[s], m_scan.at(s, 4 * n + 3))
                    pe.matmul(bank(s, 0), ident, BIG2[s][:, 2, :], start=(n == 0), stop=(n == NM - 1))\
                        .then_inc(m_ya[s], 1)

                for n in range(NM):
                    yield
                    if n == 0:
                        pe.wait_ge(m_mix[s], m_mix.at(s, 0))
                        pe.wait_ge(m_sp[s], m_sp.at(s, 1))
                    for k in range(2):
                        yield
                        if n and k == 0:
                            pe.wait_ge(m_scan[s], m_scan.at(s, 4 * n - 4))
                            pe.wait_ge(m_bs[s], m_bs.at(s, n - 1))
                        elif n:
                            pe.wait_ge(m_scan[s], m_scan.at(s, 4 * n - 1))
                        r = 16 * k + n
                        pe.matmul(bank(s, 2 + k), SM[:, r:r + 1].broadcast_to([96, P]), SPL[s][:, :],
                                  start=True, stop=True).then_inc(m_bc[s], 1)
                    if n:
                        yield from sum_states(n - 1)
                yield from sum_states(NM - 1)
                yield
                pe.wait_ge(m_mix[s], m_mix.at(s, 4))
                by_token(s, 2, lambda b, c: BIG2[s][:, b, c * P:(c + 1) * P], lambda b: w("m_out", b * P, P), 2)\
                    .then_inc(m_o[s], 1)

            def route(m, name, s):
                g = moe[m]
                for c in range(NC):
                    last = pe.matmul(bank(s, 3)[:, c * NE:(c + 1) * NE], chunk(s, c), w(name), start=True, stop=True)
                last.then_inc(g.lg[s], 1)
                yield
                pe.wait_ge(g.cb[s], g.cb.at(s, 0))
                for c in range(NC):
                    last = pe.transpose(bank(s, 3)[0:NE, c * P:(c + 1) * P], cmb[s][:, c, :], ident)
                last.then_inc(g.ct[s], 1)
                yield
                pe.wait_ge(g.cs[s], g.cs.at(s, 0))
                by_token(s, 3, lambda b, c: cmbT[s][:, c * P:(c + 1) * P], lambda b: R8[:, m * P:(m + 1) * P], 1)\
                    .then_inc(g.b[s], 1)

            loads = expert_loads()

            def loaded(m, s, e):
                q = loads.index((m, s, e))
                yield
                pe.wait_ge(ring_in[q % RING], 16 * (q // RING + 1))
                return q % RING

            def down(m, s, e):
                g = moe[m]
                slot = loads.index((m, s, e)) % RING
                wd = ring[:, slot, 512 * (m + 1):512 * (m + 2)]
                yield
                if e == 0:
                    pe.wait_ge(g.bx[s], g.bx.at(s, 0))
                else:
                    pe.wait_ge(g.x[s], g.x.at(s, e - 1))
                hidden = g.h if m else g.act
                yield
                pe.wait_ge(hidden[s], hidden.at(s, 4 * e + 3))
                by_token(s, 3, lambda b, c: BIG1[s][:, 4 * (e % 2) + b, c * P:(c + 1) * P],
                         lambda b: wd[:, b * P:(b + 1) * P], 4).then_inc(g.dn[s], 1)

            def experts_gelu(s):
                g = moe[0]
                yield from turn(g.n, s)
                yield from route(0, "r1", s)
                for e in range(NE):
                    slot = yield from loaded(0, s, e)
                    for k in range(4):
                        yield
                        if k == 3:
                            pe.wait_ge(g.act[s], g.act.at(s, 4 * e))
                        elif e:
                            pe.wait_ge(g.act[s], g.act.at(s, 4 * e - 1 if k == 0 else 4 * e - 4 + k))
                        pe.matmul(bank(s, k % 3), ring[:, slot, k * P:(k + 1) * P], XT[s][:, PAD:PAD + T],
                                  start=True, stop=True).then_inc(g.up[s], 1)
                    if e:
                        yield from down(0, s, e - 1)
                yield from down(0, s, NE - 1)

            def experts_silu(s):
                g = moe[1]
                yield from turn(g.n, s)
                yield from route(1, "r3", s)
                for e in range(NE):
                    slot = yield from loaded(1, s, e)
                    for k in range(4):
                        for r in range(2):
                            b = 8 * e + 2 * k + r
                            yield
                            if b >= 3:
                                free = g.h if (b - 3) % 2 else g.act
                                pe.wait_ge(free[s], free.at(s, (b - 3) // 2))
                            pe.matmul(bank(s, b % 3), ring[:, slot, r * T + k * P:r * T + (k + 1) * P],
                                      XT[s][:, PAD:PAD + T], start=True, stop=True).then_inc(g.up[s], 1)
                    if e:
                        yield from down(1, s, e - 1)
                yield from down(1, s, NE - 1)

            def attention(s):
                yield from turn(n4, s)
                pe.wait_ge(wsem[2], 16)
                pe.wait_ge(in_sem["sel"], 16)
                for k in range(3):
                    pe.matmul(bank(s, k), w("a_qkv", k * P, P), XT[s][:, PAD:PAD + T], start=True, stop=True)\
                        .then_inc(a_p[s], 1)

                def reduce(b):
                    yield
                    pe.wait_ge(a_qk[s], a_qk.at(s, b))
                    pe.matmul(bank(s, 3), SEL[:, b * P:(b + 1) * P], UP[s][:, 1, PAD:PAD + T], start=(b == 0),
                              stop=(b == NB0 - 1)).then_inc(a_red[s], 1)

                for b in range(NB0):
                    for k, (src, m, free) in enumerate(((1, b, a_ks), (2, NB0 + b, a_kv), (0, b, a_qk))):
                        yield
                        if b:
                            pe.wait_ge(free[s], free.at(s, b - 1))
                        else:
                            pe.wait_ge(a_lo[s], a_lo.at(s, 2))
                        for part in range(2):
                            last = pe.matmul(bank(s, k), SELR[:, m * P:(m + 1) * P], PARTS[:, part, src, :],
                                             start=(part == 0), stop=(part == 1))
                        last.then_inc(a_r[s], 1)
                    if b:
                        yield from reduce(b - 1)
                yield from reduce(NB0 - 1)
                yield
                pe.wait_ge(a_o[s], a_o.at(s, 0))
                by_token(s, 0, lambda b, c: BIG2[s][:, 0, c * P:(c + 1) * P], lambda b: w("a_out"), 1)\
                    .then_inc(a_y[s], 1)

            def ternary(s):
                yield from turn(n5, s)
                for j in range(4):
                    for r, name in enumerate(("t_w1", "t_w2")):
                        yield
                        if j >= 2:
                            free = t_h0 if r else t_sa
                            pe.wait_ge(free[s], free.at(s, j - 2))
                        pe.matmul(bank(s, 2 * r + j % 2), w(name, j * P, P), XT[s][:, PAD:PAD + T],
                                  start=True, stop=True).then_inc(t_ab[s], 1)
                for name, p, src in (("t_h1", t_p1, 0), ("t_h2", t_p2, 4)):
                    yield
                    if src == 0:
                        pe.wait_ge(t_h0[s], t_h0.at(s, 3))
                    for j in range(4):
                        for b in range(4):
                            yield
                            if src:
                                pe.wait_ge(t_g1[s], t_g1.at(s, max(b, j)))
                            last = pe.matmul(bank(s, j), w(name, (4 * b + j) * P, P), BIG1[s][:, src + b, :],
                                             start=(b == 0), stop=(b == 3))
                        last.then_inc(p[s], 1)
                yield
                pe.wait_ge(t_g2[s], t_g2.at(s, 3))
                by_token(s, 0, lambda b, c: BIG1[s][:, b, c * P:(c + 1) * P], lambda b: w("t_w3", b * P, P), 4)\
                    .then_inc(t_o[s], 1)

            def last_scan(s):
                yield from turn(n6, s)
                pe.wait_ge(wsem[3], 16)
                for j in range(4):
                    pe.matmul(bank(s, j), w("s_in", j * P, P), XT[s][:, PAD:PAD + T], start=True, stop=True)\
                        .then_inc(s_ab[s], 1)
                yield
                pe.wait_ge(s_xi[s], s_xi.at(s, 1))
                for j in range(2):
                    last = pe.matmul(bank(s, 0)[0:96, :], w("s_abc", j * 96, 96), BIG1[s][:, j, :],
                                     start=(j == 0), stop=(j == 1))
                last.then_inc(s_abc[s], 1)
                for j in range(2):
                    yield
                    if j:
                        pe.wait_ge(s_xs[s], s_xs.at(s, 0))
                    for c in range(2):
                        for b in range(2):
                            last = pe.transpose(bank4(s, 3)[:, 2 * c + b, :],
                                                BIG1[s][:, b, (2 * j + c) * P:(2 * j + c + 1) * P], ident)
                    last.then_inc(s_xt[s], 1)
                yield
                pe.wait_ge(s_f[s], s_f.at(s, 0))
                pe.wait_ge(s_xs[s], s_xs.at(s, 1))
                scores(s, N3, s_sc)
                yield
                pe.wait_ge(s_mt[s], s_mt.at(s, 3))
                for j in range(2):
                    for k in range(NC):
                        last = pe.matmul(bank(s, j)[:, k * P:T], BIG2[s][:, k, j * P:(j + 1) * P],
                                         MT[s][:, OFF_MT[k]:OFF_MT[k] + T - k * P], start=(k == 0), stop=(k == NC - 1))
                    last.then_inc(s_y[s], 1)
                yield
                pe.wait_ge(s_yt[s], s_yt.at(s, 1))
                for c in range(NC):
                    for j in range(2):
                        last = pe.matmul(bank(s, 3)[:, c:c + 1], BIG1[s][:, 4 + j, c * P:(c + 1) * P], ones[:, 0:1],
                                         start=(j == 0), stop=(j == 1))
                last.then_inc(s_o[s], 1)
                by_token(s, 2, lambda b, c: BIG1[s][:, 2 + b, c * P:(c + 1) * P], lambda b: w("s_out", b * P, P), 2)\
                    .then_inc(s_o[s], 1)

            pe.wait_ge(in_sem["c"], 32)
            pe.wait_ge(known, 1)
            for k in range(2):
                last = pe.transpose(bank(0, k)[0:N0, 0:P], BIG1[1][:, 1, k * N0:(k + 1) * N0], ident)
            last.then_inc(setup_pe, 1)
            pe.wait_ge(known, 2)
            pe.matmul(bank(0, 2)[:, 0:1], ones64[:, :], sc[0:N0, 14:15], start=True, stop=True).then_inc(setup_pe, 1)
            pe.wait_ge(known, 3)
            pe.wait_ge(ready, 2)
            pe.wait_ge(wsem[0], 16)
            alike = pe.value_load(flag[0:1, 0:1], min_val=0, max_val=1)

            with pe.Fori(0, 4 // NS):
                with pe.If(alike == 0):
                    first_block_general(pe, "pe", state_space(True))
                walk("pe", [state_space(False), feed_forward, mamba, experts_gelu, attention, ternary, last_scan,
                      experts_silu])
                end_of_pair(pe, "pe")


def layout(i):
    import numpy as np

    f = {k: np.asarray(v) for k, v in i.items()}
    blocks = lambda a: np.concatenate([a[k * P:(k + 1) * P] for k in range(a.shape[0] // P)], 1)
    cols = lambda v: np.ascontiguousarray(v.reshape(-1, P).T)
    wx = f["L1_attn_W_xproj"]
    bc = wx[:, 8:40]
    t4 = lambda a: blocks(a.T)
    gap = np.zeros((2 * P, 16), np.float32)
    hk = {
        "l0_in": f["L0_attn_in_proj_w"].T,
        "l0_out": blocks(f["L0_attn_out_proj_w"].T),
        "f0_r": f["L0_ffn_W_r"].T, "f0_k": f["L0_ffn_W_k"].T, "f0_v": f["L0_ffn_W_v"].T,
        "m_in": f["L1_attn_W_in"], 
        "m_x": blocks(np.concatenate([bc, bc, bc, wx[:, 0:8]], 1)), "m_out": blocks(f["L1_attn_W_out"]),
        "r1": f["L1_ffn_Wr"].T, "a_qkv": f["L2_attn_qkv_w"].T, "a_out": f["L2_attn_proj_w"].T,
        "t_w1": f["L2_ffn_w1_w"].T, "t_w2": f["L2_ffn_w2_w"].T, "t_h1": t4(f["L2_ffn_h1_w"]),
        "t_h2": t4(f["L2_ffn_h2_w"]), "t_w3": t4(f["L2_ffn_w3_w"]), "s_in": f["L3_attn_W_in"],
        "s_abc": blocks(np.concatenate([x for k in "ABC" for x in (f["L3_attn_W_" + k], gap)], 1)),
        "s_out": blocks(f["L3_attn_W_out"]), "r3": f["L3_ffn_Wg"],
    }
    wts = np.concatenate([hk[k] for k, _ in WCOLS], 1)
    tap = lambda a: a[:, 0, :].reshape(-1, P, 4).transpose(1, 0, 2).reshape(P, -1)
    e4 = lambda a: a.reshape(NE, 4, P).transpose(2, 0, 1).reshape(P, 32)
    a0 = f["L0_attn_A_param"][0, 0]
    pk = {
        "conv0_w": tap(f["L0_attn_conv_w"]), "conv0_b": cols(f["L0_attn_conv_b"]), "lnw": cols(f["L0_attn_ln_w"]),
        "lnb": cols(f["L0_attn_ln_b"]), "mu_r": cols(f["L0_ffn_mu_r"]), "mu_k": cols(f["L0_ffn_mu_k"]),
        "g1": cols(f["L1_attn_ln_g"]), "b1g": cols(f["L1_attn_ln_b"]), "conv1_w": tap(f["L1_attn_conv_w"]),
        "conv1_b": cols(f["L1_attn_conv_b"]), "b_dt": cols(f["L1_attn_b_dt"]),
        "alog": f["L1_attn_A_log"].reshape(2, P, NM).transpose(1, 0, 2).reshape(P, 32), "dm": cols(f["L1_attn_D"]),
        "mb1": e4(f["L1_ffn_b1"]), "w1_s": cols(f["L2_ffn_w1_s"]), "w2_s": cols(f["L2_ffn_w2_s"]),
        "h1_s": cols(f["L2_ffn_h1_s"]), "h2_s": cols(f["L2_ffn_h2_s"]), "normw": cols(f["L3_attn_norm_w"]),
        "bg": e4(f["L3_ffn_b_gate"]), "bu": e4(f["L3_ffn_b_up"]),
        "alpha": np.repeat(f["L2_attn_alpha_log"], 8)[:, None], "beta": np.repeat(f["L2_attn_beta_log"], 8)[:, None],
        "a0": np.concatenate([a0, a0])[:, None],
        "w3_s": np.broadcast_to(f["L2_ffn_w3_s"], (P, P)),
    }
    prm = np.concatenate([pk[k] for k, _ in PCOLS], 1)
    row = lambda v: np.broadcast_to(np.asarray(v, np.float32), (P, len(v)))
    t = np.arange(T)
    ck = {
        "ident": np.eye(P, dtype=np.float32),
        "tri": (np.arange(P)[:, None] <= t[None, :]).astype(np.float32),
        "pos": row(t + 1), "m_ref": row(np.arange(REF + 64) - REF), "mod128": row(t % P), "mod64": row(t % 64),
        "iota8": row(np.arange(NE)),
        "pick": (np.arange(P)[:, None] % 32 == np.arange(32)[None, :]).astype(np.float32),
    }
    cst = np.concatenate([ck[k] for k, _ in CCOLS], 1)
    r = np.arange(P)
    h2, d, e = r // 64, r // 8 % 8, r % 8
    one = lambda rows: (r[:, None] == rows[None, :]).astype(np.float32)
    byd = [one(8 * (2 * b + h2) + d) for b in range(NB0)]
    bye = [one(8 * (2 * b + h2) + e) for b in range(NB0)]
    sel = np.concatenate(byd + bye + [m.T for m in bye], 1)
    w1, w2 = f["L1_ffn_W1"], f["L1_ffn_W2"]
    fold = lambda a: a.reshape(NE, 4, P, P).transpose(0, 2, 1, 3).reshape(NE, P, 4 * P)
    x4 = lambda a: a.reshape(4, NC, P, P)
    return {
        "x": x4(f["L0_attn_x"]).transpose(0, 2, 1, 3), "w": wts, "p": prm, "c": cst, "sel": sel,
        "a": f["L0_attn_A_param"].reshape(NB0, P, N0).transpose(1, 0, 2).reshape(P, NB0 * N0),
        "e1": np.concatenate([w1, fold(w2)], 2),
        "e3": np.concatenate([f["L3_ffn_w_gate"], f["L3_ffn_w_up"], fold(f["L3_ffn_w_down"])], 2),
        "r8": np.concatenate([f["L1_ffn_b2"], f["L3_ffn_b_down"], f["L1_attn_W_dt"]], 1),
    }


def build(nc, arrays, layers=NLAYERS):
    d = {k: nc.dram_tensor(f"in_{k}_dram", a.shape, mybir.dt.from_np(a.dtype), kind="ExternalInput").ap()
         for k, a in arrays.items()}
    out = nc.dram_tensor("out_0_dram", (4, T, P), F32, kind="ExternalOutput").ap()
    network(nc, d["x"], d["w"], d["p"], d["c"], d["sel"], d["a"], d["e1"], d["e3"], d["r8"],
            out.rearrange("b (c p) n -> b p c n", c=NC), layers)


def kernel(**inputs):
    import numpy as _np
    import concourse.bacc as _bacc
    from concourse.bass_utils import run_bass_kernel_spmd as _run

    arrays = {k: _np.ascontiguousarray(v) for k, v in layout(inputs).items()}
    nc = _bacc.Bacc("TRN2", target_bir_lowering=False, num_devices=1)
    build(nc, arrays)
    r = _run(nc, [{f"in_{k}_dram": v for k, v in arrays.items()}], core_ids=[0])
    return r.results[0]["out_0_dram"]
```
